# Optimizing a Trainium2 kernel written in Bass

```python
import numpy as np
import jax
import jax.numpy as jnp

def _softmax(x, axis=-1):
    return jax.nn.softmax(x, axis=axis)
def _gelu(x):
    return jax.nn.gelu(x, approximate=True)
def _silu(x):
    return jax.nn.silu(x)
def _sigmoid(x):
    return jax.nn.sigmoid(x)
def _layernorm(x, axis=-1, eps=1e-5):
    m = jnp.mean(x, axis=axis, keepdims=True)
    v = jnp.var(x, axis=axis, keepdims=True)
    return (x - m) / jnp.sqrt(v + eps)
def _scatter_add(tgt, idx, src, axis=0):
    return tgt.at[idx].add(src)
def _segment_sum(src, seg, n):
    return jax.ops.segment_sum(src, seg, n)

kernel_name = 'mk_conv_attn_hybrid_d4_conv_nchw128_775920'

def setup_inputs(seed: int = 0):
    np.random.seed(seed)
    _w = jnp.asarray
    def _rec_inputs():
        import jax
        import jax.numpy as jnp
        _gk = jax.random.key(seed)
        x = -0.000929 + 1 * jax.random.normal(jax.random.fold_in(_gk, 1), (2, 128, 64, 64), jnp.float32)
        return x
    x = _rec_inputs()
    def _L0_conv_setup():
        import jax, jax.numpy as jnp
        import numpy as np
        NUM_HEADS = 4
        KERNEL = 7
        EPS = 1e-05

        def _na2d(x, w_qkv, b_qkv, rpb, w_p, b_p):
            B, H, W, C = x.shape
            h, k = (NUM_HEADS, KERNEL)
            d = C // h
            qkv = (x @ w_qkv.T + b_qkv).reshape(B, H, W, 3, h, d)
            q = qkv[..., 0, :, :] * d ** (-0.5)
            kk = qkv[..., 1, :, :]
            v = qkv[..., 2, :, :]
            si = jnp.clip(jnp.arange(H) - k // 2, 0, H - k)
            sj = jnp.clip(jnp.arange(W) - k // 2, 0, W - k)
            idx_i = si[:, None] + jnp.arange(k)
            idx_j = sj[:, None] + jnp.arange(k)

            def win(t):
                t = t[:, idx_i]
                t = t[:, :, :, idx_j]
                return jnp.transpose(t, (0, 1, 3, 2, 4, 5, 6))
            kw = win(kk)
            vw = win(v)
            attn = jnp.einsum('bijhd,bijpqhd->bijhpq', q, kw)
            bi = jnp.arange(k)[None, :] + (k - 1) - (jnp.arange(H) - si)[:, None]
            bj = jnp.arange(k)[None, :] + (k - 1) - (jnp.arange(W) - sj)[:, None]
            bias = rpb[:, bi[:, None, :, None], bj[None, :, None, :]]
            attn = attn + jnp.transpose(bias, (1, 2, 0, 3, 4))[None]
            attn = jax.nn.softmax(attn.reshape(B, H, W, h, k * k), axis=-1).reshape(B, H, W, h, k, k)
            out = jnp.einsum('bijhpq,bijpqhd->bijhd', attn, vw).reshape(B, H, W, C)
            return out @ w_p.T + b_p
        key = jax.random.key(seed)
        ks = jax.random.split(key, 6)
        C, depth = (128, 2)
        x = jax.random.normal(ks[0], (2, C, 64, 64), jnp.float32)
        qkv_w = jax.random.normal(ks[1], (depth, 3 * C, C), jnp.float32) * 0.05
        qkv_b = jnp.zeros((depth, 3 * C), jnp.float32)
        rpb = jax.random.normal(ks[2], (depth, NUM_HEADS, 2 * KERNEL - 1, 2 * KERNEL - 1), jnp.float32) * 0.02
        proj_w = jax.random.normal(ks[3], (depth, C, C), jnp.float32) * 0.05
        proj_b = jnp.zeros((depth, C), jnp.float32)
        ln_g = jnp.ones((C,), jnp.float32)
        ln_b = jnp.zeros((C,), jnp.float32)
        return dict(x=x, qkv_w=qkv_w, qkv_b=qkv_b, rpb=rpb, proj_w=proj_w, proj_b=proj_b, ln_g=ln_g, ln_b=ln_b)
    _L0_conv_all = _L0_conv_setup()
    _L0_conv_in = {k: v for k, v in _L0_conv_all.items() if k in ('qkv_w', 'qkv_b', 'rpb', 'proj_w', 'proj_b', 'ln_g', 'ln_b', )}
    del _L0_conv_all

    def _L1_conv_setup():
        import jax, jax.numpy as jnp
        import numpy as np
        from jax import lax
        B_, DIM, H_, W_ = (4, 128, 64, 64)
        D_STATE, D_CONV, EXPAND = (16, 4, 2)
        D_INNER = EXPAND * DIM
        DT_RANK = (DIM + 15) // 16

        def _mamba_layer2d(x, norm_w, norm_b, in_proj_w, conv_w, conv_b, x_proj_w, dt_proj_w, dt_proj_b, A_log, D, out_proj_w):
            B, C, H, W = x.shape
            L = H * W
            xs = x.reshape(B, C, L).transpose(0, 2, 1)
            mu = jnp.mean(xs, axis=-1, keepdims=True)
            var = jnp.mean(jnp.square(xs - mu), axis=-1, keepdims=True)
            xn = (xs - mu) * lax.rsqrt(var + 1e-05) * norm_w + norm_b
            xz = jnp.einsum('blc,ec->ble', xn, in_proj_w)
            xin, z = jnp.split(xz, 2, axis=-1)
            d_conv = conv_w.shape[1]
            xp = jnp.pad(xin, ((0, 0), (d_conv - 1, 0), (0, 0)))
            xc = conv_b + sum((xp[:, k:k + L, :] * conv_w[:, k] for k in range(d_conv)))
            xc = jax.nn.silu(xc)
            dbl = jnp.einsum('bld,ed->ble', xc, x_proj_w)
            dt_rank = dt_proj_w.shape[1]
            d_state = A_log.shape[1]
            dt = dbl[..., :dt_rank]
            B_ssm = dbl[..., dt_rank:dt_rank + d_state]
            C_ssm = dbl[..., dt_rank + d_state:]
            delta = jax.nn.softplus(jnp.einsum('blr,dr->bld', dt, dt_proj_w) + dt_proj_b)
            A = -jnp.exp(A_log)
            dA = jnp.exp(delta[..., None] * A)
            dBu = delta[..., None] * B_ssm[:, :, None, :] * xc[..., None]

            def step(h, inp):
                dA_t, dBu_t, C_t = inp
                h = dA_t * h + dBu_t
                y = jnp.einsum('bdn,bn->bd', h, C_t)
                return (h, y)
            h0 = jnp.zeros((B, xc.shape[-1], d_state), xc.dtype)
            _, ys = lax.scan(step, h0, (dA.transpose(1, 0, 2, 3), dBu.transpose(1, 0, 2, 3), C_ssm.transpose(1, 0, 2)))
            y = ys.transpose(1, 0, 2) + xc * D
            y = y * jax.nn.silu(z)
            out = jnp.einsum('bld,cd->blc', y, out_proj_w)
            return out.transpose(0, 2, 1).reshape(B, C, H, W)
        key = jax.random.key(seed)
        ks = jax.random.split(key, 10)
        s = lambda k, shape, sc=0.02: jax.random.normal(k, shape, jnp.float32) * sc
        inp = {'x': jax.random.normal(ks[0], (B_, DIM, H_, W_), jnp.float32), 'norm_w': jnp.ones((DIM,), jnp.float32), 'norm_b': jnp.zeros((DIM,), jnp.float32), 'in_proj_w': s(ks[1], (2 * D_INNER, DIM)), 'conv_w': s(ks[2], (D_INNER, D_CONV), 0.1), 'conv_b': s(ks[3], (D_INNER,), 0.02), 'x_proj_w': s(ks[4], (DT_RANK + 2 * D_STATE, D_INNER)), 'dt_proj_w': s(ks[5], (D_INNER, DT_RANK), 0.1), 'dt_proj_b': s(ks[6], (D_INNER,), 0.5), 'A_log': jnp.log(jnp.tile(jnp.arange(1, D_STATE + 1, dtype=jnp.float32), (D_INNER, 1))), 'D': jnp.ones((D_INNER,), jnp.float32), 'out_proj_w': s(ks[7], (DIM, D_INNER))}
        return inp
    _L1_conv_all = _L1_conv_setup()
    _L1_conv_in = {k: v for k, v in _L1_conv_all.items() if k in ('norm_w', 'norm_b', 'in_proj_w', 'conv_w', 'conv_b', 'x_proj_w', 'dt_proj_w', 'dt_proj_b', 'A_log', 'D', 'out_proj_w', )}
    del _L1_conv_all

    def _L2_attn_setup():
        import jax, jax.numpy as jnp
        import numpy as np
        NEG = -1000000000000.0
        key = jax.random.key(seed)
        k1, k2, k3, k4 = jax.random.split(key, 4)
        B, T, D, U = (4, 4096, 128, 128)
        query = jax.random.normal(k1, (B, T, D), dtype=jnp.float32)
        s = 1.0 / np.sqrt(D)
        Wq = jax.random.normal(k2, (D, U), dtype=jnp.float32) * s
        Wk = jax.random.normal(k3, (D, U), dtype=jnp.float32) * s
        Wv = jax.random.normal(k4, (D, U), dtype=jnp.float32) * s
        return {'query': query, 'Wq': Wq, 'Wk': Wk, 'Wv': Wv}
    _L2_attn_all = _L2_attn_setup()
    _L2_attn_in = {k: v for k, v in _L2_attn_all.items() if k in ('Wq', 'Wk', 'Wv', )}
    del _L2_attn_all

    def _L2_ffn_setup():
        import jax, jax.numpy as jnp
        import numpy as np
        B, N, D, C, E, K = (8, 8192, 128, 128, 8, 2)
        key = jax.random.key(seed)
        k0, k1, k2 = jax.random.split(key, 3)
        x = jax.random.normal(k0, (B, N, D), dtype=jnp.float32)
        router_w = jax.random.normal(k1, (D, E), dtype=jnp.float32) * 0.05
        router_b = jnp.zeros((E,), dtype=jnp.float32)
        expert_w = jax.random.normal(k2, (E, D, C), dtype=jnp.float32) * (1.0 / np.sqrt(D))
        expert_b = jnp.zeros((E, C), dtype=jnp.float32)
        return {'x': x, 'router_w': router_w, 'router_b': router_b, 'expert_w': expert_w, 'expert_b': expert_b}
    _L2_ffn_all = _L2_ffn_setup()
    _L2_ffn_in = {k: v for k, v in _L2_ffn_all.items() if k in ('router_w', 'router_b', 'expert_w', 'expert_b', )}
    del _L2_ffn_all

    def _L3_attn_setup():
        import jax, jax.numpy as jnp
        import numpy as np
        B, T, C = (4096, 64, 128)
        N_HEAD = 8
        D_HEAD = C // N_HEAD
        key = jax.random.key(seed)
        k1, k2, k3 = jax.random.split(key, 3)
        x = jax.random.normal(k1, (B, T, C), dtype=jnp.float32)
        w_attn = jax.random.normal(k2, (C, 3 * C), dtype=jnp.float32) * 0.02
        w_proj = jax.random.normal(k3, (C, C), dtype=jnp.float32) * 0.02
        return {'x': x, 'w_attn': w_attn, 'w_proj': w_proj}
    _L3_attn_all = _L3_attn_setup()
    _L3_attn_in = {k: v for k, v in _L3_attn_all.items() if k in ('w_attn', 'w_proj', )}
    del _L3_attn_all

    def _L3_ffn_setup():
        import jax, jax.numpy as jnp
        import numpy as np
        PADDED_SL = 8192
        TEMPERATURE = 1.0
        SIGMA_POW = 0.25

        def _stu_conv(phi, u, n):
            b, sl, d = u.shape
            sgn = jnp.where(jnp.arange(sl) % 2 == 0, 1.0, -1.0).astype(u.dtype)
            sgn3 = sgn[None, :, None]
            Vf = jnp.fft.rfft(phi, n=n, axis=0)
            Uf_p = jnp.fft.rfft(u, n=n, axis=1)
            Uf_m = jnp.fft.rfft(u * sgn3, n=n, axis=1)
            U_plus = jnp.fft.irfft(Vf[None, :, :, None] * Uf_p[:, :, None, :], n=n, axis=1)[:, :sl]
            U_minus = jnp.fft.irfft(Vf[None, :, :, None] * Uf_m[:, :, None, :], n=n, axis=1)[:, :sl]
            U_minus = U_minus * sgn[None, :, None, None]
            return (U_plus, U_minus)

        def _compute_spectral(u, sigma, phi, Mpp, Mpm):
            U_plus, U_minus = _stu_conv(phi, u, PADDED_SL)
            s = sigma ** SIGMA_POW
            out = jnp.einsum('btkd,k,kde->bte', U_plus, s, Mpp)
            out = out + jnp.einsum('btkd,k,kde->bte', U_minus, s, Mpm)
            return out

        def _compute_ar_u(Mu, u):
            sl = u.shape[1]
            out = jnp.zeros(u.shape[:2] + (Mu.shape[-1],), dtype=u.dtype)
            for i in range(Mu.shape[0]):
                ui = jnp.pad(u, ((0, 0), (i, 0), (0, 0)))[:, :sl]
                out = out + jnp.einsum('btd,de->bte', ui, Mu[i])
            return out

        def _stu(u, sigma, phi, Mu, Mpp, Mpm):
            return _compute_spectral(u, sigma, phi, Mpp, Mpm) + _compute_ar_u(Mu, u)
        key = jax.random.key(seed)
        ks = jax.random.split(key, 8)
        b, sl, d, K, k_u = (2, 4096, 128, 16, 3)
        x = jax.random.normal(ks[0], (b, sl, d), dtype=jnp.float32)
        sigma = jax.random.uniform(ks[1], (K,), dtype=jnp.float32, minval=0.001, maxval=1.0)
        phi = jax.random.normal(ks[2], (sl, K), dtype=jnp.float32) / np.sqrt(sl)
        M_u = jax.random.normal(ks[3], (4, k_u, d, d), dtype=jnp.float32) * 0.02
        M_phi_plus = jax.random.normal(ks[4], (4, K, d, d), dtype=jnp.float32) * 0.02
        M_phi_minus = jax.random.normal(ks[5], (4, K, d, d), dtype=jnp.float32) * 0.02
        log_weights = jnp.ones((4,), dtype=jnp.float32)
        u01 = jax.random.uniform(ks[6], (4,), dtype=jnp.float32, minval=1e-06, maxval=1.0 - 1e-06)
        gumbel = -jnp.log(-jnp.log(u01))
        return {'x': x, 'sigma': sigma, 'phi': phi, 'M_u': M_u, 'M_phi_plus': M_phi_plus, 'M_phi_minus': M_phi_minus, 'log_weights': log_weights, 'gumbel': gumbel}
    _L3_ffn_all = _L3_ffn_setup()
    _L3_ffn_in = {k: v for k, v in _L3_ffn_all.items() if k in ('sigma', 'phi', 'M_u', 'M_phi_plus', 'M_phi_minus', 'log_weights', 'gumbel', )}
    del _L3_ffn_all

    return {
        "x": x,
        "L0_conv_qkv_w": _L0_conv_in["qkv_w"],
        "L0_conv_qkv_b": _L0_conv_in["qkv_b"],
        "L0_conv_rpb": _L0_conv_in["rpb"],
        "L0_conv_proj_w": _L0_conv_in["proj_w"],
        "L0_conv_proj_b": _L0_conv_in["proj_b"],
        "L0_conv_ln_g": _L0_conv_in["ln_g"],
        "L0_conv_ln_b": _L0_conv_in["ln_b"],
        "L1_conv_norm_w": _L1_conv_in["norm_w"],
        "L1_conv_norm_b": _L1_conv_in["norm_b"],
        "L1_conv_in_proj_w": _L1_conv_in["in_proj_w"],
        "L1_conv_conv_w": _L1_conv_in["conv_w"],
        "L1_conv_conv_b": _L1_conv_in["conv_b"],
        "L1_conv_x_proj_w": _L1_conv_in["x_proj_w"],
        "L1_conv_dt_proj_w": _L1_conv_in["dt_proj_w"],
        "L1_conv_dt_proj_b": _L1_conv_in["dt_proj_b"],
        "L1_conv_A_log": _L1_conv_in["A_log"],
        "L1_conv_D": _L1_conv_in["D"],
        "L1_conv_out_proj_w": _L1_conv_in["out_proj_w"],
        "L2_attn_Wq": _L2_attn_in["Wq"],
        "L2_attn_Wk": _L2_attn_in["Wk"],
        "L2_attn_Wv": _L2_attn_in["Wv"],
        "L2_ffn_router_w": _L2_ffn_in["router_w"],
        "L2_ffn_router_b": _L2_ffn_in["router_b"],
        "L2_ffn_expert_w": _L2_ffn_in["expert_w"],
        "L2_ffn_expert_b": _L2_ffn_in["expert_b"],
        "L3_attn_w_attn": _L3_attn_in["w_attn"],
        "L3_attn_w_proj": _L3_attn_in["w_proj"],
        "L3_ffn_sigma": _L3_ffn_in["sigma"],
        "L3_ffn_phi": _L3_ffn_in["phi"],
        "L3_ffn_M_u": _L3_ffn_in["M_u"],
        "L3_ffn_M_phi_plus": _L3_ffn_in["M_phi_plus"],
        "L3_ffn_M_phi_minus": _L3_ffn_in["M_phi_minus"],
        "L3_ffn_log_weights": _L3_ffn_in["log_weights"],
        "L3_ffn_gumbel": _L3_ffn_in["gumbel"],
    }

def reference(x, L0_conv_qkv_w, L0_conv_qkv_b, L0_conv_rpb, L0_conv_proj_w, L0_conv_proj_b, L0_conv_ln_g, L0_conv_ln_b, L1_conv_norm_w, L1_conv_norm_b, L1_conv_in_proj_w, L1_conv_conv_w, L1_conv_conv_b, L1_conv_x_proj_w, L1_conv_dt_proj_w, L1_conv_dt_proj_b, L1_conv_A_log, L1_conv_D, L1_conv_out_proj_w, L2_attn_Wq, L2_attn_Wk, L2_attn_Wv, L2_ffn_router_w, L2_ffn_router_b, L2_ffn_expert_w, L2_ffn_expert_b, L3_attn_w_attn, L3_attn_w_proj, L3_ffn_sigma, L3_ffn_phi, L3_ffn_M_u, L3_ffn_M_phi_plus, L3_ffn_M_phi_minus, L3_ffn_log_weights, L3_ffn_gumbel):
    import jax
    import jax.numpy as jnp
    def _L0_conv_ref(x, qkv_w, qkv_b, rpb, proj_w, proj_b, ln_g, ln_b):
        import jax, jax.numpy as jnp
        import numpy as np
        NUM_HEADS = 4
        KERNEL = 7
        EPS = 1e-05

        def _na2d(x, w_qkv, b_qkv, rpb, w_p, b_p):
            B, H, W, C = x.shape
            h, k = (NUM_HEADS, KERNEL)
            d = C // h
            qkv = (x @ w_qkv.T + b_qkv).reshape(B, H, W, 3, h, d)
            q = qkv[..., 0, :, :] * d ** (-0.5)
            kk = qkv[..., 1, :, :]
            v = qkv[..., 2, :, :]
            si = jnp.clip(jnp.arange(H) - k // 2, 0, H - k)
            sj = jnp.clip(jnp.arange(W) - k // 2, 0, W - k)
            idx_i = si[:, None] + jnp.arange(k)
            idx_j = sj[:, None] + jnp.arange(k)

            def win(t):
                t = t[:, idx_i]
                t = t[:, :, :, idx_j]
                return jnp.transpose(t, (0, 1, 3, 2, 4, 5, 6))
            kw = win(kk)
            vw = win(v)
            attn = jnp.einsum('bijhd,bijpqhd->bijhpq', q, kw)
            bi = jnp.arange(k)[None, :] + (k - 1) - (jnp.arange(H) - si)[:, None]
            bj = jnp.arange(k)[None, :] + (k - 1) - (jnp.arange(W) - sj)[:, None]
            bias = rpb[:, bi[:, None, :, None], bj[None, :, None, :]]
            attn = attn + jnp.transpose(bias, (1, 2, 0, 3, 4))[None]
            attn = jax.nn.softmax(attn.reshape(B, H, W, h, k * k), axis=-1).reshape(B, H, W, h, k, k)
            out = jnp.einsum('bijhpq,bijpqhd->bijhd', attn, vw).reshape(B, H, W, C)
            return out @ w_p.T + b_p
        y = jnp.transpose(x, (0, 2, 3, 1))
        for l in range(qkv_w.shape[0]):
            y = _na2d(y, qkv_w[l], qkv_b[l], rpb[l], proj_w[l], proj_b[l])
        mu = y.mean(-1, keepdims=True)
        var = y.var(-1, keepdims=True)
        y = (y - mu) / jnp.sqrt(var + EPS) * ln_g + ln_b
        return jnp.transpose(y, (0, 3, 1, 2))

    def _L1_conv_ref(x, norm_w, norm_b, in_proj_w, conv_w, conv_b, x_proj_w, dt_proj_w, dt_proj_b, A_log, D, out_proj_w):
        import jax, jax.numpy as jnp
        import numpy as np
        from jax import lax
        B_, DIM, H_, W_ = (4, 128, 64, 64)
        D_STATE, D_CONV, EXPAND = (16, 4, 2)
        D_INNER = EXPAND * DIM
        DT_RANK = (DIM + 15) // 16

        def _mamba_layer2d(x, norm_w, norm_b, in_proj_w, conv_w, conv_b, x_proj_w, dt_proj_w, dt_proj_b, A_log, D, out_proj_w):
            B, C, H, W = x.shape
            L = H * W
            xs = x.reshape(B, C, L).transpose(0, 2, 1)
            mu = jnp.mean(xs, axis=-1, keepdims=True)
            var = jnp.mean(jnp.square(xs - mu), axis=-1, keepdims=True)
            xn = (xs - mu) * lax.rsqrt(var + 1e-05) * norm_w + norm_b
            xz = jnp.einsum('blc,ec->ble', xn, in_proj_w)
            xin, z = jnp.split(xz, 2, axis=-1)
            d_conv = conv_w.shape[1]
            xp = jnp.pad(xin, ((0, 0), (d_conv - 1, 0), (0, 0)))
            xc = conv_b + sum((xp[:, k:k + L, :] * conv_w[:, k] for k in range(d_conv)))
            xc = jax.nn.silu(xc)
            dbl = jnp.einsum('bld,ed->ble', xc, x_proj_w)
            dt_rank = dt_proj_w.shape[1]
            d_state = A_log.shape[1]
            dt = dbl[..., :dt_rank]
            B_ssm = dbl[..., dt_rank:dt_rank + d_state]
            C_ssm = dbl[..., dt_rank + d_state:]
            delta = jax.nn.softplus(jnp.einsum('blr,dr->bld', dt, dt_proj_w) + dt_proj_b)
            A = -jnp.exp(A_log)
            dA = jnp.exp(delta[..., None] * A)
            dBu = delta[..., None] * B_ssm[:, :, None, :] * xc[..., None]

            def step(h, inp):
                dA_t, dBu_t, C_t = inp
                h = dA_t * h + dBu_t
                y = jnp.einsum('bdn,bn->bd', h, C_t)
                return (h, y)
            h0 = jnp.zeros((B, xc.shape[-1], d_state), xc.dtype)
            _, ys = lax.scan(step, h0, (dA.transpose(1, 0, 2, 3), dBu.transpose(1, 0, 2, 3), C_ssm.transpose(1, 0, 2)))
            y = ys.transpose(1, 0, 2) + xc * D
            y = y * jax.nn.silu(z)
            out = jnp.einsum('bld,cd->blc', y, out_proj_w)
            return out.transpose(0, 2, 1).reshape(B, C, H, W)
        return _mamba_layer2d(x, norm_w, norm_b, in_proj_w, conv_w, conv_b, x_proj_w, dt_proj_w, dt_proj_b, A_log, D, out_proj_w)

    def _L2_attn_ref(query, Wq, Wk, Wv):
        import jax, jax.numpy as jnp
        import numpy as np
        NEG = -1000000000000.0
        q = jnp.einsum('btd,du->btu', query, Wq)
        k = jnp.einsum('btd,du->btu', query, Wk)
        v = jnp.einsum('btd,du->btu', query, Wv)
        T = v.shape[1]
        scores = jnp.einsum('bqu,bku->bqk', q, k) / jnp.sqrt(jnp.asarray(T, jnp.float32))
        causal = jnp.tril(jnp.ones((T, T), dtype=jnp.float32))
        scores = scores + NEG * (1.0 - causal)
        attn = jax.nn.softmax(scores, axis=-1)
        context = jnp.einsum('bqk,bku->bqu', attn, v)
        return context

    def _L2_ffn_ref(x, router_w, router_b, expert_w, expert_b):
        import jax, jax.numpy as jnp
        import numpy as np
        B, N, D, C, E, K = (8, 8192, 128, 128, 8, 2)
        router_probs = jax.nn.softmax(x @ router_w + router_b, axis=-1)
        top_p, top_i = jax.lax.top_k(router_probs, K)
        top_p = top_p / jnp.sum(top_p, axis=-1, keepdims=True)
        expert_out = jnp.einsum('bnd,edc->bnec', x, expert_w) + expert_b
        gathered = jnp.take_along_axis(expert_out, top_i[..., None], axis=2)
        return jnp.einsum('bnk,bnkc->bnc', top_p, gathered)

    def _L3_attn_ref(x, w_attn, w_proj):
        import jax, jax.numpy as jnp
        import numpy as np
        B, T, C = (4096, 64, 128)
        N_HEAD = 8
        D_HEAD = C // N_HEAD
        Bt, Tt, Ct = x.shape
        qkv = x @ w_attn
        q, k, v = jnp.split(qkv, 3, axis=-1)
        q = q.reshape(Bt, Tt, N_HEAD, D_HEAD)
        k = k.reshape(Bt, Tt, N_HEAD, D_HEAD)
        v = v.reshape(Bt, Tt, N_HEAD, D_HEAD)
        scale = 1.0 / jnp.sqrt(jnp.float32(D_HEAD))
        att = jnp.einsum('bqhd,bkhd->bhqk', q, k) * scale
        causal = jnp.tril(jnp.ones((Tt, Tt), dtype=bool))
        att = jnp.where(causal[None, None, :, :], att, -jnp.inf)
        att = jax.nn.softmax(att, axis=-1)
        out = jnp.einsum('bhqk,bkhd->bqhd', att, v).reshape(Bt, Tt, Ct)
        return out @ w_proj

    def _L3_ffn_ref(x, sigma, phi, M_u, M_phi_plus, M_phi_minus, log_weights, gumbel):
        import jax, jax.numpy as jnp
        import numpy as np
        PADDED_SL = 8192
        TEMPERATURE = 1.0
        SIGMA_POW = 0.25

        def _stu_conv(phi, u, n):
            b, sl, d = u.shape
            sgn = jnp.where(jnp.arange(sl) % 2 == 0, 1.0, -1.0).astype(u.dtype)
            sgn3 = sgn[None, :, None]
            Vf = jnp.fft.rfft(phi, n=n, axis=0)
            Uf_p = jnp.fft.rfft(u, n=n, axis=1)
            Uf_m = jnp.fft.rfft(u * sgn3, n=n, axis=1)
            U_plus = jnp.fft.irfft(Vf[None, :, :, None] * Uf_p[:, :, None, :], n=n, axis=1)[:, :sl]
            U_minus = jnp.fft.irfft(Vf[None, :, :, None] * Uf_m[:, :, None, :], n=n, axis=1)[:, :sl]
            U_minus = U_minus * sgn[None, :, None, None]
            return (U_plus, U_minus)

        def _compute_spectral(u, sigma, phi, Mpp, Mpm):
            U_plus, U_minus = _stu_conv(phi, u, PADDED_SL)
            s = sigma ** SIGMA_POW
            out = jnp.einsum('btkd,k,kde->bte', U_plus, s, Mpp)
            out = out + jnp.einsum('btkd,k,kde->bte', U_minus, s, Mpm)
            return out

        def _compute_ar_u(Mu, u):
            sl = u.shape[1]
            out = jnp.zeros(u.shape[:2] + (Mu.shape[-1],), dtype=u.dtype)
            for i in range(Mu.shape[0]):
                ui = jnp.pad(u, ((0, 0), (i, 0), (0, 0)))[:, :sl]
                out = out + jnp.einsum('btd,de->bte', ui, Mu[i])
            return out

        def _stu(u, sigma, phi, Mu, Mpp, Mpm):
            return _compute_spectral(u, sigma, phi, Mpp, Mpm) + _compute_ar_u(Mu, u)
        T = x.shape[1]
        outs = []
        for i, frac in enumerate((1, 2, 4, 8)):
            xi = x[:, :T // frac]
            si = _stu(xi, sigma, phi, M_u[i], M_phi_plus[i], M_phi_minus[i])
            si = jnp.pad(si, ((0, 0), (0, T - si.shape[1]), (0, 0)))
            outs.append(si)
        y_soft = jax.nn.softmax((log_weights + gumbel) / TEMPERATURE)
        y_hard = jax.nn.one_hot(jnp.argmax(y_soft), 4, dtype=y_soft.dtype)
        weights = y_hard - jax.lax.stop_gradient(y_soft) + y_soft
        stacked = jnp.stack(outs, axis=-1)
        return jnp.sum(stacked * weights, axis=-1)

    def _gn(v, G=32, eps=1e-5):
        B_, C_, H_, W_ = v.shape
        g = v.reshape(B_, G, C_ // G, H_, W_)
        m = jnp.mean(g, axis=(2, 3, 4), keepdims=True)
        s = jnp.var(g, axis=(2, 3, 4), keepdims=True)
        return ((g - m) / jnp.sqrt(s + eps)).reshape(v.shape)

    def _ln_c(v, eps=1e-6):
        m = jnp.mean(v, axis=1, keepdims=True)
        s = jnp.var(v, axis=1, keepdims=True)
        return (v - m) / jnp.sqrt(s + eps)

    def _ln_t(v, eps=1e-5):
        m = jnp.mean(v, axis=-1, keepdims=True)
        s = jnp.var(v, axis=-1, keepdims=True)
        return (v - m) / jnp.sqrt(s + eps)

    def _to_tokens(v):
        B_, C_, H_, W_ = v.shape
        return v.reshape(B_, C_, H_ * W_).transpose(0, 2, 1)
    def _from_tokens(t, like):
        B_, C_, H_, W_ = like.shape
        return t.transpose(0, 2, 1).reshape(B_, C_, H_, W_)

    x = x + _L0_conv_ref(_gn(x), L0_conv_qkv_w, L0_conv_qkv_b, L0_conv_rpb, L0_conv_proj_w, L0_conv_proj_b, L0_conv_ln_g, L0_conv_ln_b)
    x = x + _L1_conv_ref(_gn(x), L1_conv_norm_w, L1_conv_norm_b, L1_conv_in_proj_w, L1_conv_conv_w, L1_conv_conv_b, L1_conv_x_proj_w, L1_conv_dt_proj_w, L1_conv_dt_proj_b, L1_conv_A_log, L1_conv_D, L1_conv_out_proj_w)
    t = _to_tokens(x)
    t = t + _L2_attn_ref(_ln_t(t), L2_attn_Wq, L2_attn_Wk, L2_attn_Wv)
    t = t + _L2_ffn_ref(_ln_t(t), L2_ffn_router_w, L2_ffn_router_b, L2_ffn_expert_w, L2_ffn_expert_b)
    t = t + _L3_attn_ref(_ln_t(t), L3_attn_w_attn, L3_attn_w_proj)
    t = t + _L3_ffn_ref(_ln_t(t), L3_ffn_sigma, L3_ffn_phi, L3_ffn_M_u, L3_ffn_M_phi_plus, L3_ffn_M_phi_minus, L3_ffn_log_weights, L3_ffn_gumbel)
    x = _from_tokens(t, x)
    return x


_drawn_inputs = setup_inputs


def setup_inputs(seed=0):
    import zlib

    import numpy as np

    out = dict(_drawn_inputs(seed))
    spreads = {'L0_conv_qkv_b': (0.0, 0.1),
     'L0_conv_proj_b': (0.0, 0.1),
     'L0_conv_ln_g': (1.0, 0.2),
     'L0_conv_ln_b': (0.0, 0.1),
     'L1_conv_norm_w': (1.0, 0.6),
     'L1_conv_norm_b': (0.0, 0.8),
     'L1_conv_D': (1.0, 0.6),
     'L2_ffn_router_b': (0.0, 2.0),
     'L2_ffn_expert_b': (0.0, 2.0),
     'L3_ffn_log_weights': (1.0, 0.2)}
    factors = {'L0_conv_rpb': 64.0,
     'L1_conv_in_proj_w': 5.158,
     'L1_conv_conv_w': 5.524,
     'L1_conv_conv_b': 8.0,
     'L1_conv_x_proj_w': 8.0,
     'L1_conv_dt_proj_w': 8.0,
     'L1_conv_dt_proj_b': 8.0,
     'L1_conv_A_log': 8.0,
     'L1_conv_out_proj_w': 5.41,
     'L3_attn_w_attn': 112.885,
     'L2_attn_Wq': 43.635,
     'L2_attn_Wk': 44.352,
     'L2_attn_Wv': 42.268,
     'L2_ffn_router_w': 48.256,
     'L2_ffn_expert_w': 44.562,
     'L3_attn_w_proj': 40.105,
     'L3_ffn_sigma': 8.0,
     'L3_ffn_phi': 8.0,
     'L3_ffn_M_u': 64.0,
     'L3_ffn_M_phi_plus': 8.0,
     'L3_ffn_M_phi_minus': 8.0,
     'L3_ffn_gumbel': 8.0}
    for name, (base, spread) in spreads.items():
        noise = np.random.default_rng([zlib.crc32(name.encode()), seed]).standard_normal(out[name].shape)
        drawn = base * np.exp(spread * noise) if base else spread * noise
        out[name] = jnp.asarray(drawn.astype(out[name].dtype))
    for name, factor in factors.items():
        out[name] = (out[name] * factor).astype(out[name].dtype)
    return out
```

```python
from contextlib import ExitStack

import numpy as np

import concourse.bass as bass
from concourse import mybir

F32 = mybir.dt.float32
BF16 = mybir.dt.bfloat16
U32 = mybir.dt.uint32
ALU = mybir.AluOpType
ACT = mybir.ActivationFunctionType
AX = mybir.AxisListType.X

P = 128
BATCH = 2
HW = 64
T = HW * HW
TOK = BATCH * T
CH = 512
NCH = TOK // CH
NEG = -1e30
ds = bass.ds

NH0, D0, KW = 4, 32, 7
TR, TC = 8, 16
WR, WC = 15, 22
KC = 5 * WC

DIN, NST, DTR, NCONV = 256, 16, 8, 4

NH3, D3 = 8, 16
NK = 16


def block_starts(n, tile, span):
    return [min(max(i * tile - KW // 2, 0), n - span) for i in range(n // tile)]


ROW0, COL0 = block_starts(HW, TR, WR), block_starts(HW, TC, WC)


def window_masks():
    i, p = np.arange(HW), np.clip(np.arange(HW) - KW // 2, 0, HW - KW)
    kinds, masks = {}, []
    index = []
    for a in range(HW // TR):
        for b in range(HW // TC):
            qi, qj = a * TR + np.arange(TR), b * TC + np.arange(TC)[::-1]
            ki, kj = ROW0[a] + np.arange(WR), COL0[b] + np.arange(WC)
            ri = (ki[None] >= p[qi][:, None]) & (ki[None] < p[qi][:, None] + KW)
            rj = (kj[None] >= p[qj][:, None]) & (kj[None] < p[qj][:, None] + KW)
            m = np.where(ri[:, None, :, None] & rj[None, :, None, :], 0.0, NEG).reshape(P, WR * WC)
            key = m.tobytes()
            if key not in kinds:
                kinds[key] = len(masks)
                masks.append(m)
            index.append(kinds[key])
    return np.stack(masks, 1).astype(np.float32), index


OFF_R = max(i * TR - r for i, r in enumerate(ROW0))
OFF_C = max(i * TC - r for i, r in enumerate(COL0))
BR, BC = WR + OFF_R, WC + OFF_C
RPB = 2 * KW - 1
PAD_R, PAD_C = TR - 1 + OFF_R - (KW - 1), TC - 1 + OFF_C - (KW - 1)
PR, PC = PAD_R + BR - OFF_R + KW - 1, PAD_C + BC - OFF_C + KW - 1
MASKS, MASK_OF = window_masks()
NMASK = MASKS.shape[1]


def constants():
    r = np.arange(P)
    one_hot = np.zeros((DTR + 2 * NST, 2 * NST, P), np.float32)
    for n in range(2 * NST):
        one_hot[DTR + n, n, :] = 1.0
    return {
        "c_ident": np.eye(P, dtype=np.float32),
        "c_mean": np.full((P, P), 1.0 / P, np.float32),
        "c_group": np.where(r[:, None] // 4 == r[None] // 4, 0.25, 0.0).astype(np.float32),
        "c_causal": np.where(r[None] > r[:, None], NEG, 0.0).astype(np.float32),
        "c_window": MASKS,
        "c_pick": one_hot,
        "c_iota": np.tile(np.arange(8, dtype=np.float32), (P, 1)),
        "c_regime": np.stack([np.arange(4) == 3 - i for i in range(4)]).astype(np.float32),
    }


class Memory:

    def __init__(self, nc, ctx):
        self.nc, self.ctx, self.sems = nc, ctx, []
        ctx.callback(self.clear)

    def clear(self):
        if self.sems:
            with self.nc.Block() as block:
                @block.sync
                def _(sp):
                    for s in self.sems:
                        sp.sem_clear(s)

    def sb(self, name, shape, dt=F32):
        return self.ctx.enter_context(self.nc.sbuf_tensor(name, shape, dt))

    def ps(self, name, shape, dt=F32):
        return self.ctx.enter_context(self.nc.psum_tensor(name, shape, dt))

    def sem(self, name):
        self.sems.append(self.ctx.enter_context(self.nc.semaphore(name)))
        return self.sems[-1]


def wait_apart(eng, sem, value):
    with eng.register() as target:
        eng.reg_mov(target, value)
        eng.wait_ge(sem, 1)
        eng.wait_ge(sem, target)


def load_constants(nc, m, dram):
    k = {}
    k["ident"] = m.sb("ident", [P, P])
    k["mean"] = m.sb("mean_w", [P, P])
    k["group"] = m.sb("group_w", [P, P])
    k["ident16"] = m.sb("ident16", [P, P], BF16)
    k["causal"] = m.sb("causal", [P, P])
    k["causal16"] = m.sb("causal16", [P, P], BF16)
    k["causalT16"] = m.sb("causalT16", [P, P], BF16)
    k["eps5"] = m.sb("eps5", [P, 1])
    k["eps6"] = m.sb("eps6", [P, 1])
    with ExitStack() as c:
        mm = Memory(nc, c)
        loaded, turned, made = mm.sem("const_loaded"), mm.sem("const_turned"), mm.sem("const_made")
        tp = mm.ps("const_tp", [P, P])
        block = c.enter_context(nc.Block())

        @block.sync
        def _(sp):
            for name in ("ident", "mean", "group", "causal"):
                sp.dma_start(k[name][:, :], dram[f"c_{name}"]).then_inc(loaded, 16)

        @block.tensor
        def _(pe):
            pe.wait_ge(loaded, 64)
            pe.transpose(tp[:, :], k["causal"][:, :], k["ident"][:, :]).then_inc(turned, 1)

        @block.vector
        def _(dve):
            dve.memset(k["eps5"][:, :], 1e-5)
            dve.memset(k["eps6"][:, :], 1e-6)
            dve.wait_ge(loaded, 64)
            dve.tensor_copy(k["ident16"][:, :], k["ident"][:, :])
            dve.tensor_copy(k["causal16"][:, :], k["causal"][:, :])
            dve.wait_ge(turned, 1)
            dve.tensor_copy(k["causalT16"][:, :], tp[:, :]).then_inc(made, 1)
    return k


def layer_norm(nc, k, tag, src, dst, eps, gain=None, shift=None, add_to=None):
    with ExitStack() as c:
        m = Memory(nc, c)
        mean_ps, var_ps = m.ps(f"{tag}_mean", [P, 2, CH]), m.ps(f"{tag}_var", [P, 2, CH])
        square, std, rstd = (m.sb(f"{tag}_{n}", [P, 2, CH]) for n in ("square", "std", "rstd"))
        mean_ready, centered, square_ready, var_ready, std_ready, inverted, scaled, normed, added = (
            m.sem(f"{tag}_s{n}") for n in range(9))
        block = c.enter_context(nc.Block())

        def at(i, u):
            return ds(i * 2 * CH + u * CH, CH)

        @block.tensor
        def _(pe):
            pe.sem_inc(var_ready, 2)
            with pe.Fori(0, NCH // 2) as i:
                for u in range(2):
                    pe.wait_ge(centered, i * 2 + u + 1)
                    pe.matmul(mean_ps[:, u, :], k["mean"][:, :], src[:, at(i, u)], start=True, stop=True).then_inc(mean_ready, 1)
            with pe.Fori(0, NCH // 2) as i:
                for u in range(2):
                    pe.wait_ge(square_ready, i * 2 + u + 1)
                    pe.wait_ge(std_ready, i * 2 + u + 1)
                    pe.matmul(var_ps[:, u, :], k["mean"][:, :], square[:, u, :], start=True, stop=True).then_inc(var_ready, 1)

        @block.gpsimd
        def _(pool):
            with pool.Fori(0, NCH // 2) as i:
                for u in range(2):
                    pool.wait_ge(centered, i * 2 + u + 3)
                    pool.wait_ge(var_ready, i * 2 + u + 1)
                    pool.tensor_tensor(square[:, u, :], dst[:, at(i, u)], dst[:, at(i, u)], ALU.mult).then_inc(square_ready, 1)

        @block.scalar
        def _(act):
            act.sem_inc(std_ready, 2)
            with act.Fori(0, NCH // 2) as i:
                for u in range(2):
                    act.wait_ge(var_ready, i * 2 + u + 3)
                    act.wait_ge(inverted, i * 2 + u + 1)
                    act.activation(std[:, u, :], var_ps[:, u, :], ACT.Sqrt, bias=k[eps][:, :]).then_inc(std_ready, 1)

        @block.vector
        def _(dve):
            dve.sem_inc(centered, 2)
            dve.sem_inc(inverted, 2)
            with dve.Fori(0, NCH // 2) as i:
                for u in range(2):
                    dve.wait_ge(mean_ready, i * 2 + u + 1)
                    dve.tensor_tensor(dst[:, at(i, u)], src[:, at(i, u)], mean_ps[:, u, :], ALU.subtract).then_inc(centered, 1)
            with dve.Fori(0, NCH // 2) as i:
                for u in range(2):
                    dve.wait_ge(std_ready, i * 2 + u + 3)
                    dve.reciprocal(rstd[:, u, :], std[:, u, :]).then_inc(inverted, 1)
                    dve.wait_ge(inverted, i * 2 + u + 3)
                    dve.wait_ge(square_ready, i * 2 + u + 1)
                    dve.tensor_tensor(dst[:, at(i, u)], dst[:, at(i, u)], rstd[:, u, :], ALU.mult).then_inc(normed, 1)
                    if gain is not None:
                        dve.wait_ge(normed, i * 2 + u + 1)
                        dve.tensor_scalar(dst[:, at(i, u)], dst[:, at(i, u)], gain, shift, ALU.mult, ALU.add).then_inc(scaled, 1)
                    if add_to is not None:
                        dve.wait_ge(scaled, i * 2 + u + 1)
                        dve.tensor_tensor(add_to[:, at(i, u)], add_to[:, at(i, u)], dst[:, at(i, u)], ALU.add).then_inc(added, 1)


def group_norm(nc, k, tag, src, dst):
    with ExitStack() as c:
        m = Memory(nc, c)
        stats = m.sb(f"{tag}_stats", [P, NCH, 6])
        mv = m.sb(f"{tag}_mv", [P, BATCH, 2])
        mean = m.sb(f"{tag}_mean", [P, BATCH])
        part = m.sb(f"{tag}_part", [P, BATCH])
        std = m.sb(f"{tag}_std", [P, BATCH])
        rstd = m.sb(f"{tag}_rstd", [P, BATCH])
        g_ps, v_ps = m.ps(f"{tag}_g", [P, BATCH]), m.ps(f"{tag}_v", [P, BATCH])
        stat, meaned, step, varied, rooted, done = (m.sem(f"{tag}_s{n}") for n in range(6))
        block = c.enter_context(nc.Block())

        @block.vector
        def _(dve):
            for n in range(NCH):
                dve.bn_stats(stats[:, n, :], src[:, n * CH:(n + 1) * CH]).then_inc(stat, 1)
            dve.wait_ge(stat, NCH)
            for b in range(BATCH):
                dve.bn_aggr(mv[:, b, :], stats[:, b * NCH // 2:(b + 1) * NCH // 2, :]).then_inc(stat, 1)
            dve.wait_ge(meaned, 1)
            dve.tensor_copy(mean[:, :], g_ps[:, :]).then_inc(step, 1)
            dve.wait_ge(step, 1)
            dve.tensor_tensor(part[:, :], mv[:, :, 0], mean[:, :], ALU.subtract).then_inc(step, 1)
            dve.wait_ge(step, 2)
            dve.tensor_tensor(part[:, :], part[:, :], part[:, :], ALU.mult).then_inc(step, 1)
            dve.wait_ge(step, 3)
            dve.tensor_tensor(part[:, :], part[:, :], mv[:, :, 1], ALU.add).then_inc(step, 1)
            dve.wait_ge(rooted, 1)
            dve.reciprocal(rstd[:, :], std[:, :]).then_inc(step, 1)
            dve.wait_ge(step, 5)
            for n in range(NCH):
                b = n // (NCH // 2)
                dve.tensor_scalar(dst[:, n * CH:(n + 1) * CH], src[:, n * CH:(n + 1) * CH], mean[:, b:b + 1],
                                  rstd[:, b:b + 1], ALU.subtract, ALU.mult).then_inc(done, 1)

        @block.tensor
        def _(pe):
            pe.wait_ge(stat, NCH + BATCH)
            pe.matmul(g_ps[:, :], k["group"][:, :], mv[:, :, 0], start=True, stop=True).then_inc(meaned, 1)
            pe.wait_ge(step, 4)
            pe.matmul(v_ps[:, :], k["group"][:, :], part[:, :], start=True, stop=True).then_inc(varied, 1)

        @block.scalar
        def _(act):
            act.wait_ge(varied, 1)
            act.activation(std[:, :], v_ps[:, :], ACT.Sqrt, bias=k["eps5"][:, :]).then_inc(rooted, 1)


QT = T // P
SB = 4
NSB = QT // SB
NBLK = SB * NSB * (NSB + 1) // 2
MAX_RING, EXP_RING, W_RING = 3, 2, 4


def causal_attention(nc, k, tag, heads, dv, scale, buffers, score_max, score_exp, feed, loads, out_of, keep=None):
    B = len(buffers)
    banks = 1 if keep else (SB * (dv + 1) + CH - 1) // CH
    with ExitStack() as c:
        m = Memory(nc, c)
        max_ps = m.ps(f"{tag}_max_ps", [P, MAX_RING, CH])
        exp_ps = m.ps(f"{tag}_exp_ps", [P, EXP_RING, CH])
        out_ps = m.ps(f"{tag}_out_ps", [P, 2, CH])
        turn_ps = m.ps(f"{tag}_turn_ps", [P, 2 * CH], BF16)
        weights = m.sb(f"{tag}_weights", [P, W_RING, CH])
        part_max = m.sb(f"{tag}_part_max", [P, SB, NSB])
        minus = m.sb(f"{tag}_minus", [P, SB])
        rest = m.sb(f"{tag}_rest", [P, SB])
        parts = m.sb(f"{tag}_parts", [P, SB, 32], BF16)
        recip = m.sb(f"{tag}_recip", [P, SB])
        loaded = [m.sem(f"{tag}_loaded{u}") for u in range(B)]
        max_ready = m.sem(f"{tag}_max_ready")
        reduced = m.sem(f"{tag}_reduced")
        step = m.sem(f"{tag}_step")
        split = m.sem(f"{tag}_split")
        turned = m.sem(f"{tag}_turned")
        placed = m.sem(f"{tag}_placed")
        exp_ready = m.sem(f"{tag}_exp_ready")
        weighted = m.sem(f"{tag}_weighted")
        used = m.sem(f"{tag}_used")
        inverted = m.sem(f"{tag}_inverted")
        emitted = m.sem(f"{tag}_emitted")
        stored = [m.sem(f"{tag}_stored{u}") for u in range(B)]
        block = c.enter_context(nc.Block())
        credit = 2 if banks == 1 else 1

        def place_of(s, t):
            return (s % 2, t * (dv + 1)) if banks == 1 else (t // 2, (t % 2) * (dv + 1))

        def for_heads(eng, body):
            if heads == 1:
                body(0, 0, lambda per, j: j, 0)
                return
            with eng.Fori(0, heads // B) as i:
                for u in range(B):
                    body(i * B + u, u, lambda per, j, u=u: i * (B * per) + (u * per + j), i)

        if loads:
            @block.sync
            def _(sp):
                for u in range(B):
                    feed(sp, u, u, loaded[u])
                with sp.Fori(0, heads // B - 1) as i:
                    for u in range(B):
                        sp.wait_ge(used, i * (B * NBLK) + ((u + 1) * NBLK + W_RING))
                        feed(sp, u, i * B + (B + u), loaded[u])
                        sp.wait_ge(emitted, i * (B * NSB) + ((u + 1) * NSB + credit))
                        keep(sp, i * B + u, u, stored[u])
                for u in range(B):
                    sp.wait_ge(emitted, (heads - B + u + 1) * NSB + credit)
                    keep(sp, heads - B + u, u, stored[u])
                for u in range(B):
                    sp.wait_ge(stored[u], 32 * heads // B + 32)

        @block.tensor
        def _(pe):
            def head(it, u, at, i):
                if loads:
                    pe.wait_ge(loaded[u], i * (16 * loads) + 16 * loads)
                seen = {"max": 0, "exp": 0, "out": 0}

                def maxima(s, first, end):
                    for n in range(first, end):
                        t, ck = n // (s + 1), n % (s + 1)
                        g = seen["max"]
                        width = (t + 1) * P if ck == s else CH
                        bank = max_ps[:, g % MAX_RING, :]
                        pe.wait_ge(reduced, at(NBLK, g + 1))
                        mm = score_max(pe, u, bank[:, 0:width], SB * s + t, ck * CH, width)
                        if ck == s:
                            mm = pe.matmul(bank[:, t * P:width], k["ident16"][:, :], k["causal16"][:, :],
                                           start=False, stop=True, skip_group_check=True)
                        mm.then_inc(max_ready, 1)
                        seen["max"] += 1

                def turn(s):
                    pe.wait_ge(split, at(NSB, s + 1))
                    pe.wait_ge(placed, at(NSB, s + 1))
                    for t in range(SB):
                        mm = pe.transpose(turn_ps[96:128, t * P:(t + 1) * P], parts[:, t, :], k["ident16"][:, :])
                    mm.then_inc(turned, 1)

                def score(s, j):
                    g = seen["exp"]
                    q0 = max(0, j - SB * s) * P
                    bank = exp_ps[:, g % EXP_RING, :]
                    pe.wait_ge(weighted, at(NBLK, g + 1))
                    mm = score_exp(pe, u, bank[:, q0:CH], j, s * CH + q0, CH - q0)
                    if j >= SB * s:
                        mm = pe.matmul(bank[:, q0:q0 + P], k["ident16"][:, :], k["causalT16"][:, :],
                                       start=False, stop=True, skip_group_check=True)
                    mm.then_inc(exp_ready, 1)
                    seen["exp"] += 1

                def weigh(s, j):
                    g = seen["out"]
                    if j == 0:
                        pe.wait_ge(emitted, at(NSB, s + 1))
                    pe.wait_ge(weighted, at(NBLK, g + 1 + EXP_RING))
                    if keep:
                        q0 = max(0, j - SB * s) * P
                        mm = pe.matmul(out_ps[0:dv + 1, s % 2, q0:CH], buffers[u]["v"][:, j, :], weights[:, g % W_RING, q0:CH],
                                       start=(j == 0), stop=(j == SB * s + SB - 1), skip_group_check=True)
                    for t in () if keep else range(max(0, j - SB * s), SB):
                        bank, col = place_of(s, t)
                        mm = pe.matmul(out_ps[:, bank, col:col + dv + 1], weights[:, g % W_RING, t * P:(t + 1) * P],
                                       buffers[u]["v"][:, j, :], start=(j == 0 and col == 0),
                                       stop=(j == SB * s + t), skip_group_check=True)
                    mm.then_inc(used, 1)
                    seen["out"] += 1

                maxima(0, 0, SB)
                turn(0)
                for s in range(NSB):
                    pe.wait_ge(placed, at(NSB, s + 2))
                    blocks, chunks = SB * (s + 1), SB * (s + 2) if s + 1 < NSB else 0
                    steps = blocks - 2
                    for j in range(blocks + 2):
                        if j < blocks:
                            score(s, j)
                        if chunks and j < steps:
                            maxima(s + 1, chunks * j // steps, chunks * (j + 1) // steps)
                        if chunks and j == blocks:
                            turn(s + 1)
                        if j >= 2:
                            weigh(s, j - 2)
            for_heads(pe, head)

        @block.scalar
        def _(act):
            act.sem_inc(weighted, EXP_RING)
            if keep:
                act.sem_inc(emitted, credit)
                for u in range(B):
                    act.sem_inc(stored[u], 32)

            def head(it, u, at, i):
                g = 0

                def copy_out(s):
                    act.wait_ge(used, at(NBLK, SB * (s + 1) * (s + 2) // 2 + W_RING))
                    if s == 0:
                        act.wait_ge(stored[u], i * 32 + 32)
                    act.activation(buffers[u]["out"][:, s * CH:(s + 1) * CH], out_ps[0:dv + 1, s % 2, :], ACT.Copy)\
                       .then_inc(emitted, 1)

                for s in range(NSB):
                    if keep and s:
                        copy_out(s - 1)
                    for j in range(SB * (s + 1)):
                        q0 = max(0, j - SB * s) * P
                        act.wait_ge(exp_ready, at(NBLK, g + 1))
                        act.wait_ge(used, at(NBLK, g + 1))
                        act.activation(weights[:, g % W_RING, q0:CH], exp_ps[:, g % EXP_RING, q0:CH], ACT.Exp,
                                       scale=scale).then_inc(weighted, 1)
                        g += 1
                if keep:
                    copy_out(NSB - 1)
            for_heads(act, head)

        @block.vector
        def _(dve):
            dve.memset(parts[:, :, :], 0.0).then_inc(step, 1)
            dve.wait_ge(step, 1)
            dve.sem_inc(reduced, MAX_RING)
            dve.sem_inc(placed, 1)
            dve.sem_inc(used, W_RING)
            if not keep:
                dve.sem_inc(emitted, credit)

            def head(it, u, at, i):
                seen = {"max": 0, "step": 1}

                def small(ins):
                    ins.then_inc(step, 1)
                    seen["step"] += 1
                    dve.wait_ge(step, at(5 * NSB, seen["step"]))

                def maxima(s):
                    for t in range(SB):
                        for ck in range(s + 1):
                            g = seen["max"]
                            width = (t + 1) * P if ck == s else CH
                            dve.wait_ge(max_ready, at(NBLK, g + 1))
                            dve.tensor_reduce(part_max[:, t, ck:ck + 1], max_ps[:, g % MAX_RING, 0:width], AX,
                                              ALU.max).then_inc(reduced, 1)
                            seen["max"] += 1

                def split_max(s):
                    dve.wait_ge(reduced, at(NBLK, seen["max"] + MAX_RING))
                    small(dve.tensor_reduce(minus[:, :], part_max[:, :, 0:s + 1], AX, ALU.max, negate=True))
                    small(dve.tensor_copy(parts[:, :, 0], minus[:, :]))
                    small(dve.tensor_tensor(rest[:, :], minus[:, :], parts[:, :, 0], ALU.subtract))
                    small(dve.tensor_copy(parts[:, :, 1], rest[:, :]))
                    small(dve.tensor_tensor(rest[:, :], rest[:, :], parts[:, :, 1], ALU.subtract))
                    dve.tensor_copy(parts[:, :, 2], rest[:, :]).then_inc(split, 1)

                def put(s):
                    dve.wait_ge(turned, at(NSB, s + 1))
                    dve.tensor_copy(buffers[u]["minus_max"][96:99, s * CH:(s + 1) * CH], turn_ps[96:99, 0:CH])\
                       .then_inc(placed, 1)

                def emit(s):
                    dve.wait_ge(used, at(NBLK, SB * (s + 1) * (s + 2) // 2 + W_RING))
                    dve.wait_ge(emitted, at(NSB, s + credit))
                    n = SB // banks
                    for b in range(banks):
                        o = out_ps[:, s % 2 if banks == 1 else b, 0:n * (dv + 1)].rearrange("p (t e) -> p t e", t=n)
                        ins = dve.reciprocal(recip[:, b * n:(b + 1) * n], o[:, :, dv])
                    ins.then_inc(inverted, 1)
                    dve.wait_ge(inverted, at(NSB, s + 1))
                    for b in range(banks):
                        o = out_ps[:, s % 2 if banks == 1 else b, 0:n * (dv + 1)].rearrange("p (t e) -> p t e", t=n)
                        ins = dve.tensor_tensor(out_of(it)[:, SB * s + b * n:SB * s + (b + 1) * n, :], o[:, :, 0:dv],
                                                recip[:, b * n:(b + 1) * n].unsqueeze(2).to_broadcast([P, n, dv]), ALU.mult)
                    ins.then_inc(emitted, 1)

                for s in range(NSB):
                    maxima(s)
                    split_max(s)
                    put(s)
                    if s and not keep:
                        emit(s - 1)
                if not keep:
                    emit(NSB - 1)
            for_heads(dve, head)


def add_attention(nc, k, tag, image, X, ctx_out, w_out):
    with ExitStack() as c:
        m = Memory(nc, c)
        turn_ps, mix_ps = m.ps(f"{tag}_turn_ps", [P, 2, CH]), m.ps(f"{tag}_mix_ps", [P, 2, CH])
        flat = m.sb(f"{tag}_flat", [P, 2, CH])
        turned, copied, mixed, added = (m.sem(f"{tag}_{n}") for n in ("turned", "copied", "mixed", "added"))
        block = c.enter_context(nc.Block())

        @block.tensor
        def _(pe):
            for g in range(NSB + 1):
                if g < NSB:
                    if g >= 2:
                        pe.wait_ge(copied if w_out is not None else added, g - 1)
                    for t in range(SB):
                        mm = pe.transpose(turn_ps[:, g % 2, t * P:(t + 1) * P], ctx_out[:, SB * g + t, :], k["ident"][:, :])
                    mm.then_inc(turned, 1)
                if w_out is not None and g:
                    pe.wait_ge(copied, g)
                    if g >= 3:
                        pe.wait_ge(added, g - 2)
                    pe.matmul(mix_ps[:, (g - 1) % 2, :], w_out[:, :], flat[:, (g - 1) % 2, :], start=True, stop=True)\
                      .then_inc(mixed, 1)

        if w_out is not None:
            @block.scalar
            def _(act):
                for g in range(NSB):
                    act.wait_ge(turned, g + 1)
                    if g >= 2:
                        act.wait_ge(mixed, g - 1)
                    act.activation(flat[:, g % 2, :], turn_ps[:, g % 2, :], ACT.Copy).then_inc(copied, 1)

        @block.vector
        def _(dve):
            for g in range(NSB):
                dve.wait_ge(mixed if w_out is not None else turned, g + 1)
                src = mix_ps if w_out is not None else turn_ps
                x = X[:, image * T + g * CH:image * T + (g + 1) * CH]
                dve.tensor_tensor(x, x, src[:, g % 2, :], ALU.add).then_inc(added, 1)


PAIRS = ((0, 0), (0, 1), (1, 0), (1, 1), (0, 2), (2, 0))
ROWS = D3 * len(PAIRS)


def attention_l3(nc, k, dram, X):
    qk_parts = nc.dram_tensor("l3_qk_parts", [2, 3, P, T], BF16).ap()
    ctx_dram = nc.dram_tensor("l3_ctx", [P, T], F32).ap()
    den_dram, inv_dram = (nc.dram_tensor(f"l3_{n}", [NH3, T], F32) for n in ("den", "inv"))
    with ExitStack() as c:
        m = Memory(nc, c)
        w = m.sb("l3_w", [P, 3 * P])
        w_out = m.sb("l3_w_out", [P, P])
        XN = m.sb("l3_xn", [P, TOK])
        with ExitStack() as c2:
            w_loaded = Memory(nc, c2).sem("l3_w_loaded")
            block = c2.enter_context(nc.Block())

            @block.sync
            def _(sp):
                sp.dma_start(w[:, :], dram["L3_attn_w_attn"]).then_inc(w_loaded, 16)
                sp.dma_start(w_out[:, :], dram["L3_attn_w_proj"]).then_inc(w_loaded, 16)
                sp.wait_ge(w_loaded, 32)
        layer_norm(nc, k, "l3a_ln", X, XN, "eps5")
        v_all = m.sb("l3_v_all", [P, NH3, QT, D3 + 1])
        for b in range(BATCH):
            split_qkv(nc, k, f"l3p{b}", b, XN, w, v_all, qk_parts)
            with ExitStack() as c2:
                mm = Memory(nc, c2)
                bufs = [{"q": mm.sb(f"l3_q{b}{u}", [P, T], BF16), "k": mm.sb(f"l3_k{b}{u}", [P, T], BF16),
                         "v": mm.sb(f"l3_v{b}{u}", [P, QT, D3 + 1]), "out": mm.sb(f"l3_out{b}{u}", [D3 + 1, T])} for u in range(2)]
                for q in bufs:
                    q["minus_max"] = q["q"]
                with ExitStack() as c3:
                    ones = Memory(nc, c3).sem(f"l3_ones{b}")
                    block = c3.enter_context(nc.Block())

                    @block.vector
                    def _(dve):
                        for q in bufs:
                            dve.memset(q["k"][96:128, :], 1.0).then_inc(ones, 1)

                def score_max(pe, u, out, tile, k0, width):
                    return pe.matmul(out, bufs[u]["q"][0:ROWS, tile * P:(tile + 1) * P], bufs[u]["k"][0:ROWS, k0:k0 + width],
                                     start=True, stop=True)

                def score_exp(pe, u, out, j, q0, width):
                    return pe.matmul(out, bufs[u]["k"][0:ROWS + 3, j * P:(j + 1) * P], bufs[u]["q"][0:ROWS + 3, q0:q0 + width],
                                     start=True, stop=True)

                def feed(sp, u, it, sem):
                    for n, pair in enumerate(PAIRS):
                        for side, name in enumerate(("q", "k")):
                            rows = qk_parts[side, pair[side], ds(it * D3, D3), :]
                            sp.dma_start(bufs[u][name][n * D3:(n + 1) * D3, :], rows).then_inc(sem, 16)
                    sp.dma_start(bufs[u]["v"][:, :, :], v_all[:, ds(it, 1), :, :].rearrange("p h t e -> p (h t) e")).then_inc(sem, 16)

                def keep(sp, it, u, sem):
                    out = bufs[u]["out"]
                    sp.dma_start(ctx_dram[ds(it * D3, D3), :], out[0:D3, :]).then_inc(sem, 16)
                    sp.dma_start(den_dram.ap()[ds(it, 1), :], out[D3:D3 + 1, :]).then_inc(sem, 16)

                causal_attention(nc, k, f"l3s{b}", NH3, D3, 1.0 / D3 ** 0.5, bufs, score_max, score_exp, feed,
                                 2 * len(PAIRS) + 1, None, keep)
            add_heads(nc, f"l3f{b}", b, X, ctx_dram, den_dram, inv_dram, w_out)


def add_heads(nc, tag, image, X, ctx_dram, den_dram, inv_dram, w_out):
    with ExitStack() as c:
        m = Memory(nc, c)
        ctx_out, inv = m.sb(f"{tag}_ctx", [P, T]), m.sb(f"{tag}_inv", [P, T])
        den, small = m.sb(f"{tag}_den", [P, NH3 * T // P]), m.sb(f"{tag}_small", [P, NH3 * T // P])
        mix_ps = m.ps(f"{tag}_mix_ps", [P, 2, CH])
        loaded, den_loaded, inverted, inv_stored, inv_loaded, divided, mixed, added = (
            m.sem(f"{tag}_{n}") for n in ("loaded", "den_loaded", "inverted", "inv_stored", "inv_loaded", "divided",
                                          "mixed", "added"))
        block = c.enter_context(nc.Block())

        @block.sync
        def _(sp):
            wide = dict(den=den_dram.ap().rearrange("h (g x) -> (h g) x", g=P // NH3),
                        inv=inv_dram.ap().rearrange("h (g x) -> (h g) x", g=P // NH3))
            sp.dma_start(den[:, :], wide["den"]).then_inc(den_loaded, 16)
            sp.dma_start(ctx_out[:, :], ctx_dram).then_inc(loaded, 16)
            sp.wait_ge(inverted, 1)
            sp.dma_start(wide["inv"], small[:, :]).then_inc(inv_stored, 16)
            sp.wait_ge(inv_stored, 16)
            sp.dma_start(inv[:, :], bass.AP(tensor=inv_dram, offset=0, ap=[[T, NH3], [0, D3], [1, T]])).then_inc(inv_loaded, 16)

        @block.tensor
        def _(pe):
            for g in range(NSB):
                pe.wait_ge(divided, g + 1)
                if g >= 2:
                    pe.wait_ge(added, g - 1)
                pe.matmul(mix_ps[:, g % 2, :], w_out[:, :], ctx_out[:, g * CH:(g + 1) * CH], start=True, stop=True)\
                  .then_inc(mixed, 1)

        @block.gpsimd
        def _(pool):
            pool.wait_ge(loaded, 16)
            pool.wait_ge(inv_loaded, 16)
            for g in range(NSB):
                at = slice(g * CH, (g + 1) * CH)
                pool.tensor_tensor(ctx_out[:, at], ctx_out[:, at], inv[:, at], ALU.mult).then_inc(divided, 1)

        @block.vector
        def _(dve):
            dve.wait_ge(den_loaded, 16)
            dve.reciprocal(small[:, :], den[:, :]).then_inc(inverted, 1)
            for g in range(NSB):
                dve.wait_ge(mixed, g + 1)
                x = X[:, image * T + g * CH:image * T + (g + 1) * CH]
                dve.tensor_tensor(x, x, mix_ps[:, g % 2, :], ALU.add).then_inc(added, 1)


def split_qkv(nc, k, tag, b, XN, w, v_all, qk_parts):
    with ExitStack() as c:
        m = Memory(nc, c)
        qk_ps, v_ps = m.ps(f"{tag}_qk_ps", [P, 2, CH]), m.ps(f"{tag}_v_ps", [P, 2, CH])
        part = [m.sb(f"{tag}_part{n}", [P, T], BF16) for n in range(3)]
        rest = m.sb(f"{tag}_rest", [P, 2, CH])
        ready, first, rest1, second, third, stored, v_ready, v_copied = (
            m.sem(f"{tag}_{n}") for n in ("ready", "first", "rest1", "second", "third", "stored", "v_ready", "v_copied"))
        block = c.enter_context(nc.Block())
        NB = T // CH

        @block.tensor
        def _(pe):
            for g in range(2 * NB):
                if g >= 2:
                    pe.wait_ge(rest1, g - 1)
                pe.matmul(qk_ps[:, g % 2, :], w[:, g // NB * P:(g // NB + 1) * P],
                          XN[:, b * T + g % NB * CH:b * T + (g % NB + 1) * CH], start=True, stop=True).then_inc(ready, 1)
            for g in range(NB):
                if g >= 2:
                    pe.wait_ge(v_copied, g - 1)
                for t in range(4):
                    n = b * T + g * CH + t * P
                    mm = pe.matmul(v_ps[:, g % 2, t * P:(t + 1) * P], XN[:, n:n + P], w[:, 2 * P:3 * P], start=True, stop=True)
                mm.then_inc(v_ready, 1)

        @block.scalar
        def _(act):
            for g in range(2 * NB):
                at = slice(g % NB * CH, (g % NB + 1) * CH)
                if g == NB:
                    act.wait_ge(stored, 48)
                act.wait_ge(ready, g + 1)
                act.activation(part[0][:, at], qk_ps[:, g % 2, :], ACT.Copy).then_inc(first, 1)
                act.wait_ge(rest1, g + 1)
                act.activation(part[1][:, at], rest[:, g % 2, :], ACT.Copy).then_inc(second, 1)

        @block.vector
        def _(dve):
            dve.memset(v_all[:, :, :, D3:D3 + 1], 1.0)
            for g in range(2 * NB):
                at = slice(g % NB * CH, (g % NB + 1) * CH)
                dve.wait_ge(first, g + 1)
                dve.tensor_tensor(rest[:, g % 2, :], qk_ps[:, g % 2, :], part[0][:, at], ALU.subtract).then_inc(rest1, 1)
                dve.wait_ge(second, g + 1)
                dve.tensor_tensor(part[2][:, at], rest[:, g % 2, :], part[1][:, at], ALU.subtract).then_inc(third, 1)
            for g in range(NB):
                dve.wait_ge(v_ready, g + 1)
                src = v_ps[:, g % 2, :].rearrange("p (t h d) -> p h t d", t=4, h=NH3)
                for t in range(4):
                    ins = dve.tensor_copy(v_all[:, :, 4 * g + t, 0:D3], src[:, :, t, :])
                ins.then_inc(v_copied, 1)

        @block.sync
        def _(sp):
            for side in range(2):
                sp.wait_ge(third, NB * (side + 1))
                for n in range(3):
                    sp.dma_start(qk_parts[side, n], part[n][:, :]).then_inc(stored, 16)
            sp.wait_ge(stored, 96)


def attention_l2(nc, k, dram, X):
    with ExitStack() as c:
        m = Memory(nc, c)
        w = m.sb("l2_w", [P, 3, P])
        XN = m.sb("l2_xn", [P, TOK])
        q, kk = m.sb("l2_q", [P, T]), m.sb("l2_k", [P, T])
        v = m.sb("l2_v", [P, QT, P + 1])
        minus_max, ones = m.sb("l2_minus_max", [P, T], BF16), m.sb("l2_ones", [P, P], BF16)
        result = m.sb("l2_result", [P, QT, P])
        with ExitStack() as c2:
            mm = Memory(nc, c2)
            w_loaded, filled = mm.sem("l2_w_loaded"), mm.sem("l2_filled")
            block = c2.enter_context(nc.Block())

            @block.sync
            def _(sp):
                for n, name in enumerate(("L2_attn_Wq", "L2_attn_Wk", "L2_attn_Wv")):
                    sp.dma_start(w[:, n, :], dram[name]).then_inc(w_loaded, 16)
                sp.wait_ge(w_loaded, 48)

            @block.vector
            def _(dve):
                dve.memset(ones[:, :], 1.0).then_inc(filled, 1)
                dve.memset(v[:, :, P:P + 1], 1.0).then_inc(filled, 1)
        layer_norm(nc, k, "l2a_ln", X, XN, "eps5")
        for b in range(BATCH):
            project_qkv(nc, k, f"l2p{b}", b, XN, w, q, kk, v)

            def score_max(pe, u, out, tile, k0, width):
                return pe.matmul(out, q[:, tile * P:(tile + 1) * P], kk[:, k0:k0 + width], start=True, stop=True)

            def score_exp(pe, u, out, j, q0, width):
                pe.matmul(out, kk[:, j * P:(j + 1) * P], q[:, q0:q0 + width], start=True, stop=True)
                return pe.matmul(out, ones[96:99, :], minus_max[96:99, q0:q0 + width], start=False, stop=True,
                                 skip_group_check=True)

            causal_attention(nc, k, f"l2s{b}", 1, P, 1.0 / T ** 0.5, [{"minus_max": minus_max, "v": v}],
                             score_max, score_exp, None, 0, lambda it: result[:, :, :])
            add_attention(nc, k, f"l2f{b}", b, X, result, None)


def project_qkv(nc, k, tag, b, XN, w, q, kk, v):
    with ExitStack() as c:
        m = Memory(nc, c)
        ps = m.ps(f"{tag}_ps", [P, 4, CH])
        ready, copied, copied_v = m.sem(f"{tag}_ready"), m.sem(f"{tag}_copied"), m.sem(f"{tag}_copied_v")
        block = c.enter_context(nc.Block())
        NB = T // CH

        @block.tensor
        def _(pe):
            for g in range(NB):
                if g:
                    pe.wait_ge(copied, 2 * g)
                    pe.wait_ge(copied_v, g)
                at = slice(b * T + g * CH, b * T + (g + 1) * CH)
                for n in range(2):
                    pe.matmul(ps[:, n, :], w[:, n, :], XN[:, at], start=True, stop=True).then_inc(ready, 1)
                for t in range(4):
                    n = b * T + g * CH + t * P
                    mm = pe.matmul(ps[:, 2, t * P:(t + 1) * P], XN[:, n:n + P], w[:, 2, :], start=True, stop=True)
                mm.then_inc(ready, 1)

        @block.scalar
        def _(act):
            for g in range(NB):
                for n, dst in enumerate((q, kk)):
                    act.wait_ge(ready, 3 * g + n + 1)
                    act.activation(dst[:, g * CH:(g + 1) * CH], ps[:, n, :], ACT.Copy).then_inc(copied, 1)

        @block.vector
        def _(dve):
            for g in range(NB):
                dve.wait_ge(ready, 3 * g + 3)
                dve.tensor_copy(v[:, 4 * g:4 * g + 4, 0:P], ps[:, 2, :].rearrange("p (t e) -> p t e", t=4))\
                   .then_inc(copied_v, 1)


NE = 8


def experts_l2(nc, k, dram, X):
    with ExitStack() as c:
        m = Memory(nc, c)
        rw, rb = m.sb("moe_rw", [P, NE]), m.sb("moe_rb", [P, NE])
        ew, eb = m.sb("moe_ew", [P, NE, P]), m.sb("moe_eb", [NE, P])
        iota = m.sb("moe_iota", [P, NE])
        XN = m.sb("moe_xn", [P, TOK])
        with ExitStack() as c2:
            loaded = Memory(nc, c2).sem("moe_loaded")
            block = c2.enter_context(nc.Block())

            @block.sync
            def _(sp):
                sp.dma_start(rw[:, :], dram["L2_ffn_router_w"]).then_inc(loaded, 16)
                sp.dma_start(rb[:, :], dram["L2_ffn_router_b"].to_broadcast([P, NE])).then_inc(loaded, 16)
                sp.dma_start(ew[:, :, :], dram["L2_ffn_expert_w"].rearrange("e d c -> d e c")).then_inc(loaded, 16)
                sp.dma_start(eb[:, :], dram["L2_ffn_expert_b"]).then_inc(loaded, 16)
                sp.dma_start(iota[:, :], dram["c_iota"]).then_inc(loaded, 16)
                sp.wait_ge(loaded, 80)
        layer_norm(nc, k, "moe_ln", X, XN, "eps5")

        NT = TOK // P
        tile = m.sb("moe_tile", [P, 2, P])
        logits = m.sb("moe_logits", [P, 2, NE])
        best, where, wheref = m.sb("moe_best", [P, 2, 8]), m.sb("moe_where", [P, 2, 8], U32), m.sb("moe_wheref", [P, 2, 8])
        less = m.sb("moe_less", [P, 2, 2])
        e2, total, inv = m.sb("moe_e2", [P, 2, 1]), m.sb("moe_total", [P, 2, 1]), m.sb("moe_inv", [P, 2, 1])
        gate, gate2 = m.sb("moe_gate", [P, 2, NE]), m.sb("moe_gate2", [P, 2, NE])
        gate_t = m.sb("moe_gate_t", [NE, 2, P])
        mix = m.sb("moe_mix", [P, 2, P])
        route_ps = m.ps("moe_route_ps", [P, 2, CH])
        out_ps = m.ps("moe_out_ps", [P, 2, CH])
        expert_ps = m.ps("moe_expert_ps", [P, 2, 2, CH])
        taken, routed, expert_ready, gated, turned, biased, gate_copied, mixed, flat, added, e2_ready, small, acc = (
            m.sem(f"moe_{n}") for n in ("taken", "routed", "expert_ready", "gated", "turned", "biased", "gate_copied",
                                        "mixed", "flat", "added", "e2_ready", "small", "acc"))
        block = c.enter_context(nc.Block())

        @block.gpsimd
        def _(pool):
            with pool.Fori(0, NT // 2) as i:
                for u in range(2):
                    wait_apart(pool, expert_ready, i * 2 + u + 1)
                    pool.tensor_copy(tile[:, u, :], XN[:, ds(i * 2 * P + u * P, P)]).then_inc(taken, 1)

        @block.tensor
        def _(pe):
            pe.sem_inc(expert_ready, 2)
            pe.sem_inc(flat, 2)
            with pe.Fori(0, NT // 2) as i:
                for u in range(2):
                    pe.wait_ge(taken, i * 2 + u + 1)
                    pe.wait_ge(added, i * 2 + u + 1)
                    pe.matmul(route_ps[:, u, 0:NE], tile[:, u, :], rw[:, :], start=True, stop=True).then_inc(routed, 1)
                    pe.wait_ge(mixed, i * 2 + u + 1)
                    for n in range(2):
                        mm = pe.matmul(expert_ps[:, u, n, :], tile[:, u, :], ew[:, 4 * n:4 * n + 4, :], start=True, stop=True)
                    mm.then_inc(expert_ready, 1)
                for u in range(2):
                    pe.wait_ge(gated, i * 2 + u + 1)
                    pe.transpose(route_ps[0:NE, u, P:2 * P], gate[:, u, :], k["ident"][:, :]).then_inc(turned, 1)
                for u in range(2):
                    pe.wait_ge(gate_copied, i * 2 + u + 1)
                    pe.matmul(out_ps[:, u, 0:P], gate_t[:, u, :], eb[:, :], start=True, stop=True).then_inc(biased, 1)
                for u in range(2):
                    pe.wait_ge(mixed, i * 2 + u + 3)
                    pe.transpose(out_ps[:, u, P:2 * P], mix[:, u, :], k["ident"][:, :]).then_inc(flat, 1)

        @block.scalar
        def _(act):
            with act.Fori(0, NT // 2) as i:
                for u in range(2):
                    act.wait_ge(small, i * 8 + (u * 4 + 3))
                    act.activation(e2[:, u, :], less[:, u, 0:1], ACT.Exp).then_inc(e2_ready, 1)
                for u in range(2):
                    act.wait_ge(turned, i * 2 + u + 1)
                    act.activation(gate_t[:, u, :], route_ps[0:NE, u, P:2 * P], ACT.Copy).then_inc(gate_copied, 1)

        @block.vector
        def _(dve):
            dve.sem_inc(added, 2)
            dve.sem_inc(mixed, 2)
            with dve.Fori(0, NT // 2) as i:
                for u in range(2):
                    dve.wait_ge(routed, i * 2 + u + 1)
                    dve.tensor_tensor(logits[:, u, :], route_ps[:, u, 0:NE], rb[:, :], ALU.add).then_inc(small, 1)
                    wait_apart(dve, small, i * 8 + (u * 4 + 1))
                    dve.max(best[:, u, :], logits[:, u, :]).then_inc(small, 1)
                    dve.wait_ge(small, i * 8 + (u * 4 + 2))
                    dve.tensor_tensor(less[:, u, 0:1], best[:, u, 1:2], best[:, u, 0:1], ALU.subtract).then_inc(small, 1)
                    dve.max_index(where[:, u, :], best[:, u, :], logits[:, u, :]).then_inc(small, 1)
                for u in range(2):
                    def step(ins, n):
                        ins.then_inc(acc, 1)
                        dve.wait_ge(acc, i * 26 + (u * 5 + n))
                    dve.wait_ge(small, i * 8 + (u * 4 + 4))
                    step(dve.tensor_copy(wheref[:, u, :], where[:, u, :]), 1)
                    dve.wait_ge(e2_ready, i * 2 + u + 1)
                    step(dve.tensor_scalar(total[:, u, :], e2[:, u, :], 1.0, None, ALU.add), 2)
                    step(dve.reciprocal(inv[:, u, :], total[:, u, :]), 3)
                    step(dve.tensor_scalar(gate2[:, u, :], iota[:, :], wheref[:, u, 1:2], e2[:, u, :], ALU.is_equal, ALU.mult), 4)
                    step(dve.scalar_tensor_tensor(gate2[:, u, :], iota[:, :], wheref[:, u, 0:1], gate2[:, u, :],
                                                  ALU.is_equal, ALU.add), 5)
                    dve.tensor_scalar(gate[:, u, :], gate2[:, u, :], inv[:, u, :], None, ALU.mult).then_inc(gated, 1)
                for u in range(2):
                    dve.wait_ge(biased, i * 2 + u + 1)
                    dve.wait_ge(gated, i * 2 + u + 1)
                    dve.wait_ge(flat, i * 2 + u + 1)
                    dve.tensor_copy(mix[:, u, :], out_ps[:, u, 0:P]).then_inc(acc, 1)
                    dve.wait_ge(expert_ready, i * 2 + u + 3)
                    for e in range(NE):
                        dve.wait_ge(acc, i * 26 + (10 + u * 8 + e + 1))
                        ins = dve.scalar_tensor_tensor(mix[:, u, :], expert_ps[:, u, e // 4, e % 4 * P:(e % 4 + 1) * P],
                                                       gate[:, u, e:e + 1], mix[:, u, :], ALU.mult, ALU.add)
                        ins.then_inc(acc if e < NE - 1 else mixed, 1)
                for u in range(2):
                    dve.wait_ge(flat, i * 2 + u + 3)
                    x = X[:, ds(i * 2 * P + u * P, P)]
                    dve.tensor_tensor(x, x, out_ps[:, u, P:2 * P], ALU.add).then_inc(added, 1)


F32R = mybir.dt.float32r
HALF = T // 2
NJ = HALF // P
NC4 = HALF // CH
PAD = P
REG = (0, 1, 2, 3)


def filters_l3(nc, k, dram, X):
    lags = nc.dram_tensor("stu_lags", [NK, 2, 2, PAD + HALF], F32)
    n_dram = nc.dram_tensor("stu_n", [NK + 2, P, 2 * P], F32).ap()
    with ExitStack() as c:
        m = Memory(nc, c)
        reach, mu = m.sb("stu_reach", [P, 4]), m.sb("stu_mu", [P, 3, P])
        UR = m.sb("stu_ur", [P, BATCH, 2, NJ, P])
        filter_weights(nc, k, dram, n_dram, reach, mu)
        filter_lags(nc, k, dram, lags.ap())
        with ExitStack() as c2:
            XN = Memory(nc, c2).sb("stu_xn", [P, TOK])
            layer_norm(nc, k, "stu_ln", X, XN, "eps5")
            short_filter(nc, k, X, XN, UR, reach, mu)
        long_filter(nc, k, X, UR, reach, lags, n_dram)


def filter_weights(nc, k, dram, n_dram, reach, mu):
    with ExitStack() as c:
        m = Memory(nc, c)
        small = m.sb("fw_small", [P, 12, 8])
        where, wheref = m.sb("fw_where", [P, 8], U32), m.sb("fw_wheref", [P, 8])
        iota = m.sb("fw_iota", [P, 8])
        lw, gu, sig = m.sb("fw_lw", [P, 4]), m.sb("fw_gu", [P, 4]), m.sb("fw_sig", [P, NK])
        s1, s2 = m.sb("fw_s1", [P, NK]), m.sb("fw_s2", [P, NK])
        mats = m.sb("fw_mats", [P, 4, NK, P])
        acc = m.sb("fw_acc", [P, 2, NK, P])
        both = m.sb("fw_both", [P, NK, 2, P])
        mus = m.sb("fw_mus", [P, 4, 3, P])
        loaded, mats_loaded, step, exped, rooted, stored = (m.sem(f"fw_s{n}") for n in range(6))
        block = c.enter_context(nc.Block())
        MATS = 8

        @block.sync
        def _(sp):
            sp.dma_start(lw[:, :], dram["L3_ffn_log_weights"].to_broadcast([P, 4])).then_inc(loaded, 16)
            sp.dma_start(gu[:, :], dram["L3_ffn_gumbel"].to_broadcast([P, 4])).then_inc(loaded, 16)
            sp.dma_start(sig[:, :], dram["L3_ffn_sigma"].to_broadcast([P, NK])).then_inc(loaded, 16)
            sp.dma_start(iota[:, :], dram["c_iota"]).then_inc(loaded, 16)
            sp.dma_start(mus[:, :, :, :], dram["L3_ffn_M_u"].rearrange("i j d e -> d i j e")).then_inc(loaded, 16)
            for n, name in enumerate(("L3_ffn_M_phi_plus", "L3_ffn_M_phi_minus")):
                if n:
                    sp.wait_ge(step, 18)
                for i in range(4):
                    sp.dma_start(mats[:, i, :, :], dram[name][i].rearrange("k d e -> d k e")).then_inc(mats_loaded, 16)
            sp.wait_ge(step, 26)
            sp.dma_start(n_dram[0:NK].rearrange("k d e -> d k e"), both[:, :, :, :].rearrange("p k n e -> p k (n e)")).then_inc(stored, 16)
            sp.dma_start(n_dram[NK:NK + 2].rearrange("k d e -> d k e"), both[:, 0:2, :, :].rearrange("p k n e -> p k (n e)")).then_inc(stored, 16)
            sp.wait_ge(stored, 32)

        @block.scalar
        def _(act):
            act.wait_ge(loaded, 80)
            act.activation(s1[:, :], sig[:, :], ACT.Sqrt).then_inc(rooted, 1)
            act.wait_ge(rooted, 1)
            act.activation(s2[:, :], s1[:, :], ACT.Sqrt).then_inc(rooted, 1)
            act.wait_ge(step, 4)
            act.activation(small[:, 2, :], small[:, 1, :], ACT.Exp).then_inc(exped, 1)

        @block.vector
        def _(dve):
            count = [0]

            def then(ins):
                ins.then_inc(step, 1)
                count[0] += 1
                dve.wait_ge(step, count[0])

            logits, less, ex, soft, hot, wt = (small[:, n, :] for n in (0, 1, 2, 3, 4, 5))
            top, total, inv = small[:, 6, :], small[:, 7, 0:1], small[:, 7, 1:2]
            then(dve.memset(small[:, :, :], NEG))
            dve.wait_ge(loaded, 80)
            then(dve.tensor_tensor(logits[:, 0:4], lw[:, :], gu[:, :], ALU.add))
            then(dve.max(top, logits))
            then(dve.tensor_scalar(less, logits, top[:, 0:1], None, ALU.subtract))
            dve.wait_ge(exped, 1)
            then(dve.tensor_reduce(total, ex, AX, ALU.add))
            then(dve.reciprocal(inv, total))
            then(dve.tensor_scalar(soft, ex, inv, None, ALU.mult))
            then(dve.max(top, soft))
            then(dve.max_index(where[:, :], top, soft))
            then(dve.tensor_copy(wheref[:, :], where[:, :]))
            then(dve.tensor_scalar(hot, iota[:, :], wheref[:, 0:1], None, ALU.is_equal))
            then(dve.tensor_tensor(wt, hot, soft, ALU.subtract))
            then(dve.tensor_tensor(wt, wt, soft, ALU.add))
            for r in range(4):
                last = dve.tensor_reduce(reach[:, r:r + 1], hot[:, 0:4 - r], AX, ALU.add)
            then(last)
            for bank in range(2):
                dve.wait_ge(mats_loaded, 64 * (bank + 1))
                then(dve.tensor_scalar(acc[:, bank, :, :], mats[:, 0, :, :], wt[:, 0:1], None, ALU.mult))
                for i in range(1, 4):
                    then(dve.scalar_tensor_tensor(acc[:, bank, :, :], mats[:, i, :, :], wt[:, i:i + 1], acc[:, bank, :, :],
                                                  ALU.mult, ALU.add))
            dve.wait_ge(rooted, 2)
            root = s2[:, :].unsqueeze(2).to_broadcast([P, NK, P])
            for n, op in enumerate((ALU.add, ALU.subtract)):
                then(dve.tensor_tensor(both[:, :, n, :], acc[:, 0, :, :], acc[:, 1, :, :], op))
                then(dve.tensor_tensor(both[:, :, n, :], both[:, :, n, :], root, ALU.mult))
            then(dve.tensor_scalar(mu[:, :, :], mus[:, 0, :, :], wt[:, 0:1], None, ALU.mult))
            for i in range(1, 4):
                then(dve.scalar_tensor_tensor(mu[:, :, :], mus[:, i, :, :], wt[:, i:i + 1], mu[:, :, :], ALU.mult, ALU.add))


def filter_lags(nc, k, dram, lags):
    with ExitStack() as c:
        m = Memory(nc, c)
        seg = HALF // 4
        phi = m.sb("fl_phi", [P, seg])
        part = m.sb("fl_part", [P, 2, seg], F32R)
        zeros, zeros_r = m.sb("fl_zeros", [2 * NK, 2, PAD]), m.sb("fl_zeros_r", [2 * NK, 2, PAD], F32R)
        loaded, step, stored = m.sem("fl_loaded"), m.sem("fl_step"), m.sem("fl_stored")
        block = c.enter_context(nc.Block())

        @block.sync
        def _(sp):
            sp.dma_start(phi[:, :], dram["L3_ffn_phi"]).then_inc(loaded, 16)
            sp.wait_ge(step, 4)
            for n in range(2):
                for kk in range(NK):
                    sp.dma_start(lags[kk, :, n, PAD:PAD + HALF].rearrange("a (g x) -> a g x", g=4), part[kk * 8:kk * 8 + 8, n, :].bitcast(F32)).then_inc(stored, 16)
            sp.dma_start(lags[:, :, :, 0:PAD].rearrange("k a n x -> (k a) n x"), zeros_r[:, :, :].bitcast(F32)).then_inc(stored, 16)
            sp.wait_ge(stored, 16 * (2 * NK + 1))

        @block.vector
        def _(dve):
            dve.memset(zeros[:, :, :], 0.0).then_inc(step, 1)
            dve.wait_ge(step, 1)
            dve.tensor_copy(zeros_r[:, :, :], zeros[:, :, :]).then_inc(step, 1)
            dve.wait_ge(loaded, 16)
            dve.tensor_copy(part[:, 0, :], phi[:, :]).then_inc(step, 1)
            dve.wait_ge(step, 3)
            dve.tensor_tensor(part[:, 1, :], phi[:, :], part[:, 0, :].bitcast(F32), ALU.subtract).then_inc(step, 1)


def spans(c):
    return [(0, CH // 2, 0), (CH // 2, CH, 1)] if c == 0 else [(0, CH, 2 if c == 1 else 3)]


def short_filter(nc, k, X, XN, UR, reach, mu):
    with ExitStack() as c:
        m = Memory(nc, c)
        ps = m.ps("sf_ps", [P, 2, CH])
        ready, added, laid = m.sem("sf_ready"), m.sem("sf_added"), m.sem("sf_laid")
        block = c.enter_context(nc.Block())

        @block.tensor
        def _(pe):
            for g in range(NCH):
                if g >= 2:
                    pe.wait_ge(added, g - 1)
                edge = g % (NCH // 2) == 0
                for i in range(3):
                    o = i if edge else 0
                    mm = pe.matmul(ps[:, g % 2, o:CH], mu[:, i, :], XN[:, g * CH - i + o:(g + 1) * CH - i],
                                   start=(i == 0), stop=True, skip_group_check=True)
                mm.then_inc(ready, 1)

        @block.scalar
        def _(act):
            for b in range(BATCH):
                for par in range(2):
                    src = XN[:, b * T:(b + 1) * T].rearrange("p (j r a) -> p j r a", j=NJ, a=2)[:, :, ::-1, par]
                    act.activation(UR[:, b, par, :, :], src, ACT.Copy).then_inc(laid, 1)

        @block.vector
        def _(dve):
            for g in range(NCH):
                c8 = g % (NCH // 2)
                regime = 0 if c8 == 0 else 1 if c8 == 1 else 2 if c8 < 4 else 3
                x = X[:, g * CH:(g + 1) * CH]
                dve.wait_ge(ready, g + 1)
                dve.scalar_tensor_tensor(x, ps[:, g % 2, :], reach[:, regime:regime + 1], x, ALU.mult, ALU.add).then_inc(added, 1)


def long_filter(nc, k, X, UR, reach, lags, n_dram):
    with ExitStack() as c:
        m = Memory(nc, c)
        toep = [[[m.sb(f"lf_toep{kk}{a}{n}", [P, HALF + 2], F32R) for n in range(2)] for a in range(2)] for kk in range(2)]
        nk = m.sb("lf_nk", [P, 2, 2 * P])
        z = [m.sb(f"lf_z{n}", [P, 4, 2, 4, 2, P], F32R) for n in range(2)]
        z_ps = m.ps("lf_z_ps", [P, 4, 2, 2, P])
        y_ps = m.ps("lf_y_ps", [P, 2, 2, CH])
        toep_loaded = [m.sem(f"lf_toep_loaded{kk}") for kk in range(2)]
        nk_loaded = [m.sem(f"lf_nk_loaded{kk}") for kk in range(2)]
        z_ready, z_high, z_low, conv_done, summed = (m.sem(f"lf_{n}") for n in ("z_ready", "z_high", "z_low", "conv_done", "summed"))
        block = c.enter_context(nc.Block())
        ZB = 4
        GROUPS = 4

        @block.sync
        def _(sp):
            def load_toep(kk, filt):
                for a in range(2):
                    for n in range(2):
                        rows = bass.AP(tensor=lags, offset=(a * 2 + n) * (PAD + HALF) + PAD - P,
                                       ap=[[4 * (PAD + HALF), NK], [1, P], [1, HALF + 1]])
                        sp.dma_start(toep[kk][a][n][:, 0:HALF + 1].bitcast(F32),
                                     rows[ds(filt, 1)].rearrange("k r x -> (k r) x")).then_inc(toep_loaded[kk], 16)

            for kk in range(2):
                sp.dma_start(nk[:, kk, :], n_dram[kk]).then_inc(nk_loaded[kk], 16)
                load_toep(kk, kk)
            with sp.Fori(0, NK // 2 - 1) as i:
                for kk in range(2):
                    sp.wait_ge(z_ready, i * (4 * GROUPS * ZB) + (2 * kk + 2) * GROUPS * ZB)
                    sp.dma_start(nk[:, kk, :], n_dram[ds(i * 2 + kk + 2, 1)].rearrange("k d e -> (k d) e")).then_inc(nk_loaded[kk], 16)
                    sp.wait_ge(conv_done, i * (4 * GROUPS) + (2 * kk + 2) * GROUPS)
                    load_toep(kk, i * 2 + kk + 2)
            sp.wait_ge(z_ready, (NK // 2 - 1) * 4 * GROUPS * ZB + 2 * GROUPS * ZB)
            sp.dma_start(nk[:, 0, :], n_dram[NK]).then_inc(nk_loaded[0], 16)

        def units(eng, body):
            with eng.Fori(0, NK // 2) as i:
                for q in range(4):
                    body(lambda per, j, q=q: i * (4 * per) + (q * per + j), q % 2, q // 2, i)

        @block.tensor
        def _(pe):
            def sources(b, kk, group, ready_at):
                for n in range(ZB):
                    pe.wait_ge(z_low, ready_at(n))
                    par, half = n // 2, n % 2
                    for j in range(2):
                        mm = pe.matmul(z_ps[:, n, j, :, :], UR[:, b, par, 4 * group + 2 * half + j, :], nk[:, kk, :],
                                       start=(j == 0), stop=True, skip_group_check=True)
                    mm.then_inc(z_ready, 1)

            def convolve(c4, kk, at):
                pe.wait_ge(summed, at(GROUPS, GROUPS - 1 - c4 + 1))
                for J in range(4 * c4 + 3, -1, -1):
                    if J % 4 == 3 and c4 == GROUPS - 1:
                        pe.wait_ge(z_low, at(GROUPS * ZB, (GROUPS - J // 4) * ZB + ZB))
                    x0 = max(0, J - 4 * c4) * P
                    lag = CH * c4 - P * J + x0
                    for out_par in range(2):
                        for src_par in range(2):
                            a = out_par ^ src_par
                            late = 1 if (src_par, out_par) == (1, 0) else 0
                            first = J == 4 * c4 + 3 and src_par == 0
                            for zn, tn in ((0, 0), (0, 1), (1, 0)):
                                mm = pe.matmul(y_ps[:, c4 % 2, out_par, x0:CH], z[zn][:, J // 4, src_par, J % 4, a, :],
                                               toep[kk][a][tn][:, 1 - late + lag:1 - late + lag + CH - x0],
                                               start=(first and (zn, tn) == (0, 0)), stop=(J == 0 and src_par == 1),
                                               skip_group_check=True)
                mm.then_inc(conv_done, 1)

            pe.wait_ge(nk_loaded[0], 16)
            for g in range(GROUPS - 1, -1, -1):
                sources(0, 0, g, lambda n, g=g: (GROUPS - 1 - g) * ZB + n + 1)

            def unit(at, b, kk, i):
                if b == 0:
                    pe.wait_ge(toep_loaded[kk], i * 64 + 64)
                for g in range(GROUPS - 1, -1, -1):
                    convolve(g, kk, at)
                    if g == GROUPS - 1 and b == 1:
                        pe.wait_ge(nk_loaded[1 - kk], i * 16 + (16 if kk == 0 else 32))
                    sources(1 - b, kk if b == 0 else 1 - kk, g, lambda n: at(GROUPS * ZB, GROUPS * ZB + (GROUPS - 1 - g) * ZB + n + 1))
            units(pe, unit)

        @block.scalar
        def _(act):
            def high(g, at):
                for n in range(ZB):
                    act.wait_ge(z_ready, at(n + 1))
                    act.activation(z[0][:, g, n // 2, n % 2 * 2:n % 2 * 2 + 2, :, :], z_ps[:, n, :, :, :], ACT.Copy).then_inc(z_high, 1)

            for g in range(GROUPS - 1, -1, -1):
                high(g, lambda n: (GROUPS - 1 - g) * ZB + n)

            def unit(at, b, kk, i):
                for g in range(GROUPS - 1, -1, -1):
                    high(g, lambda n: at(GROUPS * ZB, GROUPS * ZB + (GROUPS - 1 - g) * ZB + n))
            units(act, unit)

        @block.vector
        def _(dve):
            dve.sem_inc(z_low, ZB)
            dve.sem_inc(summed, 2)

            def low(g, at):
                for n in range(ZB):
                    dve.wait_ge(z_high, at(n + 1))
                    at_z = (slice(None), g, n // 2, slice(n % 2 * 2, n % 2 * 2 + 2), slice(None), slice(None))
                    dve.tensor_tensor(z[1][at_z], z_ps[:, n, :, :, :], z[0][at_z].bitcast(F32), ALU.subtract).then_inc(z_low, 1)

            for g in range(GROUPS - 1, -1, -1):
                low(g, lambda n: (GROUPS - 1 - g) * ZB + n)

            def unit(at, b, kk, i):
                for g in range(GROUPS - 1, -1, -1):
                    dve.wait_ge(conv_done, at(GROUPS, GROUPS - g))
                    dve.wait_ge(summed, at(GROUPS, GROUPS - 1 - g + 2))
                    for out_par in range(2):
                        for x0, x1, regime in spans(g):
                            t0 = b * T + 2 * (CH * g + x0) + out_par
                            x = X[:, t0:t0 + 2 * (x1 - x0) - 1:2]
                            ins = dve.scalar_tensor_tensor(x, y_ps[:, g % 2, out_par, x0:x1], reach[:, regime:regime + 1], x,
                                                           ALU.mult, ALU.add)
                    ins.then_inc(summed, 1)
                    low(g, lambda n: at(GROUPS * ZB, GROUPS * ZB + (GROUPS - 1 - g) * ZB + n))
            units(dve, unit)


NTILE = (HW // TR) * (HW // TC)
KEYS = WR * WC
NKC = 3
RING = 2


def neighbourhood_l0(nc, k, dram, X):
    with ExitStack() as c:
        m = Memory(nc, c)
        ya, yb = m.sb("na_ya", [P, TOK]), m.sb("na_yb", [P, TOK])
        masks = m.sb("na_masks", [P, NMASK, KEYS], BF16)
        w = m.sb("na_w", [P, 2, 4 * P])
        bias = m.sb("na_bias", [P, 2, 4])
        ln = m.sb("na_ln", [P, 2])
        with ExitStack() as c2:
            mm = Memory(nc, c2)
            wide = mm.sb("na_masks_f32", [P, NMASK, KEYS])
            loaded, made = mm.sem("na_loaded"), mm.sem("na_made")
            block = c2.enter_context(nc.Block())

            @block.sync
            def _(sp):
                sp.dma_start(wide[:, :, :], dram["c_window"]).then_inc(loaded, 16)
                sp.dma_start(w[:, :, :], dram["L0_w"]).then_inc(loaded, 16)
                sp.dma_start(bias[:, :, :], dram["L0_bias"]).then_inc(loaded, 16)
                sp.dma_start(ln[:, :], dram["L0_ln"]).then_inc(loaded, 16)
                sp.wait_ge(loaded, 64)

            @block.vector
            def _(dve):
                dve.wait_ge(loaded, 64)
                dve.tensor_copy(masks[:, :, :], wide[:, :, :]).then_inc(made, 1)
        group_norm(nc, k, "na_gn", X, ya)
        for layer in range(2):
            src, dst = (ya, yb) if layer == 0 else (yb, ya)
            neighbourhood(nc, k, f"na{layer}", layer, dram, src, dst, masks, w[:, layer, :], bias[:, layer, :])
        layer_norm(nc, k, "na_lnf", ya, ya, "eps5", gain=ln[:, 0:1], shift=ln[:, 1:2], add_to=X)


def neighbourhood(nc, k, tag, layer, dram, src, dst, masks, w, bias):
    with ExitStack() as c:
        m = Memory(nc, c)
        table = m.sb(f"{tag}_table", [P, NH0, BR, BC])
        keys_in, q_in = m.sb(f"{tag}_keys_in", [P, RING, KEYS]), m.sb(f"{tag}_q_in", [P, RING, P])
        kt, qt = m.sb(f"{tag}_kt", [P, RING, KEYS]), m.sb(f"{tag}_qt", [P, RING, P])
        vt = m.sb(f"{tag}_vt", [KC, RING, NKC, NH0, D0 + 1])
        neg = m.sb(f"{tag}_neg", [P, RING, KEYS])
        low = m.sb(f"{tag}_low", [P, RING])
        prob = m.sb(f"{tag}_prob", [P, RING, KEYS])
        prob_t = m.sb(f"{tag}_prob_t", [KC, RING, NKC * P])
        recip = m.sb(f"{tag}_recip", [P, NH0])
        mean, mean_t = m.sb(f"{tag}_mean", [P, RING, P]), m.sb(f"{tag}_mean_t", [P, RING, P])
        k_ps, qv_ps = m.ps(f"{tag}_k_ps", [P, CH]), m.ps(f"{tag}_qv_ps", [P, CH])
        s_ps, t_ps = m.ps(f"{tag}_s_ps", [P, RING, CH]), m.ps(f"{tag}_t_ps", [P, RING, CH])
        o_ps, f_ps = m.ps(f"{tag}_o_ps", [P, CH]), m.ps(f"{tag}_f_ps", [P, CH])
        names = ("table_loaded", "taken", "k_ready", "k_copied", "qv_ready", "qv_copied", "s_ready", "s_read",
                 "p_ready", "turned", "t_copied", "o_ready", "inverted", "mean_ready", "mean_turned",
                 "mean_copied", "y_ready", "y_copied", "ones_set")
        (table_loaded, taken, k_ready, k_copied, qv_ready, qv_copied, s_ready, s_read, p_ready, turned, t_copied,
         o_ready, inverted, mean_ready, mean_turned, mean_copied, y_ready, y_copied, ones_set) = (
            m.sem(f"{tag}_{n}") for n in names)
        block = c.enter_context(nc.Block())
        G = NTILE * NH0

        def grid(t):
            return t // (HW // TC), t % (HW // TC)

        def view(y, b, r0, nr, c0, ncol):
            return y[:, :].rearrange("p (b r c) -> p b r c", b=BATCH, r=HW)[:, ds(b, 1), r0:r0 + nr, c0:c0 + ncol]\
                .rearrange("p b r c -> p (b r) c")

        def images(eng, body):
            with eng.Fori(0, BATCH) as b:
                body(b, lambda per, j: b * per + j)

        @block.sync
        def _(sp):
            for a in range(TR):
                for h in range(NH0):
                    rows = bass.AP(tensor=dram["L0_rpb"].tensor, offset=((layer * NH0 + h) * PR + TR - 1 - a) * PC,
                                   ap=[[1, TC], [PC, BR], [1, BC]])
                    sp.dma_start(table[a * TC:(a + 1) * TC, h, :, :], rows).then_inc(table_loaded, 16)
            sp.wait_ge(table_loaded, 16 * TR * NH0)

        @block.gpsimd
        def _(pool):
            def image(b, at):
                for t in range(NTILE):
                    gr, gc = grid(t)
                    wait_apart(pool, qv_ready, at(NTILE, t + 1))
                    pool.tensor_copy(keys_in[:, t % RING, :].rearrange("p (r c) -> p r c", r=WR),
                                     view(src, b, ROW0[gr], WR, COL0[gc], WC))
                    pool.tensor_copy(q_in[:, t % RING, :].rearrange("p (r c) -> p r c", r=TR)[:, :, ::-1],
                                     view(src, b, gr * TR, TR, gc * TC, TC)).then_inc(taken, 1)
            images(pool, image)

        @block.tensor
        def _(pe):
            pe.sem_inc(qv_ready, RING)
            pe.wait_ge(ones_set, 1)

            def image(b, at):
                def project(t):
                    pe.wait_ge(taken, at(NTILE, t + 1))
                    pe.wait_ge(k_copied, at(NTILE, t + 1))
                    keys = keys_in[:, t % RING, :]
                    pe.matmul(k_ps[:, 0:KEYS], w[:, P:2 * P], keys, start=True, stop=True).then_inc(k_ready, 1)
                    pe.wait_ge(qv_copied, at(NTILE, t + 1))
                    pe.matmul(qv_ps[:, 0:P], w[:, 0:P], q_in[:, t % RING, :], start=True, stop=True, skip_group_check=True)
                    for n in range(NKC):
                        mm = pe.matmul(qv_ps[0:KC, (n + 1) * P:(n + 2) * P], keys[:, n * KC:(n + 1) * KC], w[:, 2 * P:3 * P],
                                       start=False, stop=True, skip_group_check=True)
                    mm.then_inc(qv_ready, 1)

                def score(g):
                    t, h = g // NH0, g % NH0
                    pe.wait_ge(s_read, at(G, g + 1))
                    if h == 0:
                        pe.wait_ge(k_copied, at(NTILE, t + 2))
                        pe.wait_ge(qv_copied, at(NTILE, t + 2))
                    rows = slice(h * D0, (h + 1) * D0)
                    pe.matmul(s_ps[:, g % RING, 0:KEYS], qt[rows, t % RING, :], kt[rows, t % RING, :], start=True, stop=True)
                    pe.matmul(s_ps[:, g % RING, 0:KEYS], k["ident16"][:, :], masks[:, MASK_OF[t], :], start=False, stop=True,
                              skip_group_check=True).then_inc(s_ready, 1)

                def turn(g):
                    pe.wait_ge(p_ready, at(G, g + 1 + RING))
                    pe.wait_ge(t_copied, at(G, g + 1))
                    for n in range(NKC):
                        mm = pe.transpose(t_ps[0:KC, g % RING, n * P:(n + 1) * P], prob[:, g % RING, n * KC:(n + 1) * KC],
                                          k["ident"][:, :])
                    mm.then_inc(turned, 1)

                def weigh(g):
                    t, h = g // NH0, g % NH0
                    pe.wait_ge(t_copied, at(G, g + 1 + RING))
                    if h == 0:
                        pe.wait_ge(mean_ready, at(NTILE, t + 1))
                    for n in range(NKC):
                        mm = pe.matmul(o_ps[:, h * (D0 + 1):(h + 1) * (D0 + 1)], prob_t[:, g % RING, n * P:(n + 1) * P],
                                       vt[:, t % RING, n, h, :], start=(h == 0 and n == 0), stop=(n == NKC - 1),
                                       skip_group_check=True)
                    mm.then_inc(o_ready, 1)

                def finish(t, part):
                    if part == 0:
                        pe.wait_ge(mean_ready, at(NTILE, t + 2))
                        pe.wait_ge(mean_copied, at(NTILE, t + 1))
                        pe.transpose(f_ps[:, 0:P], mean[:, t % RING, :], k["ident"][:, :]).then_inc(mean_turned, 1)
                    else:
                        pe.wait_ge(mean_copied, at(NTILE, t + 2))
                        pe.wait_ge(y_copied, at(NTILE, t + 1))
                        pe.matmul(f_ps[:, P:2 * P], w[:, 3 * P:4 * P], mean_t[:, t % RING, :], start=True, stop=True)\
                          .then_inc(y_ready, 1)

                project(0)
                for g in range(G + 5):
                    if g < G:
                        if g % NH0 == 0 and g // NH0 + 1 < NTILE:
                            project(g // NH0 + 1)
                        score(g)
                    if 1 <= g <= G:
                        turn(g - 1)
                    if 2 <= g <= G + 1:
                        weigh(g - 2)
                    for part in range(2):
                        if g >= 6 + part and (g - 6 - part) % NH0 == 0 and (g - 6 - part) // NH0 < NTILE:
                            finish((g - 6 - part) // NH0, part)
            images(pe, image)

        @block.scalar
        def _(act):
            act.sem_inc(k_copied, 1)
            act.sem_inc(p_ready, RING)
            act.sem_inc(t_copied, RING)
            act.sem_inc(mean_copied, 1)
            act.sem_inc(y_copied, 1)

            def image(b, at):
                def keys(t):
                    act.wait_ge(k_ready, at(NTILE, t + 1))
                    act.activation(kt[:, t % RING, :], k_ps[:, 0:KEYS], ACT.Identity, bias=bias[:, 1:2]).then_inc(k_copied, 1)

                keys(0)
                for g in range(G + 5):
                    if g < G:
                        act.wait_ge(s_read, at(G, g + 1 + RING))
                        act.wait_ge(turned, at(G, g + 1))
                        act.activation(prob[:, g % RING, :], neg[:, g % RING, :], ACT.Exp, scale=-1.0,
                                       bias=low[:, g % RING:g % RING + 1]).then_inc(p_ready, 1)
                        if g % NH0 == 0 and g // NH0 + 1 < NTILE:
                            keys(g // NH0 + 1)
                    if 1 <= g <= G:
                        act.wait_ge(turned, at(G, g + RING))
                        act.wait_ge(o_ready, at(G, g))
                        act.activation(prob_t[:, (g - 1) % RING, :], t_ps[0:KC, (g - 1) % RING, 0:NKC * P], ACT.Copy)\
                           .then_inc(t_copied, 1)
                    if g >= 6 and (g - 6) % NH0 == 0 and (g - 6) // NH0 < NTILE:
                        t = (g - 6) // NH0
                        act.wait_ge(mean_turned, at(NTILE, t + 1))
                        act.activation(mean_t[:, t % RING, :], f_ps[:, 0:P], ACT.Identity, bias=bias[:, 2:3])\
                           .then_inc(mean_copied, 1)
                    if g >= 7 and (g - 7) % NH0 == 0 and (g - 7) // NH0 < NTILE:
                        t = (g - 7) // NH0
                        gr, gc = grid(t)
                        act.wait_ge(y_ready, at(NTILE, t + 1))
                        act.activation(view(dst, b, gr * TR, TR, gc * TC, TC), f_ps[:, P:2 * P].rearrange("p (r c) -> p r c", r=TR)[:, :, ::-1],
                                       ACT.Identity, bias=bias[:, 3:4]).then_inc(y_copied, 1)
            images(act, image)

        @block.vector
        def _(dve):
            dve.wait_ge(table_loaded, 16 * TR * NH0)
            dve.memset(vt[:, :, :, :, D0:D0 + 1], 1.0).then_inc(ones_set, 1)
            dve.sem_inc(qv_copied, 1)
            dve.sem_inc(s_read, RING)
            dve.sem_inc(mean_ready, 1)
            dve.sem_inc(turned, RING)
            dve.sem_inc(o_ready, RING)

            def image(b, at):
                def queries_values(t):
                    dve.wait_ge(qv_ready, at(NTILE, t + 1 + RING))
                    dve.tensor_scalar(qt[:, t % RING, :], qv_ps[:, 0:P], bias[:, 0:1], D0 ** -0.5, ALU.add, ALU.mult)
                    if t >= RING:
                        dve.wait_ge(o_ready, at(G, (t - RING + 1) * NH0 + RING))
                    dve.tensor_copy(vt[:, t % RING, :, :, 0:D0], qv_ps[0:KC, P:4 * P].rearrange("p (n h d) -> p n h d", n=NKC, h=NH0))\
                       .then_inc(qv_copied, 1)

                queries_values(0)
                for g in range(G + 2):
                    if g < G:
                        t, h = g // NH0, g % NH0
                        gr, gc = grid(t)
                        r0, c0 = ROW0[gr] - gr * TR + OFF_R, COL0[gc] - gc * TC + OFF_C
                        dve.wait_ge(s_ready, at(G, g + 1))
                        wait_apart(dve, p_ready, at(G, g + 1))
                        dve.tensor_tensor_reduce(neg[:, g % RING, :].rearrange("p (r c) -> p r c", r=WR),
                                                 s_ps[:, g % RING, 0:KEYS].rearrange("p (r c) -> p r c", r=WR),
                                                 table[:, h, r0:r0 + WR, c0:c0 + WC], -1.0, -NEG * 1e8, ALU.add, ALU.min,
                                                 low[:, g % RING:g % RING + 1]).then_inc(s_read, 1)
                        if h == 0 and t + 1 < NTILE:
                            queries_values(t + 1)
                    if g >= 5 and (g - 5) % NH0 == 0:
                        t = (g - 5) // NH0
                        dve.wait_ge(o_ready, at(G, (t + 1) * NH0 + RING))
                        dve.wait_ge(mean_ready, at(NTILE, t + 1))
                        o = o_ps[:, 0:NH0 * (D0 + 1)].rearrange("p (h e) -> p h e", h=NH0)
                        dve.reciprocal(recip[:, :], o[:, :, D0]).then_inc(inverted, 1)
                        dve.wait_ge(inverted, at(NTILE, t + 1))
                        dve.wait_ge(mean_turned, at(NTILE, t - 1)) if t >= RING else None
                        dve.tensor_tensor(mean[:, t % RING, :].rearrange("p (h d) -> p h d", h=NH0), o[:, :, 0:D0],
                                          recip[:, :].unsqueeze(2).to_broadcast([P, NH0, D0]), ALU.mult).then_inc(mean_ready, 1)
            images(dve, image)


NHF = DIN // P
NROW = DTR + 2 * NST
LOW = 64
CPI = T // CH
UNITS = NST * NHF
A_RING, U_RING, H_RING, HC_RING = 4, 4, 2, 4


def mamba_l1(nc, k, dram, X):
    with ExitStack() as c:
        m = Memory(nc, c)
        XN = m.sb("mb_xn", [P, TOK + CH])
        w_in, w_x = m.sb("mb_w_in", [P, 2 * DIN]), m.sb("mb_w_x", [P, NHF, NROW])
        w_dt, w_out = m.sb("mb_w_dt", [DTR, DIN]), m.sb("mb_w_out", [P, NHF, P])
        cols = m.sb("mb_cols", [P, NHF, 7])
        norm, a_log, a = m.sb("mb_norm", [P, 2]), m.sb("mb_a_log", [P, NHF, NST]), m.sb("mb_a", [P, NHF, NST])
        one = m.sb("mb_one", [P, 1])
        pick = m.sb("mb_pick", [LOW + NROW, 2 * NST, P], F32R)
        dbl = m.sb("mb_dbl", [LOW + NROW, 2, CH], F32R)
        with ExitStack() as c2:
            mm = Memory(nc, c2)
            wide = mm.sb("mb_pick_f32", [LOW + NROW, 2 * NST, P])
            loaded, step, exped = mm.sem("mb_loaded"), mm.sem("mb_step"), mm.sem("mb_exped")
            cleared = mm.sem("mb_cleared")
            block = c2.enter_context(nc.Block())

            @block.sync
            def _(sp):
                for dst, name in ((w_in, "L1_w_in"), (w_dt, "L1_w_dt"), (norm, "L1_norm")):
                    sp.dma_start(dst[:, :], dram[name]).then_inc(loaded, 16)
                for dst, name in ((w_x, "L1_w_x"), (w_out, "L1_w_out"), (cols, "L1_cols"), (a_log, "L1_a_log")):
                    sp.dma_start(dst[:, :, :], dram[name]).then_inc(loaded, 16)
                sp.wait_ge(cleared, 1)
                for row in (0, LOW):
                    sp.dma_start(wide[row:row + NROW, :, :], dram["c_pick"]).then_inc(loaded, 16)
                sp.wait_ge(loaded, 144)

            @block.scalar
            def _(act):
                act.wait_ge(loaded, 144)
                act.activation(a[:, :, :], a_log[:, :, :], ACT.Exp).then_inc(exped, 1)

            @block.vector
            def _(dve):
                dve.memset(wide[:, :, :], 0.0).then_inc(cleared, 1)
                dve.memset(one[:, :], 1.0)
                dve.memset(XN[:, TOK:TOK + CH], 0.0)
                dve.memset(dbl[:, :, :].bitcast(F32), 0.0)
                dve.wait_ge(loaded, 144)
                dve.tensor_copy(pick[:, :, :], wide[:, :, :]).then_inc(step, 1)
                dve.wait_ge(exped, 1)
                dve.tensor_scalar(a[:, :, :], a[:, :, :], -1.0, None, ALU.mult).then_inc(step, 1)
        group_norm(nc, k, "mb_gn", X, XN)
        layer_norm(nc, k, "mb_ln", XN, XN, "eps5", gain=norm[:, 0:1], shift=norm[:, 1:2])
        selective_scan(nc, k, X, XN, w_in, w_x, w_dt, w_out, cols, a, one, pick, dbl)


def selective_scan(nc, k, X, XN, w_in, w_x, w_dt, w_out, cols, a, one, pick, dbl):
    with ExitStack() as c:
        m = Memory(nc, c)
        TAP = NCONV - 1
        xin, conv = m.sb("ss_xin", [P, NHF, TAP + CH]), m.sb("ss_conv", [P, NHF, CH])
        xc, gate = m.sb("ss_xc", [P, 2, NHF, CH]), m.sb("ss_gate", [P, 2, NHF, CH])
        delta, dx = m.sb("ss_delta", [P, 2, NHF, CH]), m.sb("ss_dx", [P, 2, NHF, CH])
        dt = m.sb("ss_dt", [DTR, CH])
        mag, em, ln1, err, relu = (m.sb(f"ss_{n}", [P, NHF, CH]) for n in ("mag", "em", "ln1", "err", "relu"))
        b_row = m.sb("ss_b_row", [P, 2, CH])
        decay, drive = m.sb("ss_decay", [P, A_RING, CH]), m.sb("ss_drive", [P, U_RING, CH])
        h, hc = m.sb("ss_h", [P, H_RING, CH]), m.sb("ss_hc", [P, HC_RING, CH])
        state = m.sb("ss_state", [P, UNITS])
        y, out_sb = m.sb("ss_y", [P, NHF, CH]), m.sb("ss_out", [P, CH])
        g_ps, f_ps = m.ps("ss_g_ps", [P, 2, CH]), m.ps("ss_f_ps", [P, CH])
        b_ps, c_ps, y_ps = m.ps("ss_b_ps", [P, CH]), m.ps("ss_c_ps", [P, 2, CH]), m.ps("ss_y_ps", [P, NHF, CH])
        names = ("xin_ready", "haloed", "xin_copied", "z_ready", "convolved", "silued", "rows_ready", "rows_copied",
                 "rows_low", "dt_ready", "mag_done", "em_done", "ln_done", "relued", "err_done", "delta_done", "dx_done",
                 "b_ready", "b_copied", "c_ready", "decayed", "driven", "scanned", "kept", "weighed", "summed",
                 "y_done", "gated", "out_ready", "out_copied", "added", "reset")
        S = {n: m.sem(f"ss_{n}") for n in names}
        block = c.enter_context(nc.Block())

        def chunks(eng, first, body):
            with eng.Fori(0, BATCH) as b:
                first(Place(b, 0, 0))
                with eng.Fori(0, CPI // 2) as i:
                    for u in range(2):
                        body(Place(b, i, u), Place(b, i, u + 1))

        class Place:

            def __init__(self, b, i, u):
                self.b, self.i, self.u, self.buf = b, i, u, u % 2

            def unit(self, per, j):
                return self.b * (CPI * per) + self.i * (2 * per) + (self.u * per + j)

            def round(self, per, j):
                return self.b * ((CPI + 1) * per) + self.i * (2 * per) + (self.u * per + j)

            def tokens(self):
                return ds(self.b * T + self.i * (2 * CH) + self.u * CH, CH)

        def run(steps, rnd, slot=None):
            for at, step in steps:
                if slot is None or at == slot:
                    step(rnd)

        @block.tensor
        def _(pe):
            def into(rnd, first, ready):
                for n in range(2):
                    mm = pe.matmul(g_ps[:, n, :], w_in[:, (first + n) * P:(first + n + 1) * P], XN[:, rnd.tokens()],
                                   start=True, stop=True)
                    mm.then_inc(S[ready], 1)

            def project_x(rnd):
                pe.wait_ge(S["relued"], rnd.round(2, 2))
                into(rnd, 0, "xin_ready")

            def project_z(rnd):
                pe.wait_ge(S["xin_copied"], rnd.round(2, 2))
                into(rnd, 2, "z_ready")

            def project_rows(rnd):
                pe.wait_ge(S["silued"], rnd.round(4, 4))
                for n in range(NHF):
                    mm = pe.matmul(g_ps[0:NROW, 0, :], w_x[:, n, :], xc[:, rnd.buf, n, :], start=(n == 0), stop=(n == NHF - 1))
                mm.then_inc(S["rows_ready"], 1)

            def project_dt(rnd):
                pe.wait_ge(S["rows_copied"], rnd.round(2, 2))
                pe.wait_ge(S["rows_low"], rnd.round(1, 1))
                for n in (1, 0):
                    pe.matmul(g_ps[:, n, :], w_dt[:, n * P:(n + 1) * P], dt[:, :], start=True, stop=True).then_inc(S["dt_ready"], 1)

            steps = [(2, project_x), (5, project_z), (16, project_rows), (18, project_dt)]

            def spread(at, buf, n, n_of):
                pe.wait_ge(S["b_copied"], n_of(NST, n + 1))
                pe.matmul(b_ps[:, :], pick[:, n, :], dbl[:, buf, :], start=True, stop=True).then_inc(S["b_ready"], 1)
                pe.wait_ge(S["weighed"], n_of(UNITS, 2 * n + 2))
                pe.matmul(c_ps[:, n % 2, :], pick[:, NST + n, :], dbl[:, buf, :], start=True, stop=True).then_inc(S["c_ready"], 1)

            def first(rnd):
                run(steps, rnd)

            def body(ch, rnd):
                spread(ch, ch.buf, 0, ch.unit)
                for s in range(UNITS):
                    if s % 2 == 0 and s // 2 + 1 < NST:
                        spread(ch, ch.buf, s // 2 + 1, ch.unit)
                    run(steps, rnd, s)
                    for v in ([s - 1] if s else []) + ([s] if s == UNITS - 1 else []):
                        if v == 0:
                            pe.wait_ge(S["y_done"], ch.unit(NHF, NHF))
                        pe.wait_ge(S["weighed"], ch.unit(UNITS, v + 1 + 4))
                        pe.matmul(y_ps[:, v % 2, :], k["ident"][:, :], hc[:, v % HC_RING, :], start=(v < 2),
                                  stop=(v >= UNITS - 2)).then_inc(S["summed"], 1)
                pe.wait_ge(S["gated"], ch.unit(NHF, NHF))
                pe.wait_ge(S["out_copied"], ch.unit(1, 1))
                for n in range(NHF):
                    mm = pe.matmul(f_ps[:, :], w_out[:, n, :], y[:, n, :], start=(n == 0), stop=(n == NHF - 1))
                mm.then_inc(S["out_ready"], 1)
            chunks(pe, first, body)

        @block.scalar
        def _(act):
            act.sem_inc(S["b_copied"], 1)
            act.sem_inc(S["out_copied"], 1)

            def copy_x(rnd):
                act.wait_ge(S["haloed"], rnd.round(1, 1))
                for n in range(NHF):
                    act.wait_ge(S["xin_ready"], rnd.round(2, n + 1))
                    act.activation(xin[:, n, TAP:TAP + CH], g_ps[:, n, :], ACT.Copy).then_inc(S["xin_copied"], 1)

            def silu(rnd):
                for n in range(NHF):
                    act.wait_ge(S["z_ready"], rnd.round(2, n + 1))
                    act.activation(gate[:, rnd.buf, n, :], g_ps[:, n, :], ACT.Silu).then_inc(S["silued"], 1)
                for n in range(NHF):
                    act.wait_ge(S["convolved"], rnd.round(8, 8 + 7 + n))
                    act.activation(xc[:, rnd.buf, n, :], conv[:, n, :], ACT.Silu, bias=cols[:, n, 4:5]).then_inc(S["silued"], 1)

            def copy_rows(rnd):
                act.wait_ge(S["rows_ready"], rnd.round(1, 1))
                act.activation(dbl[0:NROW, rnd.buf, :], g_ps[0:NROW, 0, :], ACT.Copy).then_inc(S["rows_copied"], 1)
                act.activation(dt[:, :], g_ps[0:DTR, 0, :], ACT.Copy).then_inc(S["rows_copied"], 1)

            def softplus(rnd):
                for n in (1, 0):
                    act.wait_ge(S["dt_ready"], rnd.round(2, 2 - n))
                    act.activation(mag[:, n, :], g_ps[:, n, :], ACT.Abs, bias=cols[:, n, 5:6]).then_inc(S["mag_done"], 1)
                act.wait_ge(S["mag_done"], rnd.round(2, 2))
                act.activation(em[:, :, :], mag[:, :, :], ACT.Exp, scale=-1.0).then_inc(S["em_done"], 1)
                act.wait_ge(S["em_done"], rnd.round(1, 1))
                act.activation(ln1[:, :, :], em[:, :, :], ACT.Ln, bias=one[:, :]).then_inc(S["ln_done"], 1)

            steps = [(4, copy_x), (14, silu), (17, copy_rows), (19, softplus)]

            def first(rnd):
                run(steps, rnd)

            def body(ch, rnd):
                for s in range(UNITS):
                    n, half = s // 2, s % 2
                    if half == 0:
                        act.wait_ge(S["b_ready"], ch.unit(NST, n + 1))
                        act.wait_ge(S["driven"], ch.unit(UNITS, 2 * n + 2))
                        act.activation(b_row[:, n % 2, :], b_ps[:, :], ACT.Copy).then_inc(S["b_copied"], 1)
                    if s == 0:
                        act.wait_ge(S["delta_done"], ch.round(4, 4))
                    act.wait_ge(S["scanned"], ch.unit(UNITS, s + 1))
                    act.activation(decay[:, s % A_RING, :], delta[:, ch.buf, half, :], ACT.Exp, scale=a[:, half, n:n + 1])\
                       .then_inc(S["decayed"], 1)
                    run(steps, rnd, s)
                act.wait_ge(S["out_ready"], ch.unit(1, 1))
                act.wait_ge(S["added"], ch.unit(1, 1))
                act.activation(out_sb[:, :], f_ps[:, :], ACT.Copy).then_inc(S["out_copied"], 1)
            chunks(act, first, body)

        @block.gpsimd
        def _(pool):
            pool.sem_inc(S["driven"], 4)
            pool.sem_inc(S["added"], 1)

            def halo(rnd):
                wait_apart(pool, S["convolved"], rnd.round(8, 8))
                pool.tensor_copy(xin[:, :, 0:TAP], xin[:, :, CH:CH + TAP]).then_inc(S["haloed"], 1)

            def log_error(rnd):
                wait_apart(pool, S["em_done"], rnd.round(1, 1))
                pool.tensor_scalar(err[:, :, :], em[:, :, :], 1.0, 1.0, ALU.add, ALU.subtract).then_inc(S["err_done"], 1)
                pool.wait_ge(S["err_done"], rnd.round(2, 1))
                pool.tensor_tensor(err[:, :, :], em[:, :, :], err[:, :, :], ALU.subtract).then_inc(S["err_done"], 1)

            def times_x(rnd):
                pool.wait_ge(S["delta_done"], rnd.round(4, 4))
                pool.tensor_tensor(dx[:, rnd.buf, :, :], delta[:, rnd.buf, :, :], xc[:, rnd.buf, :, :], ALU.mult)\
                    .then_inc(S["dx_done"], 1)

            steps = [(3, halo), (20, log_error), (25, times_x)]

            def first(rnd):
                wait_apart(pool, S["convolved"], rnd.round(8, 8))
                pool.memset(xin[:, :, 0:TAP], 0.0).then_inc(S["haloed"], 1)
                run(steps[1:], rnd)

            def body(ch, rnd):
                for s in range(UNITS):
                    n, half = s // 2, s % 2
                    pool.wait_ge(S["b_copied"], ch.unit(NST, n + 2))
                    if s == 0:
                        pool.wait_ge(S["dx_done"], ch.round(1, 1))
                    pool.wait_ge(S["scanned"], ch.unit(UNITS, s + 1))
                    pool.tensor_tensor(drive[:, s % U_RING, :], dx[:, ch.buf, half, :], b_row[:, n % 2, :], ALU.mult)\
                        .then_inc(S["driven"], 1)
                    run(steps, rnd, s)
                for n in range(NHF):
                    pool.wait_ge(S["y_done"], ch.unit(NHF, NHF + n + 1))
                    pool.tensor_tensor(y[:, n, :], y[:, n, :], gate[:, ch.buf, n, :], ALU.mult).then_inc(S["gated"], 1)
                pool.wait_ge(S["out_copied"], ch.unit(1, 2))
                x = X[:, ch.tokens()]
                pool.tensor_tensor(x, x, out_sb[:, :], ALU.add).then_inc(S["added"], 1)
            chunks(pool, first, body)

        @block.vector
        def _(dve):
            dve.sem_inc(S["scanned"], 4)
            dve.sem_inc(S["weighed"], 4)
            dve.sem_inc(S["y_done"], NHF)
            dve.sem_inc(S["relued"], 2)
            dve.sem_inc(S["convolved"], 8)

            def taps(t):
                def step(rnd):
                    for n in range(NHF):
                        src = xin[:, n, t:t + CH]
                        if t == 0:
                            dve.wait_ge(S["xin_copied"], rnd.round(2, n + 1))
                            ins = dve.tensor_scalar(conv[:, n, :], src, cols[:, n, 0:1], None, ALU.mult)
                        else:
                            dve.wait_ge(S["convolved"], rnd.round(8, 8 + 2 * (t - 1) + n + 1))
                            ins = dve.scalar_tensor_tensor(conv[:, n, :], src, cols[:, n, t:t + 1], conv[:, n, :], ALU.mult, ALU.add)
                        ins.then_inc(S["convolved"], 1)
                return step

            def low_rows(rnd):
                dve.wait_ge(S["rows_copied"], rnd.round(2, 2))
                dve.tensor_tensor(dbl[LOW:LOW + NROW, rnd.buf, :], g_ps[0:NROW, 0, :], dbl[0:NROW, rnd.buf, :].bitcast(F32),
                                  ALU.subtract).then_inc(S["rows_low"], 1)

            def relu_dt(rnd):
                for n in (1, 0):
                    dve.wait_ge(S["mag_done"], rnd.round(2, 2 - n))
                    dve.tensor_scalar(relu[:, n, :], g_ps[:, n, :], cols[:, n, 5:6], 0.0, ALU.add, ALU.max).then_inc(S["relued"], 1)

            def make_delta(rnd):
                dve.wait_ge(S["relued"], rnd.round(2, 4))
                dve.wait_ge(S["ln_done"], rnd.round(1, 1))
                dve.wait_ge(S["err_done"], rnd.round(2, 2))
                for n in range(NHF):
                    dve.tensor_tensor(relu[:, n, :], relu[:, n, :], err[:, n, :], ALU.add).then_inc(S["delta_done"], 1)
                for n in range(NHF):
                    dve.wait_ge(S["delta_done"], rnd.round(4, n + 1))
                    dve.tensor_tensor(delta[:, rnd.buf, n, :], relu[:, n, :], ln1[:, n, :], ALU.add).then_inc(S["delta_done"], 1)

            steps = [(6, taps(0)), (8, taps(1)), (10, taps(2)), (12, taps(3)), (17, low_rows), (19, relu_dt), (23, make_delta)]

            def first(rnd):
                dve.memset(state[:, :], 0.0).then_inc(S["reset"], 1)
                dve.wait_ge(S["reset"], rnd.b * 1 + 1)
                run(steps, rnd)

            def body(ch, rnd):
                def scan(s):
                    dve.wait_ge(S["decayed"], ch.unit(UNITS, s + 1))
                    dve.wait_ge(S["driven"], ch.unit(UNITS, s + 1 + 4))
                    dve.tensor_tensor_scan(h[:, s % H_RING, :], decay[:, s % A_RING, :], drive[:, s % U_RING, :],
                                           state[:, s:s + 1], ALU.mult, ALU.add).then_inc(S["scanned"], 1)

                def weigh(s):
                    n = s // 2
                    dve.wait_ge(S["scanned"], ch.unit(UNITS, s + 1 + 4))
                    dve.tensor_copy(state[:, s:s + 1], h[:, s % H_RING, CH - 1:CH]).then_inc(S["kept"], 1)
                    dve.wait_ge(S["c_ready"], ch.unit(NST, n + 1))
                    dve.wait_ge(S["summed"], ch.unit(UNITS, s - 3)) if s >= HC_RING else None
                    dve.tensor_tensor(hc[:, s % HC_RING, :], h[:, s % H_RING, :], c_ps[:, n % 2, :], ALU.mult)\
                       .then_inc(S["weighed"], 1)

                for s in range(UNITS + 1):
                    if s < UNITS:
                        if s >= H_RING:
                            dve.wait_ge(S["weighed"], ch.unit(UNITS, s - H_RING + 1 + 4))
                        scan(s)
                    if s:
                        weigh(s - 1)
                    if s < UNITS:
                        run(steps, rnd, s)
                for n in range(NHF):
                    dve.wait_ge(S["summed"], ch.unit(UNITS, UNITS - 1 + n))
                    dve.scalar_tensor_tensor(y[:, n, :], xc[:, ch.buf, n, :], cols[:, n, 6:7], y_ps[:, n, :], ALU.mult, ALU.add)\
                       .then_inc(S["y_done"], 1)
            chunks(dve, first, body)


STAGES = {
    "L0": neighbourhood_l0,
    "L1": mamba_l1,
    "L2a": attention_l2,
    "L2f": experts_l2,
    "L3a": attention_l3,
    "L3f": filters_l3,
}


def build(nc, dram, out, stages=tuple(STAGES)):
    nc.disable_value_cache = True
    with ExitStack() as ctx:
        m = Memory(nc, ctx)
        k = load_constants(nc, m, dram)
        X = m.sb("X", [P, TOK])
        with ExitStack() as c:
            loaded = Memory(nc, c).sem("x_loaded")
            block = c.enter_context(nc.Block())

            @block.sync
            def _(sp):
                for b in range(BATCH):
                    sp.dma_start(X[:, b * T:(b + 1) * T], dram["x"][b]).then_inc(loaded, 16)
                sp.wait_ge(loaded, 16 * BATCH)

        for s in stages:
            STAGES[s](nc, k, dram, X)
        with ExitStack() as c:
            stored = Memory(nc, c).sem("x_stored")
            block = c.enter_context(nc.Block())

            @block.sync
            def _(sp):
                for b in range(BATCH):
                    sp.dma_start(out[b], X[:, b * T:(b + 1) * T]).then_inc(stored, 16)
                sp.wait_ge(stored, 16 * BATCH)


def lay_out(inputs):
    f = {n: np.asarray(a) for n, a in inputs.items()}

    def halves(a):
        return a.reshape(NHF, P, -1).transpose(1, 0, 2)

    o = constants()
    o["x"] = f["x"].reshape(BATCH, P, T)
    o["L0_w"] = np.concatenate([f["L0_conv_qkv_w"], f["L0_conv_proj_w"]], 1).transpose(2, 0, 1)
    o["L0_bias"] = np.concatenate([f["L0_conv_qkv_b"], f["L0_conv_proj_b"]], 1).reshape(2, 4, P).transpose(2, 0, 1)
    o["L0_ln"] = np.stack([f["L0_conv_ln_g"], f["L0_conv_ln_b"]], 1)
    o["L0_rpb"] = np.zeros((2, NH0, PR, PC), f["L0_conv_rpb"].dtype)
    o["L0_rpb"][:, :, PAD_R:PAD_R + RPB, PAD_C:PAD_C + RPB] = f["L0_conv_rpb"]
    o["L1_w_in"] = f["L1_conv_in_proj_w"].T
    o["L1_w_x"] = halves(f["L1_conv_x_proj_w"].T)
    o["L1_w_dt"] = f["L1_conv_dt_proj_w"].T
    o["L1_w_out"] = halves(f["L1_conv_out_proj_w"].T)
    o["L1_norm"] = np.stack([f["L1_conv_norm_w"], f["L1_conv_norm_b"]], 1)
    o["L1_cols"] = halves(np.concatenate([f["L1_conv_conv_w"]] + [f[n][:, None] for n in (
        "L1_conv_conv_b", "L1_conv_dt_proj_b", "L1_conv_D")], 1))
    o["L1_a_log"] = halves(f["L1_conv_A_log"])
    for n in ("L2_attn_Wq", "L2_attn_Wk", "L2_attn_Wv", "L2_ffn_router_w", "L2_ffn_expert_w", "L2_ffn_expert_b",
              "L3_attn_w_attn", "L3_attn_w_proj", "L3_ffn_M_u", "L3_ffn_M_phi_plus", "L3_ffn_M_phi_minus"):
        o[n] = f[n]
    for n in ("L2_ffn_router_b", "L3_ffn_sigma", "L3_ffn_log_weights", "L3_ffn_gumbel"):
        o[n] = f[n].reshape(1, -1)
    o["L3_ffn_phi"] = f["L3_ffn_phi"].reshape(HALF, 2, NK).transpose(2, 1, 0).reshape(P, HALF // 4)
    return {n: np.ascontiguousarray(a) for n, a in o.items()}


def kernel(**inputs):
    import concourse.bacc as bacc
    from concourse.bass_utils import run_bass_kernel_spmd

    nc = bacc.Bacc("TRN2", target_bir_lowering=False, num_devices=1)
    arrays = lay_out(inputs)
    dram = {n: nc.dram_tensor(n, a.shape, mybir.dt.from_np(a.dtype), kind="ExternalInput").ap() for n, a in arrays.items()}
    out = nc.dram_tensor("out", [BATCH, P, T], F32, kind="ExternalOutput").ap()
    build(nc, dram, out)
    r = run_bass_kernel_spmd(nc, [arrays], core_ids=[0])
    return r.results[0]["out"].reshape(BATCH, P, HW, HW)
```

```python
from contextlib import ExitStack

import numpy as np

import concourse.bass as bass
from concourse import mybir

F32 = mybir.dt.float32
BF16 = mybir.dt.bfloat16
U32 = mybir.dt.uint32
ALU = mybir.AluOpType
ACT = mybir.ActivationFunctionType
AX = mybir.AxisListType.X

P = 128
BATCH = 2
HW = 64
T = HW * HW
TOK = BATCH * T
CH = 512
NCH = TOK // CH
NEG = -1e30
ds = bass.ds

NH0, D0, KW = 4, 32, 7
TR, TC = 8, 16
WR, WC = 15, 22
KC = 5 * WC

DIN, NST, DTR, NCONV = 256, 16, 8, 4

NH3, D3 = 8, 16
NK = 16


def block_starts(n, tile, span):
    return [min(max(i * tile - KW // 2, 0), n - span) for i in range(n // tile)]


ROW0, COL0 = block_starts(HW, TR, WR), block_starts(HW, TC, WC)


def window_masks():
    i, p = np.arange(HW), np.clip(np.arange(HW) - KW // 2, 0, HW - KW)
    kinds, masks = {}, []
    index = []
    for a in range(HW // TR):
        for b in range(HW // TC):
            qi, qj = a * TR + np.arange(TR), b * TC + np.arange(TC)[::-1]
            ki, kj = ROW0[a] + np.arange(WR), COL0[b] + np.arange(WC)
            ri = (ki[None] >= p[qi][:, None]) & (ki[None] < p[qi][:, None] + KW)
            rj = (kj[None] >= p[qj][:, None]) & (kj[None] < p[qj][:, None] + KW)
            m = np.where(ri[:, None, :, None] & rj[None, :, None, :], 0.0, NEG).reshape(P, WR * WC)
            key = m.tobytes()
            if key not in kinds:
                kinds[key] = len(masks)
                masks.append(m)
            index.append(kinds[key])
    return np.stack(masks, 1).astype(np.float32), index


OFF_R = max(i * TR - r for i, r in enumerate(ROW0))
OFF_C = max(i * TC - r for i, r in enumerate(COL0))
BR, BC = WR + OFF_R, WC + OFF_C
RPB = 2 * KW - 1
PAD_R, PAD_C = TR - 1 + OFF_R - (KW - 1), TC - 1 + OFF_C - (KW - 1)
PR, PC = PAD_R + BR - OFF_R + KW - 1, PAD_C + BC - OFF_C + KW - 1
MASKS, MASK_OF = window_masks()
NMASK = MASKS.shape[1]


def constants():
    r = np.arange(P)
    one_hot = np.zeros((DTR + 2 * NST, 2 * NST, P), np.float32)
    for n in range(2 * NST):
        one_hot[DTR + n, n, :] = 1.0
    return {
        "c_ident": np.eye(P, dtype=np.float32),
        "c_mean": np.full((P, P), 1.0 / P, np.float32),
        "c_group": np.where(r[:, None] // 4 == r[None] // 4, 0.25, 0.0).astype(np.float32),
        "c_causal": np.where(r[None] > r[:, None], NEG, 0.0).astype(np.float32),
        "c_window": MASKS,
        "c_pick": one_hot,
        "c_iota": np.tile(np.arange(8, dtype=np.float32), (P, 1)),
        "c_regime": np.stack([np.arange(4) == 3 - i for i in range(4)]).astype(np.float32),
    }


class Memory:

    def __init__(self, nc, ctx):
        self.nc, self.ctx, self.sems = nc, ctx, []
        ctx.callback(self.clear)

    def clear(self):
        if self.sems:
            with self.nc.Block() as block:
                @block.sync
                def _(sp):
                    for s in self.sems:
                        sp.sem_clear(s)

    def sb(self, name, shape, dt=F32):
        return self.ctx.enter_context(self.nc.sbuf_tensor(name, shape, dt))

    def ps(self, name, shape, dt=F32):
        return self.ctx.enter_context(self.nc.psum_tensor(name, shape, dt))

    def sem(self, name):
        self.sems.append(self.ctx.enter_context(self.nc.semaphore(name)))
        return self.sems[-1]


def wait_apart(eng, sem, value):
    with eng.register() as target:
        eng.reg_mov(target, value)
        eng.wait_ge(sem, 1)
        eng.wait_ge(sem, target)


def load_constants(nc, m, dram):
    k = {}
    k["ident"] = m.sb("ident", [P, P])
    k["mean"] = m.sb("mean_w", [P, P])
    k["group"] = m.sb("group_w", [P, P])
    k["ident16"] = m.sb("ident16", [P, P], BF16)
    k["causal"] = m.sb("causal", [P, P])
    k["causal16"] = m.sb("causal16", [P, P], BF16)
    k["causalT16"] = m.sb("causalT16", [P, P], BF16)
    k["eps5"] = m.sb("eps5", [P, 1])
    k["eps6"] = m.sb("eps6", [P, 1])
    with ExitStack() as c:
        mm = Memory(nc, c)
        loaded, turned, made = mm.sem("const_loaded"), mm.sem("const_turned"), mm.sem("const_made")
        tp = mm.ps("const_tp", [P, P])
        block = c.enter_context(nc.Block())

        @block.sync
        def _(sp):
            for name in ("ident", "mean", "group", "causal"):
                sp.dma_start(k[name][:, :], dram[f"c_{name}"]).then_inc(loaded, 16)

        @block.tensor
        def _(pe):
            pe.wait_ge(loaded, 64)
            pe.transpose(tp[:, :], k["causal"][:, :], k["ident"][:, :]).then_inc(turned, 1)

        @block.vector
        def _(dve):
            dve.memset(k["eps5"][:, :], 1e-5)
            dve.memset(k["eps6"][:, :], 1e-6)
            dve.wait_ge(loaded, 64)
            dve.tensor_copy(k["ident16"][:, :], k["ident"][:, :])
            dve.tensor_copy(k["causal16"][:, :], k["causal"][:, :])
            dve.wait_ge(turned, 1)
            dve.tensor_copy(k["causalT16"][:, :], tp[:, :]).then_inc(made, 1)
    return k


LN_UNIT = 4


def layer_norm(nc, k, tag, src, dst, eps, gain=None, shift=None, add_to=None):
    N = LN_UNIT
    with ExitStack() as c:
        m = Memory(nc, c)
        mean_ps, var_ps = m.ps(f"{tag}_mean", [P, 2, CH]), m.ps(f"{tag}_var", [P, N, CH])
        square, rstd = m.sb(f"{tag}_square", [P, 2, CH]), m.sb(f"{tag}_rstd", [P, N, CH])
        mean_ready, centered, square_ready, var_ready, logged, rstd_ready, scaled, normed, added = (
            m.sem(f"{tag}_{n}") for n in ("mean_ready", "centered", "square_ready", "var_ready", "logged", "rstd_ready",
                                          "scaled", "normed", "added"))
        block = c.enter_context(nc.Block())

        def at(i, u):
            return ds(i * N * CH + u * CH, CH)

        @block.tensor
        def _(pe):
            pe.sem_inc(var_ready, 2)
            with pe.Fori(0, NCH // N) as i:
                for u in range(N):
                    pe.wait_ge(centered, i * N + u + 1)
                    pe.matmul(mean_ps[:, u % 2, :], k["mean"][:, :], src[:, at(i, u)], start=True, stop=True).then_inc(mean_ready, 1)
            with pe.Fori(0, NCH // N) as i:
                for u in range(N):
                    pe.wait_ge(square_ready, i * N + u + 1)
                    pe.wait_ge(logged, i * N + u + 1)
                    pe.matmul(var_ps[:, u, :], k["mean"][:, :], square[:, u % 2, :], start=True, stop=True).then_inc(var_ready, 1)

        @block.gpsimd
        def _(pool):
            with pool.Fori(0, NCH // N) as i:
                for u in range(N):
                    pool.wait_ge(centered, i * N + u + 3)
                    pool.wait_ge(var_ready, i * N + u + 1)
                    pool.tensor_tensor(square[:, u % 2, :], dst[:, at(i, u)], dst[:, at(i, u)], ALU.mult).then_inc(square_ready, 1)

        @block.scalar
        def _(act):
            act.sem_inc(logged, N)
            with act.Fori(0, NCH // N) as i:
                for u in range(N):
                    act.wait_ge(var_ready, i * N + u + 3)
                    act.wait_ge(normed, i * N + u + 1)
                    act.activation(rstd[:, u, :], var_ps[:, u, :], ACT.Ln, bias=k[eps][:, :]).then_inc(logged, 1)
                for u in range(N):
                    act.wait_ge(logged, i * N + u + 1 + N)
                    act.activation(rstd[:, u, :], rstd[:, u, :], ACT.Exp, scale=-0.5).then_inc(rstd_ready, 1)

        @block.vector
        def _(dve):
            dve.sem_inc(centered, 2)
            dve.sem_inc(normed, N)
            with dve.Fori(0, NCH // N) as i:
                for u in range(N):
                    dve.wait_ge(mean_ready, i * N + u + 1)
                    dve.tensor_tensor(dst[:, at(i, u)], src[:, at(i, u)], mean_ps[:, u % 2, :], ALU.subtract).then_inc(centered, 1)
            with dve.Fori(0, NCH // N) as i:
                for u in range(N):
                    dve.wait_ge(rstd_ready, i * N + u + 1)
                    dve.wait_ge(square_ready, i * N + u + 1)
                    dve.tensor_tensor(dst[:, at(i, u)], dst[:, at(i, u)], rstd[:, u, :], ALU.mult).then_inc(normed, 1)
                    if gain is not None:
                        dve.wait_ge(normed, i * N + u + 1 + N)
                        dve.tensor_scalar(dst[:, at(i, u)], dst[:, at(i, u)], gain, shift, ALU.mult, ALU.add).then_inc(scaled, 1)
                    if add_to is not None:
                        dve.wait_ge(scaled, i * N + u + 1)
                        dve.tensor_tensor(add_to[:, at(i, u)], add_to[:, at(i, u)], dst[:, at(i, u)], ALU.add).then_inc(added, 1)


def group_norm(nc, k, tag, src, dst):
    with ExitStack() as c:
        m = Memory(nc, c)
        stats = m.sb(f"{tag}_stats", [P, NCH, 6])
        mv = m.sb(f"{tag}_mv", [P, BATCH, 2])
        mean = m.sb(f"{tag}_mean", [P, BATCH])
        part = m.sb(f"{tag}_part", [P, BATCH])
        std = m.sb(f"{tag}_std", [P, BATCH])
        rstd = m.sb(f"{tag}_rstd", [P, BATCH])
        g_ps, v_ps = m.ps(f"{tag}_g", [P, BATCH]), m.ps(f"{tag}_v", [P, BATCH])
        stat, meaned, step, varied, rooted, done = (m.sem(f"{tag}_s{n}") for n in range(6))
        block = c.enter_context(nc.Block())

        @block.vector
        def _(dve):
            for n in range(NCH):
                dve.bn_stats(stats[:, n, :], src[:, n * CH:(n + 1) * CH]).then_inc(stat, 1)
            dve.wait_ge(stat, NCH)
            for b in range(BATCH):
                dve.bn_aggr(mv[:, b, :], stats[:, b * NCH // 2:(b + 1) * NCH // 2, :]).then_inc(stat, 1)
            dve.wait_ge(meaned, 1)
            dve.tensor_copy(mean[:, :], g_ps[:, :]).then_inc(step, 1)
            dve.wait_ge(step, 1)
            dve.tensor_tensor(part[:, :], mv[:, :, 0], mean[:, :], ALU.subtract).then_inc(step, 1)
            dve.wait_ge(step, 2)
            dve.tensor_tensor(part[:, :], part[:, :], part[:, :], ALU.mult).then_inc(step, 1)
            dve.wait_ge(step, 3)
            dve.tensor_tensor(part[:, :], part[:, :], mv[:, :, 1], ALU.add).then_inc(step, 1)
            dve.wait_ge(rooted, 1)
            dve.reciprocal(rstd[:, :], std[:, :]).then_inc(step, 1)
            dve.wait_ge(step, 5)
            for n in range(NCH):
                b = n // (NCH // 2)
                dve.tensor_scalar(dst[:, n * CH:(n + 1) * CH], src[:, n * CH:(n + 1) * CH], mean[:, b:b + 1],
                                  rstd[:, b:b + 1], ALU.subtract, ALU.mult).then_inc(done, 1)

        @block.tensor
        def _(pe):
            pe.wait_ge(stat, NCH + BATCH)
            pe.matmul(g_ps[:, :], k["group"][:, :], mv[:, :, 0], start=True, stop=True).then_inc(meaned, 1)
            pe.wait_ge(step, 4)
            pe.matmul(v_ps[:, :], k["group"][:, :], part[:, :], start=True, stop=True).then_inc(varied, 1)

        @block.scalar
        def _(act):
            act.wait_ge(varied, 1)
            act.activation(std[:, :], v_ps[:, :], ACT.Sqrt, bias=k["eps5"][:, :]).then_inc(rooted, 1)


QT = T // P
SB = 4
NSB = QT // SB
NBLK = SB * NSB * (NSB + 1) // 2
MAX_RING, EXP_RING, W_RING = 3, 2, 4


def causal_attention(nc, k, tag, heads, dv, scale, buffers, score_max, score_exp, feed, loads, out_of, keep=None):
    B = len(buffers)
    banks = 1 if keep else (SB * (dv + 1) + CH - 1) // CH
    with ExitStack() as c:
        m = Memory(nc, c)
        max_ps = m.ps(f"{tag}_max_ps", [P, MAX_RING, CH])
        exp_ps = m.ps(f"{tag}_exp_ps", [P, EXP_RING, CH])
        out_ps = m.ps(f"{tag}_out_ps", [P, 2, CH])
        turn_ps = m.ps(f"{tag}_turn_ps", [P, 2 * CH], BF16)
        weights = m.sb(f"{tag}_weights", [P, W_RING, CH])
        part_max = m.sb(f"{tag}_part_max", [P, SB, NSB])
        minus = m.sb(f"{tag}_minus", [P, SB])
        rest = m.sb(f"{tag}_rest", [P, SB])
        parts = m.sb(f"{tag}_parts", [P, SB, 32], BF16)
        recip = m.sb(f"{tag}_recip", [P, SB])
        loaded = [m.sem(f"{tag}_loaded{u}") for u in range(B)]
        max_ready = m.sem(f"{tag}_max_ready")
        reduced = m.sem(f"{tag}_reduced")
        step = m.sem(f"{tag}_step")
        split = m.sem(f"{tag}_split")
        turned = m.sem(f"{tag}_turned")
        placed = m.sem(f"{tag}_placed")
        exp_ready = m.sem(f"{tag}_exp_ready")
        weighted = m.sem(f"{tag}_weighted")
        used = m.sem(f"{tag}_used")
        inverted = m.sem(f"{tag}_inverted")
        emitted = m.sem(f"{tag}_emitted")
        stored = [m.sem(f"{tag}_stored{u}") for u in range(B)]
        block = c.enter_context(nc.Block())
        credit = 2 if banks == 1 else 1

        def place_of(s, t):
            return (s % 2, t * (dv + 1)) if banks == 1 else (t // 2, (t % 2) * (dv + 1))

        def for_heads(eng, body):
            if heads == 1:
                body(0, 0, lambda per, j: j, 0)
                return
            with eng.Fori(0, heads // B) as i:
                for u in range(B):
                    body(i * B + u, u, lambda per, j, u=u: i * (B * per) + (u * per + j), i)

        if loads:
            @block.sync
            def _(sp):
                for u in range(B):
                    feed(sp, u, u, loaded[u])

        @block.tensor
        def _(pe):
            def head(it, u, at, i):
                if loads:
                    pe.wait_ge(loaded[u], i * (16 * loads) + 16 * loads)
                seen = {"max": 0, "exp": 0, "out": 0}

                def maxima(s, first, end):
                    for n in range(first, end):
                        t, ck = n // (s + 1), n % (s + 1)
                        g = seen["max"]
                        width = (t + 1) * P if ck == s else CH
                        bank = max_ps[:, g % MAX_RING, :]
                        pe.wait_ge(reduced, at(NBLK, g + 1))
                        mm = score_max(pe, u, bank[:, 0:width], SB * s + t, ck * CH, width)
                        if ck == s:
                            mm = pe.matmul(bank[:, t * P:width], k["ident16"][:, :], k["causal16"][:, :],
                                           start=False, stop=True, skip_group_check=True)
                        mm.then_inc(max_ready, 1)
                        seen["max"] += 1

                def turn(s):
                    pe.wait_ge(split, at(NSB, s + 1))
                    pe.wait_ge(placed, at(NSB, s + 1))
                    for t in range(SB):
                        mm = pe.transpose(turn_ps[96:128, t * P:(t + 1) * P], parts[:, t, :], k["ident16"][:, :])
                    mm.then_inc(turned, 1)

                def score(s, j):
                    g = seen["exp"]
                    q0 = max(0, j - SB * s) * P
                    bank = exp_ps[:, g % EXP_RING, :]
                    pe.wait_ge(weighted, at(NBLK, g + 1))
                    mm = score_exp(pe, u, bank[:, q0:CH], j, s * CH + q0, CH - q0)
                    if j >= SB * s:
                        mm = pe.matmul(bank[:, q0:q0 + P], k["ident16"][:, :], k["causalT16"][:, :],
                                       start=False, stop=True, skip_group_check=True)
                    mm.then_inc(exp_ready, 1)
                    seen["exp"] += 1

                def weigh(s, j):
                    g = seen["out"]
                    if j == 0:
                        pe.wait_ge(emitted, at(NSB, s + 1))
                    pe.wait_ge(weighted, at(NBLK, g + 1 + EXP_RING))
                    if keep:
                        q0 = max(0, j - SB * s) * P
                        mm = pe.matmul(out_ps[0:dv + 1, s % 2, q0:CH], buffers[u]["v"][:, j, :], weights[:, g % W_RING, q0:CH],
                                       start=(j == 0), stop=(j == SB * s + SB - 1), skip_group_check=True)
                    for t in () if keep else range(max(0, j - SB * s), SB):
                        bank, col = place_of(s, t)
                        mm = pe.matmul(out_ps[:, bank, col:col + dv + 1], weights[:, g % W_RING, t * P:(t + 1) * P],
                                       buffers[u]["v"][:, j, :], start=(j == 0 and col == 0),
                                       stop=(j == SB * s + t), skip_group_check=True)
                    mm.then_inc(used, 1)
                    seen["out"] += 1

                maxima(0, 0, SB)
                turn(0)
                for s in range(NSB):
                    pe.wait_ge(placed, at(NSB, s + 2))
                    blocks, chunks = SB * (s + 1), SB * (s + 2) if s + 1 < NSB else 0
                    steps = blocks - 2
                    for j in range(blocks + 2):
                        if j < blocks:
                            score(s, j)
                        if chunks and j < steps:
                            maxima(s + 1, chunks * j // steps, chunks * (j + 1) // steps)
                        if chunks and j == blocks:
                            turn(s + 1)
                        if j >= 2:
                            weigh(s, j - 2)
            for_heads(pe, head)

        @block.scalar
        def _(act):
            act.sem_inc(weighted, EXP_RING)
            if keep:
                act.sem_inc(emitted, credit)
                for u in range(B):
                    act.sem_inc(stored[u], 32)

            def head(it, u, at, i):
                g = 0

                def copy_out(s):
                    act.wait_ge(used, at(NBLK, SB * (s + 1) * (s + 2) // 2 + W_RING))
                    if s == 0:
                        act.wait_ge(stored[u], i * 32 + 32)
                    act.activation(buffers[u]["out"][:, s * CH:(s + 1) * CH], out_ps[0:dv + 1, s % 2, :], ACT.Copy)\
                       .then_inc(emitted, 1)

                for s in range(NSB):
                    if keep and s:
                        copy_out(s - 1)
                    for j in range(SB * (s + 1)):
                        q0 = max(0, j - SB * s) * P
                        act.wait_ge(exp_ready, at(NBLK, g + 1))
                        act.wait_ge(used, at(NBLK, g + 1))
                        act.activation(weights[:, g % W_RING, q0:CH], exp_ps[:, g % EXP_RING, q0:CH], ACT.Exp,
                                       scale=scale).then_inc(weighted, 1)
                        g += 1
                if keep:
                    copy_out(NSB - 1)
            for_heads(act, head)

        @block.vector
        def _(dve):
            dve.memset(parts[:, :, :], 0.0).then_inc(step, 1)
            dve.wait_ge(step, 1)
            dve.sem_inc(reduced, MAX_RING)
            dve.sem_inc(placed, 1)
            dve.sem_inc(used, W_RING)
            if not keep:
                dve.sem_inc(emitted, credit)

            def head(it, u, at, i):
                seen = {"max": 0, "step": 1}

                def small(ins):
                    ins.then_inc(step, 1)
                    seen["step"] += 1
                    dve.wait_ge(step, at(5 * NSB, seen["step"]))

                def maxima(s):
                    for t in range(SB):
                        for ck in range(s + 1):
                            g = seen["max"]
                            width = (t + 1) * P if ck == s else CH
                            dve.wait_ge(max_ready, at(NBLK, g + 1))
                            dve.tensor_reduce(part_max[:, t, ck:ck + 1], max_ps[:, g % MAX_RING, 0:width], AX,
                                              ALU.max).then_inc(reduced, 1)
                            seen["max"] += 1

                def split_max(s):
                    dve.wait_ge(reduced, at(NBLK, seen["max"] + MAX_RING))
                    small(dve.tensor_reduce(minus[:, :], part_max[:, :, 0:s + 1], AX, ALU.max, negate=True))
                    small(dve.tensor_copy(parts[:, :, 0], minus[:, :]))
                    small(dve.tensor_tensor(rest[:, :], minus[:, :], parts[:, :, 0], ALU.subtract))
                    small(dve.tensor_copy(parts[:, :, 1], rest[:, :]))
                    small(dve.tensor_tensor(rest[:, :], rest[:, :], parts[:, :, 1], ALU.subtract))
                    dve.tensor_copy(parts[:, :, 2], rest[:, :]).then_inc(split, 1)

                def put(s):
                    dve.wait_ge(turned, at(NSB, s + 1))
                    dve.tensor_copy(buffers[u]["minus_max"][96:99, s * CH:(s + 1) * CH], turn_ps[96:99, 0:CH])\
                       .then_inc(placed, 1)

                def emit(s):
                    dve.wait_ge(used, at(NBLK, SB * (s + 1) * (s + 2) // 2 + W_RING))
                    dve.wait_ge(emitted, at(NSB, s + credit))
                    n = SB // banks
                    for b in range(banks):
                        o = out_ps[:, s % 2 if banks == 1 else b, 0:n * (dv + 1)].rearrange("p (t e) -> p t e", t=n)
                        ins = dve.reciprocal(recip[:, b * n:(b + 1) * n], o[:, :, dv])
                    ins.then_inc(inverted, 1)
                    dve.wait_ge(inverted, at(NSB, s + 1))
                    for b in range(banks):
                        o = out_ps[:, s % 2 if banks == 1 else b, 0:n * (dv + 1)].rearrange("p (t e) -> p t e", t=n)
                        ins = dve.tensor_tensor(out_of(it)[:, SB * s + b * n:SB * s + (b + 1) * n, :], o[:, :, 0:dv],
                                                recip[:, b * n:(b + 1) * n].unsqueeze(2).to_broadcast([P, n, dv]), ALU.mult)
                    ins.then_inc(emitted, 1)

                for s in range(NSB):
                    maxima(s)
                    split_max(s)
                    put(s)
                    if s and not keep:
                        emit(s - 1)
                if not keep:
                    emit(NSB - 1)
            for_heads(dve, head)


F32R = mybir.dt.float32r
EXACT_RING, PART_RING = 3, 6
LAG = 4
VPART = 32


def attention_heads(nc, k, tag, heads, dv, scale, buffers, rows, feed, loads, keep):
    B = len(buffers)
    OUT_RING = 4
    last_block = [SB * (s + 1) * (s + 2) // 2 for s in range(NSB)]
    with ExitStack() as c:
        m = Memory(nc, c)
        max_ps, exp_ps = m.ps(f"{tag}_max_ps", [P, MAX_RING, CH]), m.ps(f"{tag}_exp_ps", [P, EXP_RING, CH])
        out_ps = m.ps(f"{tag}_out_ps", [P, 2, CH])
        turn_ps = m.ps(f"{tag}_turn_ps", [P, 2 * CH], BF16)
        exact = m.sb(f"{tag}_exact", [P, EXACT_RING, CH])
        high, low = m.sb(f"{tag}_high", [P, PART_RING, CH], F32R), m.sb(f"{tag}_low", [P, PART_RING, CH], F32R)
        v_parts = [m.sb(f"{tag}_v_parts{u}", [P, QT, 2, VPART], F32R) for u in range(B)]
        out = m.sb(f"{tag}_out", [2 * VPART, OUT_RING, CH])
        part_max = m.sb(f"{tag}_part_max", [P, SB, NSB])
        minus, rest = m.sb(f"{tag}_minus", [P, SB]), m.sb(f"{tag}_rest", [P, SB])
        parts = m.sb(f"{tag}_parts", [P, SB, 32], BF16)
        loaded = [m.sem(f"{tag}_loaded{u}") for u in range(B)]
        stored = [m.sem(f"{tag}_stored{n}") for n in range(OUT_RING)]
        max_ready = m.sem(f"{tag}_max_ready")
        reduced = m.sem(f"{tag}_reduced")
        step = m.sem(f"{tag}_step")
        split = m.sem(f"{tag}_split")
        turned = m.sem(f"{tag}_turned")
        placed = m.sem(f"{tag}_placed")
        exp_ready = m.sem(f"{tag}_exp_ready")
        weighted = m.sem(f"{tag}_weighted")
        low_dve, low_pool = m.sem(f"{tag}_low_dve"), m.sem(f"{tag}_low_pool")
        rounded = m.sem(f"{tag}_rounded")
        cleared = m.sem(f"{tag}_cleared")
        v_split = m.sem(f"{tag}_v_split")
        used = m.sem(f"{tag}_used")
        emitted = m.sem(f"{tag}_emitted")
        block = c.enter_context(nc.Block())

        def head_at(i, u):
            return lambda per, j: i * (B * per) + (u * per + j)

        def for_heads(eng, body):
            with eng.Fori(0, heads // B) as i:
                for u in range(B):
                    body(u, head_at(i, u))

        def low_done(g, at):
            return (low_dve, at(NBLK // 3, g // 3 + 2)) if g % 3 == 0 else (low_pool, at(NBLK // 3 * 2, g // 3 * 2 + g % 3 + 2))

        def place_free(g, at):
            return (low_dve, at(NBLK // 3, g // 3 + 1)) if g % 3 == 0 else (low_pool, at(NBLK // 3 * 2, g // 3 * 2 + g % 3))

        by_dve = [g for g in range(0, NBLK, 3) if g >= last_block[NSB - 2]]

        def low_part(eng, g, q0, at):
            eng.wait_ge(weighted, at(NBLK, g + 1 + EXP_RING))
            if g in by_dve:
                eng.tensor_copy(high[:, g % PART_RING, q0:CH], exact[:, g % EXACT_RING, q0:CH]).then_inc(rounded, 1)
                eng.wait_ge(rounded, at(len(by_dve), by_dve.index(g) + 1))
            eng.tensor_tensor(low[:, g % PART_RING, q0:CH], exact[:, g % EXACT_RING, q0:CH],
                              high[:, g % PART_RING, q0:CH].bitcast(F32), ALU.subtract)\
               .then_inc(low_dve if g % 3 == 0 else low_pool, 1)

        def blocks_of_head():
            return [(last_block[s] - SB * (s + 1) + j, s, j, max(0, j - SB * s) * P) for s in range(NSB) for j in range(SB * (s + 1))]

        def chunks_at(s, j):
            steps, chunks = SB * (s + 1) - 3, SB * (s + 2)
            return range(chunks * j // steps, chunks * (j + 1) // steps) if s + 1 < NSB and j < steps else range(0)

        @block.sync
        def _(sp):
            def store(it, u, at):
                for s in range(NSB):
                    sp.wait_ge(emitted, at(NSB, s + 1 + 2))
                    keep(sp, it, s, out[:, s % OUT_RING, :], stored[s % OUT_RING])

            for u in range(B):
                feed(sp, u, u, loaded[u])
            with sp.Fori(0, heads // B - 1) as i:
                for u in range(B):
                    store(i * B + u, u, head_at(i, u))
                    sp.wait_ge(used, i * (B * NBLK) + ((u + 1) * NBLK + PART_RING))
                    feed(sp, u, i * B + (B + u), loaded[u])
            for u in range(B):
                store(heads - B + u, u, head_at(heads // B - 1, u))
            for n in range(OUT_RING):
                sp.wait_ge(stored[n], 48 * (heads * NSB // OUT_RING + 1))

        @block.tensor
        def _(pe):
            def head(u, at):
                pe.wait_ge(loaded[u], at(8 * loads, (2 - u) * 8 * loads))
                q, kk = buffers[u]["q"], buffers[u]["k"]
                seen = {"max": 0}

                def maxima(s, chunks):
                    for n in chunks:
                        t, ck = n // (s + 1), n % (s + 1)
                        g, k0 = seen["max"], ck * CH
                        width = (t + 1) * P if ck == s else CH
                        bank = max_ps[:, g % MAX_RING, :]
                        pe.wait_ge(reduced, at(NBLK, g + 1))
                        mm = pe.matmul(bank[:, 0:width], q[0:rows, (SB * s + t) * P:(SB * s + t + 1) * P],
                                       kk[0:rows, k0:k0 + width], start=True, stop=True)
                        if ck == s:
                            mm = pe.matmul(bank[:, t * P:width], k["ident16"][:, :], k["causal16"][:, :],
                                           start=False, stop=True, skip_group_check=True)
                        mm.then_inc(max_ready, 1)
                        seen["max"] += 1

                def turn(s):
                    pe.wait_ge(split, at(NSB, s + 1))
                    pe.wait_ge(placed, at(NSB, s + 1))
                    for t in range(SB):
                        mm = pe.transpose(turn_ps[96:128, t * P:(t + 1) * P], parts[:, t, :], k["ident16"][:, :])
                    mm.then_inc(turned, 1)

                def score(g, s, j, q0):
                    bank = exp_ps[:, g % EXP_RING, :]
                    if j == 0:
                        pe.wait_ge(placed, at(NSB, s + 2))
                    pe.wait_ge(weighted, at(NBLK, g + 1))
                    mm = pe.matmul(bank[:, q0:CH], kk[0:rows + 3, j * P:(j + 1) * P], q[0:rows + 3, s * CH + q0:(s + 1) * CH],
                                   start=True, stop=True)
                    if j >= SB * s:
                        mm = pe.matmul(bank[:, q0:q0 + P], k["ident16"][:, :], k["causalT16"][:, :],
                                       start=False, stop=True, skip_group_check=True)
                    mm.then_inc(exp_ready, 1)

                def weigh(g, s, j, q0):
                    if j == 0:
                        pe.wait_ge(emitted, at(NSB, s + 1))
                    if g == 0:
                        pe.wait_ge(v_split, at(1, 1))
                    pe.wait_ge(*low_done(g, at))
                    for n, part in enumerate((high, low)):
                        mm = pe.matmul(out_ps[0:2 * VPART, s % 2, q0:CH], v_parts[u][:, j, :, :], part[:, g % PART_RING, q0:CH],
                                       start=(j == 0 and n == 0), stop=(n == 1 and j == SB * s + SB - 1), skip_group_check=True)
                    mm.then_inc(used, 1)

                maxima(0, range(SB))
                turn(0)
                work = blocks_of_head()
                for g in range(NBLK + LAG):
                    if g < NBLK:
                        _, s, j, q0 = work[g]
                        score(g, s, j, q0)
                        maxima(s + 1, chunks_at(s, j))
                        if j == SB * (s + 1) - 1 and s + 1 < NSB:
                            turn(s + 1)
                    if g >= LAG:
                        weigh(*work[g - LAG])
            for_heads(pe, head)

        @block.scalar
        def _(act):
            act.sem_inc(weighted, EXP_RING)
            act.sem_inc(emitted, 2)
            for n in range(OUT_RING):
                act.sem_inc(stored[n], 48)

            def head(u, at):
                def copy_out(s):
                    act.wait_ge(used, at(NBLK, last_block[s] + PART_RING))
                    act.wait_ge(stored[s % OUT_RING], at(48 * NSB // OUT_RING, 48 * (s // OUT_RING + 1)))
                    act.activation(out[:, s % OUT_RING, :], out_ps[0:2 * VPART, s % 2, :], ACT.Copy).then_inc(emitted, 1)

                for g, s, j, q0 in blocks_of_head():
                    if s and j == LAG:
                        copy_out(s - 1)
                    act.wait_ge(exp_ready, at(NBLK, g + 1))
                    act.wait_ge(*place_free(g, at))
                    act.wait_ge(used, at(NBLK, g + 1))
                    scores = exp_ps[:, g % EXP_RING, q0:CH]
                    ins = act.activation(exact[:, g % EXACT_RING, q0:CH], scores, ACT.Exp, scale=scale)
                    if g in by_dve:
                        ins.then_inc(weighted, 1)
                        continue
                    act.activation(high[:, g % PART_RING, q0:CH], scores, ACT.Exp, scale=scale).then_inc(weighted, 1)
                copy_out(NSB - 1)
            for_heads(act, head)

        @block.gpsimd
        def _(pool):
            pool.memset(exact[:, 1, :], 0.0).then_inc(cleared, 1)
            pool.wait_ge(cleared, 1)
            for u in range(B):
                for n in range(QT * 2 * VPART // CH):
                    pool.tensor_copy(v_parts[u][:, :, :, :].rearrange("p t n e -> p (t n e)")[:, n * CH:(n + 1) * CH], exact[:, 1, :])\
                        .then_inc(cleared, 1)
            pool.wait_ge(cleared, 1 + B * QT * 2 * VPART // CH)
            pool.sem_inc(low_pool, 2)

            def head(u, at):
                wait_apart(pool, loaded[u], at(8 * loads, (2 - u) * 8 * loads))
                v, vh, vl = buffers[u]["v"], v_parts[u][:, :, 0, 0:dv + 1], v_parts[u][:, :, 1, 0:dv + 1]
                pool.tensor_copy(vh, v[:, :, :]).then_inc(cleared, 1)
                wait_apart(pool, cleared, at(1, 2 + B * QT * 2 * VPART // CH))
                pool.tensor_tensor(vl, v[:, :, :], vh.bitcast(F32), ALU.subtract).then_inc(v_split, 1)
                for g, s, j, q0 in blocks_of_head():
                    if g % 3:
                        low_part(pool, g, q0, at)
            for_heads(pool, head)

        @block.vector
        def _(dve):
            dve.memset(parts[:, :, :], 0.0).then_inc(step, 1)
            dve.wait_ge(step, 1)
            dve.sem_inc(reduced, MAX_RING)
            dve.sem_inc(placed, 1)
            dve.sem_inc(used, PART_RING)
            dve.sem_inc(low_dve, 1)

            def head(u, at):
                seen = {"max": 0, "step": 1}

                def small(ins):
                    ins.then_inc(step, 1)
                    seen["step"] += 1
                    dve.wait_ge(step, at(5 * NSB, seen["step"]))

                def maxima(s, chunks):
                    for n in chunks:
                        t, ck = n // (s + 1), n % (s + 1)
                        g = seen["max"]
                        width = (t + 1) * P if ck == s else CH
                        dve.wait_ge(max_ready, at(NBLK, g + 1))
                        dve.tensor_reduce(part_max[:, t, ck:ck + 1], max_ps[:, g % MAX_RING, 0:width], AX, ALU.max)\
                           .then_inc(reduced, 1)
                        seen["max"] += 1

                def split_max(s):
                    dve.wait_ge(reduced, at(NBLK, seen["max"] + MAX_RING))
                    small(dve.tensor_reduce(minus[:, :], part_max[:, :, 0:s + 1], AX, ALU.max, negate=True))
                    small(dve.tensor_copy(parts[:, :, 0], minus[:, :]))
                    small(dve.tensor_tensor(rest[:, :], minus[:, :], parts[:, :, 0], ALU.subtract))
                    small(dve.tensor_copy(parts[:, :, 1], rest[:, :]))
                    small(dve.tensor_tensor(rest[:, :], rest[:, :], parts[:, :, 1], ALU.subtract))
                    dve.tensor_copy(parts[:, :, 2], rest[:, :]).then_inc(split, 1)

                def put(s):
                    dve.wait_ge(turned, at(NSB, s + 1))
                    dve.tensor_copy(buffers[u]["q"][96:99, s * CH:(s + 1) * CH], turn_ps[96:99, 0:CH]).then_inc(placed, 1)

                maxima(0, range(SB))
                split_max(0)
                put(0)
                work = blocks_of_head()
                for g in range(NBLK + 1):
                    if g < NBLK:
                        _, s, j, q0 = work[g]
                        maxima(s + 1, chunks_at(s, j))
                        if s + 1 < NSB and j == SB * (s + 1) - 4:
                            split_max(s + 1)
                    if g and (g - 1) % 3 == 0:
                        low_part(dve, g - 1, work[g - 1][3], at)
                    if g < NBLK and s + 1 < NSB and j == SB * (s + 1) - 1:
                        put(s + 1)
            for_heads(dve, head)


def add_attention(nc, k, tag, image, X, ctx_out, w_out):
    with ExitStack() as c:
        m = Memory(nc, c)
        turn_ps, mix_ps = m.ps(f"{tag}_turn_ps", [P, 2, CH]), m.ps(f"{tag}_mix_ps", [P, 2, CH])
        flat = m.sb(f"{tag}_flat", [P, 2, CH])
        turned, copied, mixed, added = (m.sem(f"{tag}_{n}") for n in ("turned", "copied", "mixed", "added"))
        block = c.enter_context(nc.Block())

        @block.tensor
        def _(pe):
            for g in range(NSB + 1):
                if g < NSB:
                    if g >= 2:
                        pe.wait_ge(copied if w_out is not None else added, g - 1)
                    for t in range(SB):
                        mm = pe.transpose(turn_ps[:, g % 2, t * P:(t + 1) * P], ctx_out[:, SB * g + t, :], k["ident"][:, :])
                    mm.then_inc(turned, 1)
                if w_out is not None and g:
                    pe.wait_ge(copied, g)
                    if g >= 3:
                        pe.wait_ge(added, g - 2)
                    pe.matmul(mix_ps[:, (g - 1) % 2, :], w_out[:, :], flat[:, (g - 1) % 2, :], start=True, stop=True)\
                      .then_inc(mixed, 1)

        if w_out is not None:
            @block.scalar
            def _(act):
                for g in range(NSB):
                    act.wait_ge(turned, g + 1)
                    if g >= 2:
                        act.wait_ge(mixed, g - 1)
                    act.activation(flat[:, g % 2, :], turn_ps[:, g % 2, :], ACT.Copy).then_inc(copied, 1)

        @block.vector
        def _(dve):
            for g in range(NSB):
                dve.wait_ge(mixed if w_out is not None else turned, g + 1)
                src = mix_ps if w_out is not None else turn_ps
                x = X[:, image * T + g * CH:image * T + (g + 1) * CH]
                dve.tensor_tensor(x, x, src[:, g % 2, :], ALU.add).then_inc(added, 1)


PAIRS = ((0, 0), (0, 1), (1, 0), (1, 1), (0, 2), (2, 0))
ROWS = D3 * len(PAIRS)


def attention_l3(nc, k, dram, X):
    qk_parts = nc.dram_tensor("l3_qk_parts", [2, 3, P, T], BF16).ap()
    ctx_dram = nc.dram_tensor("l3_ctx", [2, P, T], F32).ap()
    den_dram, inv_dram = (nc.dram_tensor(f"l3_{n}", [NH3, T], F32) for n in ("den", "inv"))
    with ExitStack() as c:
        m = Memory(nc, c)
        w = m.sb("l3_w", [P, 3 * P])
        w_out = m.sb("l3_w_out", [P, P])
        XN = m.sb("l3_xn", [P, TOK])
        with ExitStack() as c2:
            w_loaded = Memory(nc, c2).sem("l3_w_loaded")
            block = c2.enter_context(nc.Block())

            @block.sync
            def _(sp):
                sp.dma_start(w[:, :], dram["L3_attn_w_attn"]).then_inc(w_loaded, 16)
                sp.dma_start(w_out[:, :], dram["L3_attn_w_proj"]).then_inc(w_loaded, 16)
                sp.wait_ge(w_loaded, 32)
        layer_norm(nc, k, "l3a_ln", X, XN, "eps5")
        v_all = m.sb("l3_v_all", [P, NH3, QT, D3 + 1])
        for b in range(BATCH):
            split_qkv(nc, k, f"l3p{b}", b, XN, w, v_all, qk_parts)
            with ExitStack() as c2:
                mm = Memory(nc, c2)
                bufs = [{"q": mm.sb(f"l3_q{b}{u}", [P, T], BF16), "k": mm.sb(f"l3_k{b}{u}", [P, T], BF16),
                         "v": mm.sb(f"l3_v{b}{u}", [P, QT, D3 + 1])} for u in range(2)]
                for q in bufs:
                    q["minus_max"] = q["q"]
                with ExitStack() as c3:
                    ones = Memory(nc, c3).sem(f"l3_ones{b}")
                    block = c3.enter_context(nc.Block())

                    @block.vector
                    def _(dve):
                        for q in bufs:
                            dve.memset(q["k"][96:128, :], 1.0).then_inc(ones, 1)

                def feed(sp, u, it, sem):
                    for n, pair in enumerate(PAIRS):
                        for side, name in enumerate(("q", "k")):
                            rows = qk_parts[side, pair[side], ds(it * D3, D3), :]
                            sp.dma_start(bufs[u][name][n * D3:(n + 1) * D3, :], rows).then_inc(sem, 16)
                    sp.dma_start(bufs[u]["v"][:, :, :], v_all[:, ds(it, 1), :, :].rearrange("p h t e -> p (h t) e")).then_inc(sem, 16)

                def keep(sp, it, s, out, sem):
                    at = slice(s * CH, (s + 1) * CH)
                    for n in range(2):
                        sp.dma_start(ctx_dram[n][ds(it * D3, D3), at], out[n * VPART:n * VPART + D3, :]).then_inc(sem, 16)
                    sp.dma_start(den_dram.ap()[ds(it, 1), at], out[D3:D3 + 1, :]).then_inc(sem, 16)

                attention_heads(nc, k, f"l3s{b}", NH3, D3, 1.0 / D3 ** 0.5, bufs, ROWS, feed, 2 * len(PAIRS) + 1, keep)
            add_heads(nc, f"l3f{b}", b, X, ctx_dram, den_dram, inv_dram, w_out)


def add_heads(nc, tag, image, X, ctx_dram, den_dram, inv_dram, w_out):
    with ExitStack() as c:
        m = Memory(nc, c)
        ctx_out, ctx_low, inv = (m.sb(f"{tag}_{n}", [P, T]) for n in ("ctx", "ctx_low", "inv"))
        den, small = m.sb(f"{tag}_den", [P, NH3 * T // P]), m.sb(f"{tag}_small", [P, NH3 * T // P])
        mix_ps = m.ps(f"{tag}_mix_ps", [P, 2, CH])
        loaded, summed, den_loaded, inverted, inv_stored, inv_loaded, divided, mixed, added = (
            m.sem(f"{tag}_{n}") for n in ("loaded", "summed", "den_loaded", "inverted", "inv_stored", "inv_loaded", "divided",
                                          "mixed", "added"))
        block = c.enter_context(nc.Block())

        @block.sync
        def _(sp):
            wide = dict(den=den_dram.ap().rearrange("h (g x) -> (h g) x", g=P // NH3),
                        inv=inv_dram.ap().rearrange("h (g x) -> (h g) x", g=P // NH3))
            sp.dma_start(den[:, :], wide["den"]).then_inc(den_loaded, 16)
            sp.dma_start(ctx_out[:, :], ctx_dram[0]).then_inc(loaded, 16)
            sp.dma_start(ctx_low[:, :], ctx_dram[1]).then_inc(loaded, 16)
            sp.wait_ge(inverted, 1)
            sp.dma_start(wide["inv"], small[:, :]).then_inc(inv_stored, 16)
            sp.wait_ge(inv_stored, 16)
            sp.dma_start(inv[:, :], bass.AP(tensor=inv_dram, offset=0, ap=[[T, NH3], [0, D3], [1, T]])).then_inc(inv_loaded, 16)

        @block.tensor
        def _(pe):
            for g in range(NSB):
                pe.wait_ge(divided, g + 1)
                if g >= 2:
                    pe.wait_ge(added, g - 1)
                pe.matmul(mix_ps[:, g % 2, :], w_out[:, :], ctx_out[:, g * CH:(g + 1) * CH], start=True, stop=True)\
                  .then_inc(mixed, 1)

        @block.gpsimd
        def _(pool):
            pool.wait_ge(summed, 1)
            pool.wait_ge(inv_loaded, 16)
            for g in range(NSB):
                at = slice(g * CH, (g + 1) * CH)
                pool.tensor_tensor(ctx_out[:, at], ctx_out[:, at], inv[:, at], ALU.mult).then_inc(divided, 1)

        @block.vector
        def _(dve):
            dve.wait_ge(den_loaded, 16)
            dve.reciprocal(small[:, :], den[:, :]).then_inc(inverted, 1)
            dve.wait_ge(loaded, 32)
            dve.tensor_tensor(ctx_out[:, :], ctx_out[:, :], ctx_low[:, :], ALU.add).then_inc(summed, 1)
            for g in range(NSB):
                dve.wait_ge(mixed, g + 1)
                x = X[:, image * T + g * CH:image * T + (g + 1) * CH]
                dve.tensor_tensor(x, x, mix_ps[:, g % 2, :], ALU.add).then_inc(added, 1)


def split_qkv(nc, k, tag, b, XN, w, v_all, qk_parts):
    with ExitStack() as c:
        m = Memory(nc, c)
        R = 4
        qk_ps, v_ps = m.ps(f"{tag}_qk_ps", [P, R, CH]), m.ps(f"{tag}_v_ps", [P, 2, CH])
        part = [m.sb(f"{tag}_part{n}", [P, T], BF16) for n in range(6)]
        rest = m.sb(f"{tag}_rest", [P, R, CH])
        ready, first, rest1, second, third, stored, v_ready, v_copied = (
            m.sem(f"{tag}_{n}") for n in ("ready", "first", "rest1", "second", "third", "stored", "v_ready", "v_copied"))
        block = c.enter_context(nc.Block())
        NB = T // CH

        def columns(g):
            return slice(g % NB * CH, (g % NB + 1) * CH)

        @block.tensor
        def _(pe):
            for g in range(2 * NB):
                if g >= R:
                    pe.wait_ge(rest1, g - R + 1)
                pe.matmul(qk_ps[:, g % R, :], w[:, g // NB * P:(g // NB + 1) * P],
                          XN[:, b * T + g % NB * CH:b * T + (g % NB + 1) * CH], start=True, stop=True).then_inc(ready, 1)
            for g in range(NB):
                if g >= 2:
                    pe.wait_ge(v_copied, g - 1)
                for t in range(4):
                    n = b * T + g * CH + t * P
                    mm = pe.matmul(v_ps[:, g % 2, t * P:(t + 1) * P], XN[:, n:n + P], w[:, 2 * P:3 * P], start=True, stop=True)
                mm.then_inc(v_ready, 1)

        @block.scalar
        def _(act):
            for g in range(2 * NB + 1):
                if g < 2 * NB:
                    act.wait_ge(ready, g + 1)
                    act.activation(part[g // NB * 3][:, columns(g)], qk_ps[:, g % R, :], ACT.Copy).then_inc(first, 1)
                if g:
                    act.wait_ge(rest1, g)
                    act.activation(part[(g - 1) // NB * 3 + 1][:, columns(g - 1)], rest[:, (g - 1) % R, :], ACT.Copy).then_inc(second, 1)

        @block.vector
        def _(dve):
            dve.memset(v_all[:, :, :, D3:D3 + 1], 1.0)
            for g in range(2 * NB + 1):
                if g < 2 * NB:
                    dve.wait_ge(first, g + 1)
                    if g >= R:
                        dve.wait_ge(third, g - R + 1)
                    dve.tensor_tensor(rest[:, g % R, :], qk_ps[:, g % R, :], part[g // NB * 3][:, columns(g)], ALU.subtract)\
                       .then_inc(rest1, 1)
                if g:
                    dve.wait_ge(second, g)
                    n = (g - 1) // NB * 3
                    dve.tensor_tensor(part[n + 2][:, columns(g - 1)], rest[:, (g - 1) % R, :], part[n + 1][:, columns(g - 1)],
                                      ALU.subtract).then_inc(third, 1)
            for g in range(NB):
                dve.wait_ge(v_ready, g + 1)
                src = v_ps[:, g % 2, :].rearrange("p (t h d) -> p h t d", t=4, h=NH3)
                for t in range(4):
                    ins = dve.tensor_copy(v_all[:, :, 4 * g + t, 0:D3], src[:, :, t, :])
                ins.then_inc(v_copied, 1)

        @block.sync
        def _(sp):
            for side in range(2):
                sp.wait_ge(third, NB * (side + 1))
                for n in range(3):
                    sp.dma_start(qk_parts[side, n], part[side * 3 + n][:, :]).then_inc(stored, 16)
            sp.wait_ge(stored, 96)


def attention_l2(nc, k, dram, X):
    with ExitStack() as c:
        m = Memory(nc, c)
        w = m.sb("l2_w", [P, 3, P])
        XN = m.sb("l2_xn", [P, TOK])
        q, kk = ([m.sb(f"l2_{name}{n}", [P, T], F32R) for n in range(2)] for name in ("q", "k"))
        v = m.sb("l2_v", [P, QT, P + 1])
        minus_max, ones = m.sb("l2_minus_max", [P, T], BF16), m.sb("l2_ones", [P, P], BF16)
        result = m.sb("l2_result", [P, QT, P])
        with ExitStack() as c2:
            mm = Memory(nc, c2)
            w_loaded, filled = mm.sem("l2_w_loaded"), mm.sem("l2_filled")
            block = c2.enter_context(nc.Block())

            @block.sync
            def _(sp):
                for n, name in enumerate(("L2_attn_Wq", "L2_attn_Wk", "L2_attn_Wv")):
                    sp.dma_start(w[:, n, :], dram[name]).then_inc(w_loaded, 16)
                sp.wait_ge(w_loaded, 48)

            @block.vector
            def _(dve):
                dve.memset(ones[:, :], 1.0).then_inc(filled, 1)
                dve.memset(v[:, :, P:P + 1], 1.0).then_inc(filled, 1)
        layer_norm(nc, k, "l2a_ln", X, XN, "eps5")
        for b in range(BATCH):
            project_qkv(nc, k, f"l2p{b}", b, XN, w, q, kk, v)

            def product(pe, out, left, rows, right, cols):
                for n, (i, j) in enumerate(((0, 0), (0, 1), (1, 0))):
                    mm = pe.matmul(out, left[i][:, rows], right[j][:, cols], start=(n == 0), stop=(n == 2), skip_group_check=True)
                return mm

            def score_max(pe, u, out, tile, k0, width):
                return product(pe, out, q, slice(tile * P, (tile + 1) * P), kk, slice(k0, k0 + width))

            def score_exp(pe, u, out, j, q0, width):
                product(pe, out, kk, slice(j * P, (j + 1) * P), q, slice(q0, q0 + width))
                return pe.matmul(out, ones[96:99, :], minus_max[96:99, q0:q0 + width], start=False, stop=True,
                                 skip_group_check=True)

            causal_attention(nc, k, f"l2s{b}", 1, P, 1.0 / T ** 0.5, [{"minus_max": minus_max, "v": v}],
                             score_max, score_exp, None, 0, lambda it: result[:, :, :])
            add_attention(nc, k, f"l2f{b}", b, X, result, None)


def project_qkv(nc, k, tag, b, XN, w, q, kk, v):
    with ExitStack() as c:
        m = Memory(nc, c)
        ps = m.ps(f"{tag}_ps", [P, 4, CH])
        ready, high, low, copied_v = (m.sem(f"{tag}_{n}") for n in ("ready", "high", "low", "copied_v"))
        block = c.enter_context(nc.Block())
        NB = T // CH

        @block.tensor
        def _(pe):
            for g in range(NB):
                if g:
                    pe.wait_ge(low, 2 * g)
                    pe.wait_ge(copied_v, g)
                at = slice(b * T + g * CH, b * T + (g + 1) * CH)
                for n in range(2):
                    pe.matmul(ps[:, n, :], w[:, n, :], XN[:, at], start=True, stop=True).then_inc(ready, 1)
                for t in range(4):
                    n = b * T + g * CH + t * P
                    mm = pe.matmul(ps[:, 2, t * P:(t + 1) * P], XN[:, n:n + P], w[:, 2, :], start=True, stop=True)
                mm.then_inc(ready, 1)

        @block.scalar
        def _(act):
            for g in range(NB):
                for n, dst in enumerate((q, kk)):
                    act.wait_ge(ready, 3 * g + n + 1)
                    act.activation(dst[0][:, g * CH:(g + 1) * CH], ps[:, n, :], ACT.Copy).then_inc(high, 1)

        @block.vector
        def _(dve):
            for g in range(NB):
                at = slice(g * CH, (g + 1) * CH)
                for n, dst in enumerate((q, kk)):
                    dve.wait_ge(high, 2 * g + n + 1)
                    dve.tensor_tensor(dst[1][:, at], ps[:, n, :], dst[0][:, at].bitcast(F32), ALU.subtract).then_inc(low, 1)
                dve.wait_ge(ready, 3 * g + 3)
                dve.tensor_copy(v[:, 4 * g:4 * g + 4, 0:P], ps[:, 2, :].rearrange("p (t e) -> p t e", t=4))\
                   .then_inc(copied_v, 1)


NE = 8


def experts_l2(nc, k, dram, X):
    with ExitStack() as c:
        m = Memory(nc, c)
        rw, rb = m.sb("moe_rw", [P, NE]), m.sb("moe_rb", [P, NE])
        ew, eb = m.sb("moe_ew", [P, NE, P]), m.sb("moe_eb", [NE * 8, 8, P])
        iota = m.sb("moe_iota", [P, NE])
        XN = m.sb("moe_xn", [P, TOK])
        with ExitStack() as c2:
            mm = Memory(nc, c2)
            loaded, cleared = mm.sem("moe_loaded"), mm.sem("moe_cleared")
            block = c2.enter_context(nc.Block())

            @block.sync
            def _(sp):
                sp.dma_start(rw[:, :], dram["L2_ffn_router_w"]).then_inc(loaded, 16)
                sp.dma_start(rb[:, :], dram["L2_ffn_router_b"].to_broadcast([P, NE])).then_inc(loaded, 16)
                sp.dma_start(ew[:, :, :], dram["L2_ffn_expert_w"].rearrange("e d c -> d e c")).then_inc(loaded, 16)
                sp.wait_ge(cleared, 1)
                for u in range(8):
                    sp.dma_start(eb[u * NE:(u + 1) * NE, u, :], dram["L2_ffn_expert_b"]).then_inc(loaded, 16)
                sp.dma_start(iota[:, :], dram["c_iota"]).then_inc(loaded, 16)
                sp.wait_ge(loaded, 12 * 16)

            @block.vector
            def _(dve):
                dve.memset(eb[:, :, :], 0.0).then_inc(cleared, 1)
        layer_norm(nc, k, "moe_ln", X, XN, "eps5")

        G = 8
        tile = m.sb("moe_tile", [P, G, P])
        logits, best, wheref, gate2, gate = (m.sb(f"moe_{n}", [P, G, NE]) for n in ("logits", "best", "wheref", "gate2", "gate"))
        where = m.sb("moe_where", [P, G, NE], U32)
        less, e2, total, inv = (m.sb(f"moe_{n}", [P, G]) for n in ("less", "e2", "total", "inv"))
        gate_t = m.sb("moe_gate_t", [G * NE, P])
        mix, odd = m.sb("moe_mix", [P, 2, P]), m.sb("moe_odd", [P, P])
        route_ps = m.ps("moe_route_ps", [P, CH])
        bias_ps = m.ps("moe_bias_ps", [P, 2, CH])
        flat_ps = m.ps("moe_flat_ps", [P, CH])
        expert_ps = m.ps("moe_expert_ps", [P, 2, 2, CH])
        taken, routed, expert_ready, step, e2_ready, gated, turned, gate_copied, biased, seeded, acc, mixed, flat, added = (
            m.sem(f"moe_{n}") for n in ("taken", "routed", "expert_ready", "step", "e2_ready", "gated", "turned",
                                        "gate_copied", "biased", "seeded", "acc", "mixed", "flat", "added"))
        block = c.enter_context(nc.Block())
        STEPS = 10 + 2 * G

        @block.gpsimd
        def _(pool):
            with pool.Fori(0, TOK // (G * P)) as i:
                for u in range(G):
                    wait_apart(pool, expert_ready, i * G + u + 1)
                    pool.tensor_copy(tile[:, u, :], XN[:, ds(i * G * P + u * P, P)]).then_inc(taken, 1)

        @block.tensor
        def _(pe):
            pe.sem_inc(expert_ready, G)
            with pe.Fori(0, TOK // (G * P)) as i:
                def experts(u):
                    pe.wait_ge(mixed, i * G + u + 1)
                    for n in range(2):
                        mm = pe.matmul(expert_ps[:, u % 2, n, :], tile[:, u, :], ew[:, 4 * n:4 * n + 4, :], start=True, stop=True)
                    mm.then_inc(expert_ready, 1)

                def biases(u):
                    pe.matmul(bias_ps[:, u % 2, 0:P], gate_t[:, :], eb[:, u, :], start=True, stop=True).then_inc(biased, 1)

                for u in range(G):
                    pe.wait_ge(taken, i * G + u + 1)
                    mm = pe.matmul(route_ps[:, u * NE:(u + 1) * NE], tile[:, u, :], rw[:, :], start=(u == 0), stop=True,
                                   skip_group_check=True)
                mm.then_inc(routed, 1)
                experts(0)
                experts(1)
                pe.wait_ge(gated, i + 1)
                pe.matmul(route_ps[0:G * NE, P:2 * P], gate[:, :, :].rearrange("p g e -> p (g e)"), k["ident"][:, :],
                          start=True, stop=True).then_inc(turned, 1)
                pe.wait_ge(gate_copied, i + 1)
                biases(0)
                biases(1)
                for u in range(G):
                    if u % 2 == 0:
                        pe.wait_ge(added, i * (G // 2) + u // 2 + 1)
                    pe.wait_ge(mixed, i * G + u + 3)
                    pe.transpose(flat_ps[:, u % 2 * P:(u % 2 + 1) * P], mix[:, u % 2, :], k["ident"][:, :]).then_inc(flat, 1)
                    if u + 2 < G:
                        experts(u + 2)
                        biases(u + 2)

        @block.scalar
        def _(act):
            act.sem_inc(flat, 2)
            with act.Fori(0, TOK // (G * P)) as i:
                act.wait_ge(step, i * STEPS + (2 * G + 2))
                act.activation(e2[:, :], less[:, :], ACT.Exp).then_inc(e2_ready, 1)
                act.wait_ge(turned, i + 1)
                act.activation(gate_t[:, :], route_ps[0:G * NE, P:2 * P], ACT.Copy).then_inc(gate_copied, 1)
                for u in range(G):
                    act.wait_ge(biased, i * G + u + 1)
                    act.wait_ge(flat, i * G + u + 1)
                    act.activation(mix[:, u % 2, :], bias_ps[:, u % 2, 0:P], ACT.Copy).then_inc(seeded, 1)

        @block.vector
        def _(dve):
            dve.sem_inc(added, 1)
            dve.sem_inc(mixed, 2)
            with dve.Fori(0, TOK // (G * P)) as i:
                count = [0]

                def then(ins):
                    ins.then_inc(step, 1)
                    count[0] += 1

                def settle():
                    dve.wait_ge(step, i * STEPS + count[0])

                def over_experts(a):
                    return a.unsqueeze(2).to_broadcast([P, G, NE])

                def over_tiles(a):
                    return a.unsqueeze(1).to_broadcast([P, G, NE])

                dve.wait_ge(routed, i + 1)
                then(dve.tensor_tensor(logits[:, :, :], route_ps[:, 0:G * NE].rearrange("p (g e) -> p g e", g=G), over_tiles(rb[:, :]), ALU.add))
                wait_apart(dve, step, i * STEPS + count[0])
                for g in range(G):
                    then(dve.max(best[:, g, :], logits[:, g, :]))
                wait_apart(dve, step, i * STEPS + count[0])
                then(dve.tensor_tensor(less[:, :], best[:, :, 1], best[:, :, 0], ALU.subtract))
                for g in range(G):
                    then(dve.max_index(where[:, g, :], best[:, g, :], logits[:, g, :]))
                settle()
                then(dve.tensor_copy(wheref[:, :, :], where[:, :, :]))
                dve.wait_ge(e2_ready, i + 1)
                then(dve.tensor_scalar(total[:, :], e2[:, :], 1.0, None, ALU.add))
                settle()
                then(dve.reciprocal(inv[:, :], total[:, :]))
                then(dve.tensor_tensor(gate2[:, :, :], over_tiles(iota[:, :]), over_experts(wheref[:, :, 1]), ALU.is_equal))
                then(dve.tensor_tensor(gate[:, :, :], over_tiles(iota[:, :]), over_experts(wheref[:, :, 0]), ALU.is_equal))
                settle()
                then(dve.tensor_tensor(gate2[:, :, :], gate2[:, :, :], over_experts(e2[:, :]), ALU.mult))
                settle()
                then(dve.tensor_tensor(gate[:, :, :], gate[:, :, :], gate2[:, :, :], ALU.add))
                settle()
                then(dve.tensor_tensor(gate[:, :, :], gate[:, :, :], over_experts(inv[:, :]), ALU.mult))
                assert count[0] == STEPS
                settle()
                dve.sem_inc(gated, 1)

                def add(n):
                    dve.wait_ge(flat, i * G + 2 * n + 4)
                    x = X[:, ds(i * G * P + n * 2 * P, 2 * P)]
                    dve.tensor_tensor(x, x, flat_ps[:, 0:2 * P], ALU.add).then_inc(added, 1)

                for u in range(G):
                    dve.wait_ge(expert_ready, i * G + u + 1 + G)
                    for e in range(NE):
                        to = odd[:, :] if e % 2 else mix[:, u % 2, :]
                        values, weight = expert_ps[:, u % 2, e // 4, e % 4 * P:(e % 4 + 1) * P], gate[:, u, e:e + 1]
                        if e == 0:
                            dve.wait_ge(seeded, i * G + u + 1)
                        if e == 1:
                            dve.wait_ge(mixed, i * G + u + 2)
                            ins = dve.tensor_scalar(to, values, weight, None, ALU.mult)
                        else:
                            if e:
                                dve.wait_ge(acc, i * (G * NE) + (u * NE + e - 1))
                            ins = dve.scalar_tensor_tensor(to, values, weight, to, ALU.mult, ALU.add)
                        ins.then_inc(acc, 1)
                    dve.wait_ge(acc, i * (G * NE) + (u + 1) * NE)
                    dve.tensor_tensor(mix[:, u % 2, :], mix[:, u % 2, :], odd[:, :], ALU.add).then_inc(mixed, 1)
                    if u and u % 2 == 0:
                        add(u // 2 - 1)
                add(G // 2 - 1)



HALF = T // 2
NJ = HALF // P
NC4 = HALF // CH
PAD = P
REG = (0, 1, 2, 3)


def filters_l3(nc, k, dram, X):
    lags = nc.dram_tensor("stu_lags", [NK, 2, 2, PAD + HALF], F32)
    n_dram = nc.dram_tensor("stu_n", [NK + 2, P, 2 * P], F32).ap()
    with ExitStack() as c:
        m = Memory(nc, c)
        reach, mu = m.sb("stu_reach", [P, 4]), m.sb("stu_mu", [P, 3, P])
        UR = m.sb("stu_ur", [P, BATCH, 2, NJ, P])
        filter_inputs(nc, k, dram, n_dram, lags.ap(), reach, mu)
        with ExitStack() as c2:
            XN = Memory(nc, c2).sb("stu_xn", [P, TOK])
            layer_norm(nc, k, "stu_ln", X, XN, "eps5")
            short_filter(nc, k, X, XN, UR, reach, mu)
        long_filter(nc, k, X, UR, reach, lags, n_dram)


def filter_inputs(nc, k, dram, n_dram, lags, reach, mu):
    with ExitStack() as c:
        m = Memory(nc, c)
        small = m.sb("fw_small", [P, 12, 8])
        where, wheref = m.sb("fw_where", [P, 8], U32), m.sb("fw_wheref", [P, 8])
        iota = m.sb("fw_iota", [P, 8])
        lw, gu, sig = m.sb("fw_lw", [P, 4]), m.sb("fw_gu", [P, 4]), m.sb("fw_sig", [P, NK])
        s1, s2 = m.sb("fw_s1", [P, NK]), m.sb("fw_s2", [P, NK])
        mats = m.sb("fw_mats", [P, 2, 4, NK, P])
        seg = HALF // 4
        phi, phi_part = m.sb("fw_phi", [P, seg]), m.sb("fw_phi_part", [P, 2, seg], F32R)
        zeros, zeros_r = m.sb("fw_zeros", [2 * NK, 2, PAD]), m.sb("fw_zeros_r", [2 * NK, 2, PAD], F32R)
        acc = m.sb("fw_acc", [P, 2, NK, P])
        both = m.sb("fw_both", [P, NK, 2, P])
        mus = m.sb("fw_mus", [P, 4, 3, P])
        mats_loaded = [m.sem(f"fw_mats_loaded{n}") for n in range(2)]
        loaded, step, exped, rooted, stored, phi_loaded, phi_step, phi_stored = (
            m.sem(f"fw_{n}") for n in ("loaded", "step", "exped", "rooted", "stored", "phi_loaded",
                                       "phi_step", "phi_stored"))
        block = c.enter_context(nc.Block())

        @block.sync
        def _(sp):
            sp.dma_start(phi[:, :], dram["L3_ffn_phi"]).then_inc(phi_loaded, 16)
            sp.dma_start(lw[:, :], dram["L3_ffn_log_weights"].to_broadcast([P, 4])).then_inc(loaded, 16)
            sp.dma_start(gu[:, :], dram["L3_ffn_gumbel"].to_broadcast([P, 4])).then_inc(loaded, 16)
            sp.dma_start(sig[:, :], dram["L3_ffn_sigma"].to_broadcast([P, NK])).then_inc(loaded, 16)
            sp.dma_start(iota[:, :], dram["c_iota"]).then_inc(loaded, 16)
            sp.dma_start(mus[:, :, :, :], dram["L3_ffn_M_u"].rearrange("i j d e -> d i j e")).then_inc(loaded, 16)
            for n, name in enumerate(("L3_ffn_M_phi_plus", "L3_ffn_M_phi_minus")):
                for i in range(4):
                    sp.dma_start(mats[:, n, i, :, :], dram[name][i].rearrange("k d e -> d k e")).then_inc(mats_loaded[n], 16)
            sp.wait_ge(phi_step, 4)
            for n in range(2):
                for kk in range(NK):
                    sp.dma_start(lags[kk, :, n, PAD:PAD + HALF].rearrange("a (g x) -> a g x", g=4),
                                 phi_part[kk * 8:kk * 8 + 8, n, :].bitcast(F32)).then_inc(phi_stored, 16)
            sp.dma_start(lags[:, :, :, 0:PAD].rearrange("k a n x -> (k a) n x"), zeros_r[:, :, :].bitcast(F32)).then_inc(phi_stored, 16)
            sp.wait_ge(phi_stored, 16 * (2 * NK + 1))
            sp.wait_ge(step, 26)
            sp.dma_start(n_dram[0:NK].rearrange("k d e -> d k e"), both[:, :, :, :].rearrange("p k n e -> p k (n e)")).then_inc(stored, 16)
            sp.dma_start(n_dram[NK:NK + 2].rearrange("k d e -> d k e"), both[:, 0:2, :, :].rearrange("p k n e -> p k (n e)")).then_inc(stored, 16)
            sp.wait_ge(stored, 32)

        @block.scalar
        def _(act):
            act.wait_ge(loaded, 80)
            act.activation(s1[:, :], sig[:, :], ACT.Sqrt).then_inc(rooted, 1)
            act.wait_ge(rooted, 1)
            act.activation(s2[:, :], s1[:, :], ACT.Sqrt).then_inc(rooted, 1)
            act.wait_ge(step, 4)
            act.activation(small[:, 2, :], small[:, 1, :], ACT.Exp).then_inc(exped, 1)

        @block.vector
        def _(dve):
            count = [0]

            def then(ins):
                ins.then_inc(step, 1)
                count[0] += 1
                dve.wait_ge(step, count[0])

            logits, less, ex, soft, hot, wt = (small[:, n, :] for n in (0, 1, 2, 3, 4, 5))
            top, total, inv = small[:, 6, :], small[:, 7, 0:1], small[:, 7, 1:2]
            dve.memset(zeros[:, :, :], 0.0).then_inc(phi_step, 1)
            dve.wait_ge(phi_step, 1)
            dve.tensor_copy(zeros_r[:, :, :], zeros[:, :, :]).then_inc(phi_step, 1)
            dve.wait_ge(phi_loaded, 16)
            dve.tensor_copy(phi_part[:, 0, :], phi[:, :]).then_inc(phi_step, 1)
            dve.wait_ge(phi_step, 3)
            dve.tensor_tensor(phi_part[:, 1, :], phi[:, :], phi_part[:, 0, :].bitcast(F32), ALU.subtract).then_inc(phi_step, 1)

            then(dve.memset(small[:, :, :], NEG))
            dve.wait_ge(loaded, 80)
            then(dve.tensor_tensor(logits[:, 0:4], lw[:, :], gu[:, :], ALU.add))
            then(dve.max(top, logits))
            then(dve.tensor_scalar(less, logits, top[:, 0:1], None, ALU.subtract))
            dve.wait_ge(exped, 1)
            then(dve.tensor_reduce(total, ex, AX, ALU.add))
            then(dve.reciprocal(inv, total))
            then(dve.tensor_scalar(soft, ex, inv, None, ALU.mult))
            then(dve.max(top, soft))
            then(dve.max_index(where[:, :], top, soft))
            then(dve.tensor_copy(wheref[:, :], where[:, :]))
            then(dve.tensor_scalar(hot, iota[:, :], wheref[:, 0:1], None, ALU.is_equal))
            then(dve.tensor_tensor(wt, hot, soft, ALU.subtract))
            then(dve.tensor_tensor(wt, wt, soft, ALU.add))
            for r in range(4):
                last = dve.tensor_reduce(reach[:, r:r + 1], hot[:, 0:4 - r], AX, ALU.add)
            then(last)
            for bank in range(2):
                dve.wait_ge(mats_loaded[bank], 64)
                then(dve.tensor_scalar(acc[:, bank, :, :], mats[:, bank, 0, :, :], wt[:, 0:1], None, ALU.mult))
                for i in range(1, 4):
                    then(dve.scalar_tensor_tensor(acc[:, bank, :, :], mats[:, bank, i, :, :], wt[:, i:i + 1], acc[:, bank, :, :],
                                                  ALU.mult, ALU.add))
            dve.wait_ge(rooted, 2)
            root = s2[:, :].unsqueeze(2).to_broadcast([P, NK, P])
            for n, op in enumerate((ALU.add, ALU.subtract)):
                then(dve.tensor_tensor(both[:, :, n, :], acc[:, 0, :, :], acc[:, 1, :, :], op))
                then(dve.tensor_tensor(both[:, :, n, :], both[:, :, n, :], root, ALU.mult))
            then(dve.tensor_scalar(mu[:, :, :], mus[:, 0, :, :], wt[:, 0:1], None, ALU.mult))
            for i in range(1, 4):
                then(dve.scalar_tensor_tensor(mu[:, :, :], mus[:, i, :, :], wt[:, i:i + 1], mu[:, :, :], ALU.mult, ALU.add))


def spans(c):
    return [(0, CH // 2, 0), (CH // 2, CH, 1)] if c == 0 else [(0, CH, 2 if c == 1 else 3)]


def short_filter(nc, k, X, XN, UR, reach, mu):
    with ExitStack() as c:
        m = Memory(nc, c)
        ps = m.ps("sf_ps", [P, 2, CH])
        ready, added, laid = m.sem("sf_ready"), m.sem("sf_added"), m.sem("sf_laid")
        block = c.enter_context(nc.Block())

        @block.tensor
        def _(pe):
            for g in range(NCH):
                if g >= 2:
                    pe.wait_ge(added, g - 1)
                edge = g % (NCH // 2) == 0
                for i in range(3):
                    o = i if edge else 0
                    mm = pe.matmul(ps[:, g % 2, o:CH], mu[:, i, :], XN[:, g * CH - i + o:(g + 1) * CH - i],
                                   start=(i == 0), stop=True, skip_group_check=True)
                mm.then_inc(ready, 1)

        @block.scalar
        def _(act):
            for b in range(BATCH):
                for par in range(2):
                    src = XN[:, b * T:(b + 1) * T].rearrange("p (j r a) -> p j r a", j=NJ, a=2)[:, :, ::-1, par]
                    act.activation(UR[:, b, par, :, :], src, ACT.Copy).then_inc(laid, 1)

        @block.vector
        def _(dve):
            for g in range(NCH):
                c8 = g % (NCH // 2)
                regime = 0 if c8 == 0 else 1 if c8 == 1 else 2 if c8 < 4 else 3
                x = X[:, g * CH:(g + 1) * CH]
                dve.wait_ge(ready, g + 1)
                dve.scalar_tensor_tensor(x, ps[:, g % 2, :], reach[:, regime:regime + 1], x, ALU.mult, ALU.add).then_inc(added, 1)


def long_filter(nc, k, X, UR, reach, lags, n_dram):
    with ExitStack() as c:
        m = Memory(nc, c)
        toep = [[[m.sb(f"lf_toep{kk}{a}{n}", [P, HALF + 2], F32R) for n in range(2)] for a in range(2)] for kk in range(2)]
        nk = m.sb("lf_nk", [P, 2, 2 * P])
        z = [m.sb(f"lf_z{n}", [P, 4, 2, 4, 2, P], F32R) for n in range(2)]
        z_ps = m.ps("lf_z_ps", [P, 4, 2, 2, P])
        y_ps = m.ps("lf_y_ps", [P, 2, 2, CH])
        toep_loaded = [m.sem(f"lf_toep_loaded{kk}") for kk in range(2)]
        nk_loaded = [m.sem(f"lf_nk_loaded{kk}") for kk in range(2)]
        z_ready, z_high, z_low, conv_done, summed = (m.sem(f"lf_{n}") for n in ("z_ready", "z_high", "z_low", "conv_done", "summed"))
        block = c.enter_context(nc.Block())
        ZB = 4
        GROUPS = 4

        @block.sync
        def _(sp):
            def load_toep(kk, filt):
                for a in range(2):
                    for n in range(2):
                        rows = bass.AP(tensor=lags, offset=(a * 2 + n) * (PAD + HALF) + PAD - P,
                                       ap=[[4 * (PAD + HALF), NK], [1, P], [1, HALF + 1]])
                        sp.dma_start(toep[kk][a][n][:, 0:HALF + 1].bitcast(F32),
                                     rows[ds(filt, 1)].rearrange("k r x -> (k r) x")).then_inc(toep_loaded[kk], 16)

            for kk in range(2):
                sp.dma_start(nk[:, kk, :], n_dram[kk]).then_inc(nk_loaded[kk], 16)
                load_toep(kk, kk)
            with sp.Fori(0, NK // 2 - 1) as i:
                for kk in range(2):
                    sp.wait_ge(z_ready, i * (4 * GROUPS * ZB) + (2 * kk + 2) * GROUPS * ZB)
                    sp.dma_start(nk[:, kk, :], n_dram[ds(i * 2 + kk + 2, 1)].rearrange("k d e -> (k d) e")).then_inc(nk_loaded[kk], 16)
                    sp.wait_ge(conv_done, i * (4 * GROUPS) + (2 * kk + 2) * GROUPS)
                    load_toep(kk, i * 2 + kk + 2)
            sp.wait_ge(z_ready, (NK // 2 - 1) * 4 * GROUPS * ZB + 2 * GROUPS * ZB)
            sp.dma_start(nk[:, 0, :], n_dram[NK]).then_inc(nk_loaded[0], 16)

        def units(eng, body):
            with eng.Fori(0, NK // 2) as i:
                for q in range(4):
                    body(lambda per, j, q=q: i * (4 * per) + (q * per + j), q % 2, q // 2, i)

        @block.tensor
        def _(pe):
            def sources(b, kk, group, ready_at):
                for n in range(ZB):
                    pe.wait_ge(z_low, ready_at(n))
                    par, half = n // 2, n % 2
                    for j in range(2):
                        mm = pe.matmul(z_ps[:, n, j, :, :], UR[:, b, par, 4 * group + 2 * half + j, :], nk[:, kk, :],
                                       start=(j == 0), stop=True, skip_group_check=True)
                    mm.then_inc(z_ready, 1)

            def convolve(c4, kk, at):
                pe.wait_ge(summed, at(GROUPS, GROUPS - 1 - c4 + 1))
                for J in range(4 * c4 + 3, -1, -1):
                    if J % 4 == 3 and c4 == GROUPS - 1:
                        pe.wait_ge(z_low, at(GROUPS * ZB, (GROUPS - J // 4) * ZB + ZB))
                    x0 = max(0, J - 4 * c4) * P
                    lag = CH * c4 - P * J + x0
                    for out_par in range(2):
                        for src_par in range(2):
                            a = out_par ^ src_par
                            late = 1 if (src_par, out_par) == (1, 0) else 0
                            first = J == 4 * c4 + 3 and src_par == 0
                            for zn, tn in ((0, 0), (0, 1), (1, 0)):
                                mm = pe.matmul(y_ps[:, c4 % 2, out_par, x0:CH], z[zn][:, J // 4, src_par, J % 4, a, :],
                                               toep[kk][a][tn][:, 1 - late + lag:1 - late + lag + CH - x0],
                                               start=(first and (zn, tn) == (0, 0)), stop=(J == 0 and src_par == 1),
                                               skip_group_check=True)
                mm.then_inc(conv_done, 1)

            pe.wait_ge(nk_loaded[0], 16)
            for g in range(GROUPS - 1, -1, -1):
                sources(0, 0, g, lambda n, g=g: (GROUPS - 1 - g) * ZB + n + 1)

            def unit(at, b, kk, i):
                if b == 0:
                    pe.wait_ge(toep_loaded[kk], i * 64 + 64)
                for g in range(GROUPS - 1, -1, -1):
                    convolve(g, kk, at)
                    if g == GROUPS - 1 and b == 1:
                        pe.wait_ge(nk_loaded[1 - kk], i * 16 + (16 if kk == 0 else 32))
                    sources(1 - b, kk if b == 0 else 1 - kk, g, lambda n: at(GROUPS * ZB, GROUPS * ZB + (GROUPS - 1 - g) * ZB + n + 1))
            units(pe, unit)

        @block.scalar
        def _(act):
            def high(g, at):
                for n in range(ZB):
                    act.wait_ge(z_ready, at(n + 1))
                    act.activation(z[0][:, g, n // 2, n % 2 * 2:n % 2 * 2 + 2, :, :], z_ps[:, n, :, :, :], ACT.Copy).then_inc(z_high, 1)

            for g in range(GROUPS - 1, -1, -1):
                high(g, lambda n: (GROUPS - 1 - g) * ZB + n)

            def unit(at, b, kk, i):
                for g in range(GROUPS - 1, -1, -1):
                    high(g, lambda n: at(GROUPS * ZB, GROUPS * ZB + (GROUPS - 1 - g) * ZB + n))
            units(act, unit)

        @block.vector
        def _(dve):
            dve.sem_inc(z_low, ZB)
            dve.sem_inc(summed, 2)

            def low(g, at):
                for n in range(ZB):
                    dve.wait_ge(z_high, at(n + 1))
                    at_z = (slice(None), g, n // 2, slice(n % 2 * 2, n % 2 * 2 + 2), slice(None), slice(None))
                    dve.tensor_tensor(z[1][at_z], z_ps[:, n, :, :, :], z[0][at_z].bitcast(F32), ALU.subtract).then_inc(z_low, 1)

            for g in range(GROUPS - 1, -1, -1):
                low(g, lambda n: (GROUPS - 1 - g) * ZB + n)

            def unit(at, b, kk, i):
                for g in range(GROUPS - 1, -1, -1):
                    dve.wait_ge(conv_done, at(GROUPS, GROUPS - g))
                    dve.wait_ge(summed, at(GROUPS, GROUPS - 1 - g + 2))
                    for out_par in range(2):
                        for x0, x1, regime in spans(g):
                            t0 = b * T + 2 * (CH * g + x0) + out_par
                            x = X[:, t0:t0 + 2 * (x1 - x0) - 1:2]
                            ins = dve.scalar_tensor_tensor(x, y_ps[:, g % 2, out_par, x0:x1], reach[:, regime:regime + 1], x,
                                                           ALU.mult, ALU.add)
                    ins.then_inc(summed, 1)
                    low(g, lambda n: at(GROUPS * ZB, GROUPS * ZB + (GROUPS - 1 - g) * ZB + n))
            units(dve, unit)


NTILE = (HW // TR) * (HW // TC)
KEYS = WR * WC
NKC = 3
RING, PROB_RING = 2, 4


def neighbourhood_l0(nc, k, dram, X):
    with ExitStack() as c:
        m = Memory(nc, c)
        ya, yb = m.sb("na_ya", [P, TOK]), m.sb("na_yb", [P, TOK])
        masks = m.sb("na_masks", [P, NMASK, KEYS], BF16)
        w = m.sb("na_w", [P, 2, 4 * P])
        bias = m.sb("na_bias", [P, 2, 4])
        ln = m.sb("na_ln", [P, 2])
        with ExitStack() as c2:
            mm = Memory(nc, c2)
            wide = mm.sb("na_masks_f32", [P, NMASK, KEYS])
            loaded, made = mm.sem("na_loaded"), mm.sem("na_made")
            block = c2.enter_context(nc.Block())

            @block.sync
            def _(sp):
                sp.dma_start(wide[:, :, :], dram["c_window"]).then_inc(loaded, 16)
                sp.dma_start(w[:, :, :], dram["L0_w"]).then_inc(loaded, 16)
                sp.dma_start(bias[:, :, :], dram["L0_bias"]).then_inc(loaded, 16)
                sp.dma_start(ln[:, :], dram["L0_ln"]).then_inc(loaded, 16)
                sp.wait_ge(loaded, 64)

            @block.vector
            def _(dve):
                dve.wait_ge(loaded, 64)
                dve.tensor_copy(masks[:, :, :], wide[:, :, :]).then_inc(made, 1)
        group_norm(nc, k, "na_gn", X, ya)
        for layer in range(2):
            src, dst = (ya, yb) if layer == 0 else (yb, ya)
            neighbourhood(nc, k, f"na{layer}", layer, dram, src, dst, masks, w[:, layer, :], bias[:, layer, :])
        layer_norm(nc, k, "na_lnf", ya, ya, "eps5", gain=ln[:, 0:1], shift=ln[:, 1:2], add_to=X)


def neighbourhood(nc, k, tag, layer, dram, src, dst, masks, w, bias):
    with ExitStack() as c:
        m = Memory(nc, c)
        table = m.sb(f"{tag}_table", [P, NH0, BR, BC])
        keys_in, q_in = m.sb(f"{tag}_keys_in", [P, RING, KEYS]), m.sb(f"{tag}_q_in", [P, RING, P])
        kt, qt = m.sb(f"{tag}_kt", [P, RING, KEYS]), m.sb(f"{tag}_qt", [P, RING, P])
        vt = m.sb(f"{tag}_vt", [KC, RING, NKC, NH0, D0])
        neg = m.sb(f"{tag}_neg", [P, RING, KEYS])
        low = m.sb(f"{tag}_low", [P, RING])
        prob = m.sb(f"{tag}_prob", [P, PROB_RING, KEYS])
        prob_t = m.sb(f"{tag}_prob_t", [KC, RING, NKC * P])
        total, recip = m.sb(f"{tag}_total", [P, PROB_RING]), m.sb(f"{tag}_recip", [P, PROB_RING])
        mean_t = m.sb(f"{tag}_mean_t", [P, RING, P])
        k_ps, qv_ps = m.ps(f"{tag}_k_ps", [P, CH]), m.ps(f"{tag}_qv_ps", [P, CH])
        s_ps, t_ps = m.ps(f"{tag}_s_ps", [P, RING, CH]), m.ps(f"{tag}_t_ps", [P, RING, CH])
        o_ps = m.ps(f"{tag}_o_ps", [P, RING, CH])
        names = ("table_loaded", "taken", "k_ready", "k_copied", "qv_ready", "qv_copied", "s_ready", "s_read",
                 "p_ready", "inverted", "normed", "turned", "t_copied", "o_ready", "mean_copied", "y_ready", "y_copied")
        (table_loaded, taken, k_ready, k_copied, qv_ready, qv_copied, s_ready, s_read, p_ready, inverted, normed,
         turned, t_copied, o_ready, mean_copied, y_ready, y_copied) = (
            m.sem(f"{tag}_{n}") for n in names)
        block = c.enter_context(nc.Block())
        G = NTILE * NH0

        def grid(t):
            return t // (HW // TC), t % (HW // TC)

        def view(y, b, r0, nr, c0, ncol):
            return y[:, :].rearrange("p (b r c) -> p b r c", b=BATCH, r=HW)[:, ds(b, 1), r0:r0 + nr, c0:c0 + ncol]\
                .rearrange("p b r c -> p (b r) c")

        def images(eng, body):
            with eng.Fori(0, BATCH) as b:
                body(b, lambda per, j: b * per + j)

        @block.sync
        def _(sp):
            for a in range(TR):
                for h in range(NH0):
                    rows = bass.AP(tensor=dram["L0_rpb"].tensor, offset=((layer * NH0 + h) * PR + TR - 1 - a) * PC,
                                   ap=[[1, TC], [PC, BR], [1, BC]])
                    sp.dma_start(table[a * TC:(a + 1) * TC, h, :, :], rows).then_inc(table_loaded, 16)
            sp.wait_ge(table_loaded, 16 * TR * NH0)

        @block.gpsimd
        def _(pool):
            def image(b, at):
                for t in range(NTILE):
                    gr, gc = grid(t)
                    wait_apart(pool, qv_ready, at(NTILE, t + 1))
                    pool.tensor_copy(keys_in[:, t % RING, :].rearrange("p (r c) -> p r c", r=WR),
                                     view(src, b, ROW0[gr], WR, COL0[gc], WC))
                    pool.tensor_copy(q_in[:, t % RING, :].rearrange("p (r c) -> p r c", r=TR)[:, :, ::-1],
                                     view(src, b, gr * TR, TR, gc * TC, TC)).then_inc(taken, 1)
            images(pool, image)

        @block.tensor
        def _(pe):
            pe.sem_inc(qv_ready, RING)

            def image(b, at):
                def project(t):
                    pe.wait_ge(taken, at(NTILE, t + 1))
                    pe.wait_ge(k_copied, at(NTILE, t + 1))
                    keys = keys_in[:, t % RING, :]
                    pe.matmul(k_ps[:, 0:KEYS], w[:, P:2 * P], keys, start=True, stop=True).then_inc(k_ready, 1)
                    pe.wait_ge(qv_copied, at(NTILE, t + 1))
                    pe.matmul(qv_ps[:, 0:P], w[:, 0:P], q_in[:, t % RING, :], start=True, stop=True, skip_group_check=True)
                    for n in range(NKC):
                        mm = pe.matmul(qv_ps[0:KC, (n + 1) * P:(n + 2) * P], keys[:, n * KC:(n + 1) * KC], w[:, 2 * P:3 * P],
                                       start=False, stop=True, skip_group_check=True)
                    mm.then_inc(qv_ready, 1)

                def score(g):
                    t, h = g // NH0, g % NH0
                    pe.wait_ge(s_read, at(G, g + 1))
                    if h == 0:
                        pe.wait_ge(k_copied, at(NTILE, t + 2))
                        pe.wait_ge(qv_copied, at(NTILE, t + 2))
                    rows = slice(h * D0, (h + 1) * D0)
                    pe.matmul(s_ps[:, g % RING, 0:KEYS], qt[rows, t % RING, :], kt[rows, t % RING, :], start=True, stop=True)
                    pe.matmul(s_ps[:, g % RING, 0:KEYS], k["ident16"][:, :], masks[:, MASK_OF[t], :], start=False, stop=True,
                              skip_group_check=True).then_inc(s_ready, 1)

                def turn(g):
                    pe.wait_ge(normed, at(G, g + 1))
                    pe.wait_ge(t_copied, at(G, g + 1))
                    for n in range(NKC):
                        mm = pe.transpose(t_ps[0:KC, g % RING, n * P:(n + 1) * P], prob[:, g % PROB_RING, n * KC:(n + 1) * KC],
                                          k["ident"][:, :])
                    mm.then_inc(turned, 1)

                def weigh(g):
                    t, h = g // NH0, g % NH0
                    pe.wait_ge(t_copied, at(G, g + 1 + RING))
                    if h == 0:
                        pe.wait_ge(y_copied, at(NTILE, t + 1))
                    for n in range(NKC):
                        mm = pe.matmul(o_ps[h * D0:(h + 1) * D0, t % RING, 0:P], vt[:, t % RING, n, h, :],
                                       prob_t[:, g % RING, n * P:(n + 1) * P], start=(n == 0), stop=(n == NKC - 1),
                                       skip_group_check=True)
                    mm.then_inc(o_ready, 1)

                def finish(t):
                    pe.wait_ge(mean_copied, at(NTILE, t + 1))
                    pe.matmul(o_ps[:, t % RING, P:2 * P], w[:, 3 * P:4 * P], mean_t[:, t % RING, :], start=True, stop=True,
                              skip_group_check=True).then_inc(y_ready, 1)

                project(0)
                for g in range(G + 5):
                    if g < G:
                        if g % NH0 == 0 and g // NH0 + 1 < NTILE:
                            project(g // NH0 + 1)
                        score(g)
                    if 2 <= g < G + 2:
                        turn(g - 2)
                    if 3 <= g < G + 3:
                        weigh(g - 3)
                    if g >= 8 and (g - 8) % NH0 == 0:
                        finish((g - 8) // NH0)
            images(pe, image)

        @block.scalar
        def _(act):
            act.sem_inc(k_copied, 1)
            act.sem_inc(p_ready, RING)
            act.sem_inc(t_copied, RING)
            act.sem_inc(y_copied, RING)

            def image(b, at):
                def keys(t):
                    act.wait_ge(k_ready, at(NTILE, t + 1))
                    act.activation(kt[:, t % RING, :], k_ps[:, 0:KEYS], ACT.Identity, bias=bias[:, 1:2]).then_inc(k_copied, 1)

                keys(0)
                for g in range(G + 6):
                    if g < G:
                        act.wait_ge(s_read, at(G, g + 1 + RING))
                        act.wait_ge(turned, at(G, g + 1))
                        act.activation(prob[:, g % PROB_RING, :], neg[:, g % RING, :], ACT.Exp, scale=-1.0,
                                       bias=low[:, g % RING:g % RING + 1],
                                       accum_out=total[:, g % PROB_RING:g % PROB_RING + 1]).then_inc(p_ready, 1)
                        if g % NH0 == 0 and g // NH0 + 1 < NTILE:
                            keys(g // NH0 + 1)
                    if 2 <= g < G + 2:
                        act.wait_ge(turned, at(G, g - 1 + PROB_RING))
                        act.wait_ge(o_ready, at(G, g - 1))
                        act.activation(prob_t[:, g % RING, :], t_ps[0:KC, g % RING, 0:NKC * P], ACT.Copy).then_inc(t_copied, 1)
                    if g >= 7 and (g - 7) % NH0 == 0 and (g - 7) // NH0 < NTILE:
                        t = (g - 7) // NH0
                        act.wait_ge(o_ready, at(G, (t + 1) * NH0 + RING))
                        act.activation(mean_t[:, t % RING, :], o_ps[:, t % RING, 0:P], ACT.Identity, bias=bias[:, 2:3])\
                           .then_inc(mean_copied, 1)
                    if g >= 9 and (g - 9) % NH0 == 0:
                        t = (g - 9) // NH0
                        gr, gc = grid(t)
                        act.wait_ge(y_ready, at(NTILE, t + 1))
                        act.activation(view(dst, b, gr * TR, TR, gc * TC, TC),
                                       o_ps[:, t % RING, P:2 * P].rearrange("p (r c) -> p r c", r=TR)[:, :, ::-1],
                                       ACT.Identity, bias=bias[:, 3:4]).then_inc(y_copied, 1)
            images(act, image)

        @block.vector
        def _(dve):
            dve.wait_ge(table_loaded, 16 * TR * NH0)
            dve.sem_inc(qv_copied, 1)
            dve.sem_inc(s_read, RING)
            dve.sem_inc(turned, PROB_RING)
            dve.sem_inc(o_ready, RING)

            def image(b, at):
                def queries_values(t):
                    dve.wait_ge(qv_ready, at(NTILE, t + 1 + RING))
                    dve.tensor_scalar(qt[:, t % RING, :], qv_ps[:, 0:P], bias[:, 0:1], D0 ** -0.5, ALU.add, ALU.mult)
                    if t == 0 or t >= RING:
                        dve.wait_ge(o_ready, at(G, max(0, t - RING + 1) * NH0 + RING))
                    dve.tensor_copy(vt[:, t % RING, :, :, :], qv_ps[0:KC, P:4 * P].rearrange("p (n h d) -> p n h d", n=NKC, h=NH0))\
                       .then_inc(qv_copied, 1)

                queries_values(0)
                for g in range(G + 1):
                    if g < G:
                        t, h = g // NH0, g % NH0
                        gr, gc = grid(t)
                        r0, c0 = ROW0[gr] - gr * TR + OFF_R, COL0[gc] - gc * TC + OFF_C
                        dve.wait_ge(s_ready, at(G, g + 1))
                        wait_apart(dve, p_ready, at(G, g + 1))
                        dve.tensor_tensor_reduce(neg[:, g % RING, :].rearrange("p (r c) -> p r c", r=WR),
                                                 s_ps[:, g % RING, 0:KEYS].rearrange("p (r c) -> p r c", r=WR),
                                                 table[:, h, r0:r0 + WR, c0:c0 + WC], -1.0, -NEG * 1e8, ALU.add, ALU.min,
                                                 low[:, g % RING:g % RING + 1]).then_inc(s_read, 1)
                    if g:
                        v = g - 1
                        dve.wait_ge(p_ready, at(G, v + 1 + RING))
                        dve.reciprocal(recip[:, v % PROB_RING:v % PROB_RING + 1], total[:, v % PROB_RING:v % PROB_RING + 1])\
                           .then_inc(inverted, 1)
                        dve.wait_ge(inverted, at(G, v + 1))
                        dve.tensor_scalar(prob[:, v % PROB_RING, :], prob[:, v % PROB_RING, :],
                                          recip[:, v % PROB_RING:v % PROB_RING + 1], None, ALU.mult).then_inc(normed, 1)
                    if g < G and h == 2 and t + 1 < NTILE:
                        queries_values(t + 1)
            images(dve, image)


NHF = DIN // P
NROW = DTR + 2 * NST
LOW = 64
CPI = T // CH
UNITS = NST * NHF
A_RING, U_RING, H_RING, HC_RING, B_RING = 8, 4, 4, 4, 4


def mamba_l1(nc, k, dram, X):
    with ExitStack() as c:
        m = Memory(nc, c)
        XN = m.sb("mb_xn", [P, TOK + CH])
        w_in, w_x = m.sb("mb_w_in", [P, 2 * DIN]), m.sb("mb_w_x", [P, NHF, NROW])
        w_dt, w_out = m.sb("mb_w_dt", [DTR, DIN]), m.sb("mb_w_out", [P, NHF, P])
        cols = m.sb("mb_cols", [P, NHF, 7])
        norm, a_log, a = m.sb("mb_norm", [P, 2]), m.sb("mb_a_log", [P, NHF, NST]), m.sb("mb_a", [P, NHF, NST])
        one = m.sb("mb_one", [P, 1])
        pick = m.sb("mb_pick", [LOW + NROW, 2 * NST, P], F32R)
        dbl = m.sb("mb_dbl", [LOW + NROW, 2, CH], F32R)
        with ExitStack() as c2:
            mm = Memory(nc, c2)
            wide = mm.sb("mb_pick_f32", [LOW + NROW, 2 * NST, P])
            loaded, step, exped = mm.sem("mb_loaded"), mm.sem("mb_step"), mm.sem("mb_exped")
            cleared = mm.sem("mb_cleared")
            block = c2.enter_context(nc.Block())

            @block.sync
            def _(sp):
                for dst, name in ((w_in, "L1_w_in"), (w_dt, "L1_w_dt"), (norm, "L1_norm")):
                    sp.dma_start(dst[:, :], dram[name]).then_inc(loaded, 16)
                for dst, name in ((w_x, "L1_w_x"), (w_out, "L1_w_out"), (cols, "L1_cols"), (a_log, "L1_a_log")):
                    sp.dma_start(dst[:, :, :], dram[name]).then_inc(loaded, 16)
                sp.wait_ge(cleared, 1)
                for row in (0, LOW):
                    sp.dma_start(wide[row:row + NROW, :, :], dram["c_pick"]).then_inc(loaded, 16)
                sp.wait_ge(loaded, 144)

            @block.scalar
            def _(act):
                act.wait_ge(loaded, 144)
                act.activation(a[:, :, :], a_log[:, :, :], ACT.Exp).then_inc(exped, 1)

            @block.vector
            def _(dve):
                dve.memset(wide[:, :, :], 0.0).then_inc(cleared, 1)
                dve.memset(one[:, :], 1.0)
                dve.memset(XN[:, TOK:TOK + CH], 0.0)
                dve.memset(dbl[:, :, :].bitcast(F32), 0.0)
                dve.wait_ge(loaded, 144)
                dve.tensor_copy(pick[:, :, :], wide[:, :, :]).then_inc(step, 1)
                dve.wait_ge(exped, 1)
                dve.tensor_scalar(a[:, :, :], a[:, :, :], -1.0, None, ALU.mult).then_inc(step, 1)
        group_norm(nc, k, "mb_gn", X, XN)
        layer_norm(nc, k, "mb_ln", XN, XN, "eps5", gain=norm[:, 0:1], shift=norm[:, 1:2])
        selective_scan(nc, k, X, XN, w_in, w_x, w_dt, w_out, cols, a, one, pick, dbl)


def selective_scan(nc, k, X, XN, w_in, w_x, w_dt, w_out, cols, a, one, pick, dbl):
    with ExitStack() as c:
        m = Memory(nc, c)
        TAP = NCONV - 1
        xin, conv = m.sb("ss_xin", [P, NHF, TAP + CH]), m.sb("ss_conv", [P, NHF, CH])
        xc, gate = m.sb("ss_xc", [P, 2, NHF, CH]), m.sb("ss_gate", [P, 2, NHF, CH])
        delta, dx = m.sb("ss_delta", [P, 2, NHF, CH]), m.sb("ss_dx", [P, 2, NHF, CH])
        dt = m.sb("ss_dt", [DTR, CH])
        mag, em, ln1, err, relu = (m.sb(f"ss_{n}", [P, NHF, CH]) for n in ("mag", "em", "ln1", "err", "relu"))
        b_row = m.sb("ss_b_row", [P, B_RING, CH])
        decay, drive = m.sb("ss_decay", [P, A_RING, CH]), m.sb("ss_drive", [P, U_RING, CH])
        h, hc = m.sb("ss_h", [P, H_RING, CH]), m.sb("ss_hc", [P, HC_RING, CH])
        state = m.sb("ss_state", [P, UNITS])
        y = m.sb("ss_y", [P, NHF, CH])
        g_ps, f_ps = m.ps("ss_g_ps", [P, 2, CH]), m.ps("ss_f_ps", [P, CH])
        b_ps, c_ps, y_ps = m.ps("ss_b_ps", [P, CH]), m.ps("ss_c_ps", [P, 2, CH]), m.ps("ss_y_ps", [P, NHF, CH])
        names = ("xin_ready", "haloed", "xin_copied", "z_ready", "convolved", "silued", "rows_ready", "rows_copied",
                 "rows_low", "dt_ready", "mag_done", "em_done", "ln_done", "relued", "err_done", "delta_done", "dx_done",
                 "b_ready", "b_copied", "c_ready", "decayed", "driven", "scanned", "kept", "weighed", "summed",
                 "y_done", "gated", "out_ready", "added", "reset")
        S = {n: m.sem(f"ss_{n}") for n in names}
        block = c.enter_context(nc.Block())

        def chunks(eng, first, body):
            with eng.Fori(0, BATCH) as b:
                first(Place(b, 0, 0))
                with eng.Fori(0, CPI // 2) as i:
                    for u in range(2):
                        body(Place(b, i, u), Place(b, i, u + 1))

        class Place:

            def __init__(self, b, i, u):
                self.b, self.i, self.u, self.buf = b, i, u, u % 2

            def unit(self, per, j):
                return self.b * (CPI * per) + self.i * (2 * per) + (self.u * per + j)

            def round(self, per, j):
                return self.b * ((CPI + 1) * per) + self.i * (2 * per) + (self.u * per + j)

            def spread(self, lead, j):
                return self.b * (CPI * NST + lead) + self.i * (2 * NST) + (self.u * NST + j)

            def tokens(self):
                return ds(self.b * T + self.i * (2 * CH) + self.u * CH, CH)

        B_LEAD, C_LEAD = 2, 1

        def two_chunks(eng, first, body, tail, slot):
            def chunk(ch, rnd):
                body(ch, rnd, lambda s: tail(Place(ch.b, ch.i, 0)) if ch.u == 1 and s == slot else None)
                if ch.u == 1:
                    tail(ch)
            chunks(eng, first, chunk)

        def run(steps, rnd, slot=None):
            for at, step in steps:
                if slot is None or at == slot:
                    step(rnd)

        @block.tensor
        def _(pe):
            def into(rnd, first, ready):
                for n in range(2):
                    mm = pe.matmul(g_ps[:, n, :], w_in[:, (first + n) * P:(first + n + 1) * P], XN[:, rnd.tokens()],
                                   start=True, stop=True)
                    mm.then_inc(S[ready], 1)

            def project_x(rnd):
                pe.wait_ge(S["relued"], rnd.round(2, 2))
                into(rnd, 0, "xin_ready")

            def project_z(rnd):
                pe.wait_ge(S["xin_copied"], rnd.round(2, 2))
                into(rnd, 2, "z_ready")

            def project_rows(rnd):
                pe.wait_ge(S["silued"], rnd.round(4, 4))
                for n in range(NHF):
                    mm = pe.matmul(g_ps[0:NROW, 0, :], w_x[:, n, :], xc[:, rnd.buf, n, :], start=(n == 0), stop=(n == NHF - 1))
                mm.then_inc(S["rows_ready"], 1)

            def project_dt(rnd):
                pe.wait_ge(S["rows_copied"], rnd.round(2, 2))
                pe.wait_ge(S["rows_low"], rnd.round(1, 1))
                for n in (1, 0):
                    pe.matmul(g_ps[:, n, :], w_dt[:, n * P:(n + 1) * P], dt[:, :], start=True, stop=True).then_inc(S["dt_ready"], 1)

            steps = [(2, project_x), (5, project_z), (15, project_rows), (17, project_dt)]

            def spread_b(ch, n):
                pe.wait_ge(S["b_copied"], ch.spread(B_LEAD, n + 1))
                pe.matmul(b_ps[:, :], pick[:, n % NST, :], dbl[:, (ch.buf + n // NST) % 2, :], start=True, stop=True)\
                    .then_inc(S["b_ready"], 1)

            def spread_c(ch, n):
                pe.wait_ge(S["weighed"], ch.unit(UNITS, 2 * n + 2))
                pe.matmul(c_ps[:, n % 2, :], pick[:, NST + n % NST, :], dbl[:, (ch.buf + n // NST) % 2, :], start=True, stop=True)\
                    .then_inc(S["c_ready"], 1)

            def first(rnd):
                run(steps, rnd)
                for n in range(B_LEAD):
                    spread_b(rnd, n)
                spread_c(rnd, 0)

            def body(ch, rnd, tail_before):
                for s in range(UNITS):
                    if s % 2 == 0:
                        spread_b(ch, s // 2 + B_LEAD)
                        spread_c(ch, s // 2 + C_LEAD)
                    run(steps, rnd, s)
                    tail_before(s)
                    for v in ([s - 1] if s else []) + ([s] if s == UNITS - 1 else []):
                        if v == 0:
                            pe.wait_ge(S["y_done"], ch.unit(NHF, NHF))
                        pe.wait_ge(S["weighed"], ch.unit(UNITS, v + 1 + 4))
                        pe.matmul(y_ps[:, v % 2, :], k["ident"][:, :], hc[:, v % HC_RING, :], start=(v < 2),
                                  stop=(v >= UNITS - 2)).then_inc(S["summed"], 1)

            def tail(ch):
                pe.wait_ge(S["added"], ch.unit(1, 1))
                pe.matmul(f_ps[:, :], k["ident"][:, :], X[:, ch.tokens()], start=True, stop=False)
                pe.wait_ge(S["gated"], ch.unit(NHF, NHF))
                for n in range(NHF):
                    mm = pe.matmul(f_ps[:, :], w_out[:, n, :], y[:, n, :], start=False, stop=(n == NHF - 1))
                mm.then_inc(S["out_ready"], 1)
            two_chunks(pe, first, body, tail, 3)

        @block.scalar
        def _(act):
            act.sem_inc(S["b_copied"], 1)
            act.sem_inc(S["added"], 1)

            def copy_x(rnd):
                act.wait_ge(S["haloed"], rnd.round(1, 1))
                for n in range(NHF):
                    act.wait_ge(S["xin_ready"], rnd.round(2, n + 1))
                    act.activation(xin[:, n, TAP:TAP + CH], g_ps[:, n, :], ACT.Copy).then_inc(S["xin_copied"], 1)

            def silu(rnd):
                for n in range(NHF):
                    act.wait_ge(S["z_ready"], rnd.round(2, n + 1))
                    act.activation(gate[:, rnd.buf, n, :], g_ps[:, n, :], ACT.Silu).then_inc(S["silued"], 1)
                for n in range(NHF):
                    act.wait_ge(S["convolved"], rnd.round(8, 8 + 7 + n))
                    act.activation(xc[:, rnd.buf, n, :], conv[:, n, :], ACT.Silu, bias=cols[:, n, 4:5]).then_inc(S["silued"], 1)

            def copy_rows(rnd):
                act.wait_ge(S["rows_ready"], rnd.round(1, 1))
                act.activation(dbl[0:NROW, rnd.buf, :], g_ps[0:NROW, 0, :], ACT.Copy).then_inc(S["rows_copied"], 1)
                act.activation(dt[:, :], g_ps[0:DTR, 0, :], ACT.Copy).then_inc(S["rows_copied"], 1)

            def softplus(rnd):
                for n in (1, 0):
                    act.wait_ge(S["dt_ready"], rnd.round(2, 2 - n))
                    act.activation(mag[:, n, :], g_ps[:, n, :], ACT.Abs, bias=cols[:, n, 5:6]).then_inc(S["mag_done"], 1)
                act.wait_ge(S["mag_done"], rnd.round(2, 2))
                act.activation(em[:, :, :], mag[:, :, :], ACT.Exp, scale=-1.0).then_inc(S["em_done"], 1)
                act.wait_ge(S["em_done"], rnd.round(1, 1))
                act.activation(ln1[:, :, :], em[:, :, :], ACT.Ln, bias=one[:, :]).then_inc(S["ln_done"], 1)

            steps = [(4, copy_x), (14, silu), (17, copy_rows), (19, softplus)]

            def copy_b(ch, n):
                act.wait_ge(S["b_ready"], ch.spread(B_LEAD, n + 1))
                act.wait_ge(S["driven"], ch.unit(UNITS, 2 * n + 2))
                act.activation(b_row[:, n % B_RING, :], b_ps[:, :], ACT.Copy).then_inc(S["b_copied"], 1)

            def first(rnd):
                run(steps, rnd)
                for n in range(B_LEAD):
                    copy_b(rnd, n)

            def body(ch, rnd, tail_before):
                for s in range(UNITS):
                    n, half = s // 2, s % 2
                    if s == 0:
                        act.wait_ge(S["delta_done"], ch.round(4, 4))
                    act.wait_ge(S["scanned"], ch.unit(UNITS, s + 1))
                    act.activation(decay[:, s % A_RING, :], delta[:, ch.buf, half, :], ACT.Exp, scale=a[:, half, n:n + 1])\
                       .then_inc(S["decayed"], 1)
                    if half:
                        copy_b(ch, n + B_LEAD)
                    run(steps, rnd, s)
                    tail_before(s)

            def tail(ch):
                act.wait_ge(S["out_ready"], ch.unit(1, 1))
                act.activation(X[:, ch.tokens()], f_ps[:, :], ACT.Copy).then_inc(S["added"], 1)
            two_chunks(act, first, body, tail, 5)

        @block.gpsimd
        def _(pool):
            pool.sem_inc(S["driven"], NHF * B_RING)

            def halo(rnd):
                wait_apart(pool, S["convolved"], rnd.round(8, 8))
                pool.tensor_copy(xin[:, :, 0:TAP], xin[:, :, CH:CH + TAP]).then_inc(S["haloed"], 1)

            def log_error(rnd):
                pool.wait_ge(S["err_done"], rnd.round(2, 1))
                pool.tensor_tensor(err[:, :, :], em[:, :, :], err[:, :, :], ALU.subtract).then_inc(S["err_done"], 1)

            def times_x(rnd):
                pool.wait_ge(S["delta_done"], rnd.round(4, 4))
                pool.tensor_tensor(dx[:, rnd.buf, :, :], delta[:, rnd.buf, :, :], xc[:, rnd.buf, :, :], ALU.mult)\
                    .then_inc(S["dx_done"], 1)

            steps = [(3, halo), (25, log_error), (31, times_x)]

            def first(rnd):
                wait_apart(pool, S["convolved"], rnd.round(8, 8))
                pool.memset(xin[:, :, 0:TAP], 0.0).then_inc(S["haloed"], 1)
                run(steps[1:], rnd)

            def body(ch, rnd):
                for s in range(UNITS):
                    n, half = s // 2, s % 2
                    pool.wait_ge(S["b_copied"], ch.spread(B_LEAD, n + 2))
                    if s == 0:
                        pool.wait_ge(S["dx_done"], ch.round(1, 1))
                    pool.wait_ge(S["scanned"], ch.unit(UNITS, s + 1 + A_RING - U_RING))
                    pool.tensor_tensor(drive[:, s % U_RING, :], dx[:, ch.buf, half, :], b_row[:, n % B_RING, :], ALU.mult)\
                        .then_inc(S["driven"], 1)
                    run(steps, rnd, s)
            chunks(pool, first, body)

        @block.vector
        def _(dve):
            dve.sem_inc(S["scanned"], A_RING)
            dve.sem_inc(S["weighed"], 4)
            dve.sem_inc(S["y_done"], NHF)
            dve.sem_inc(S["relued"], 2)
            dve.sem_inc(S["convolved"], 8)

            def taps(t):
                def step(rnd):
                    for n in range(NHF):
                        src = xin[:, n, t:t + CH]
                        if t == 0:
                            dve.wait_ge(S["xin_copied"], rnd.round(2, n + 1))
                            ins = dve.tensor_scalar(conv[:, n, :], src, cols[:, n, 0:1], None, ALU.mult)
                        else:
                            dve.wait_ge(S["convolved"], rnd.round(8, 8 + 2 * (t - 1) + n + 1))
                            ins = dve.scalar_tensor_tensor(conv[:, n, :], src, cols[:, n, t:t + 1], conv[:, n, :], ALU.mult, ALU.add)
                        ins.then_inc(S["convolved"], 1)
                return step

            def low_rows(rnd):
                dve.wait_ge(S["rows_copied"], rnd.round(2, 2))
                dve.tensor_tensor(dbl[LOW:LOW + NROW, rnd.buf, :], g_ps[0:NROW, 0, :], dbl[0:NROW, rnd.buf, :].bitcast(F32),
                                  ALU.subtract).then_inc(S["rows_low"], 1)

            def relu_dt(rnd):
                for n in (1, 0):
                    dve.wait_ge(S["mag_done"], rnd.round(2, 2 - n))
                    dve.tensor_scalar(relu[:, n, :], g_ps[:, n, :], cols[:, n, 5:6], 0.0, ALU.add, ALU.max).then_inc(S["relued"], 1)

            def round_off(rnd):
                dve.wait_ge(S["em_done"], rnd.round(1, 1))
                dve.tensor_scalar(err[:, :, :], em[:, :, :], 1.0, 1.0, ALU.add, ALU.subtract).then_inc(S["err_done"], 1)

            def make_delta(rnd):
                dve.wait_ge(S["relued"], rnd.round(2, 4))
                dve.wait_ge(S["ln_done"], rnd.round(1, 1))
                dve.wait_ge(S["err_done"], rnd.round(2, 2))
                for n in range(NHF):
                    dve.tensor_tensor(relu[:, n, :], relu[:, n, :], err[:, n, :], ALU.add).then_inc(S["delta_done"], 1)
                for n in range(NHF):
                    dve.wait_ge(S["delta_done"], rnd.round(4, n + 1))
                    dve.tensor_tensor(delta[:, rnd.buf, n, :], relu[:, n, :], ln1[:, n, :], ALU.add).then_inc(S["delta_done"], 1)

            steps = [(6, taps(0)), (8, taps(1)), (10, taps(2)), (12, taps(3)), (17, low_rows), (19, relu_dt), (20, round_off), (27, make_delta)]

            def first(rnd):
                dve.memset(state[:, :], 0.0).then_inc(S["reset"], 1)
                dve.wait_ge(S["reset"], rnd.b * 1 + 1)
                run(steps, rnd)

            def body(ch, rnd):
                def scan(s):
                    dve.wait_ge(S["decayed"], ch.unit(UNITS, s + 1))
                    dve.wait_ge(S["driven"], ch.unit(UNITS, s + 1 + NHF * B_RING))
                    dve.tensor_tensor_scan(h[:, s % H_RING, :], decay[:, s % A_RING, :], drive[:, s % U_RING, :],
                                           state[:, s:s + 1], ALU.mult, ALU.add).then_inc(S["scanned"], 1)

                def weigh(s):
                    n = s // 2
                    dve.wait_ge(S["scanned"], ch.unit(UNITS, s + 1 + A_RING))
                    dve.tensor_copy(state[:, s:s + 1], h[:, s % H_RING, CH - 1:CH]).then_inc(S["kept"], 1)
                    dve.wait_ge(S["c_ready"], ch.spread(C_LEAD, n + 1))
                    dve.wait_ge(S["summed"], ch.unit(UNITS, s - 3)) if s >= HC_RING else None
                    dve.tensor_tensor(hc[:, s % HC_RING, :], h[:, s % H_RING, :], c_ps[:, n % 2, :], ALU.mult)\
                       .then_inc(S["weighed"], 1)

                for s in range(UNITS + 1):
                    if s < UNITS:
                        if s >= H_RING:
                            dve.wait_ge(S["weighed"], ch.unit(UNITS, s - H_RING + 1 + 4))
                        scan(s)
                    if s:
                        weigh(s - 1)
                    if s < UNITS:
                        run(steps, rnd, s)
                for n in range(NHF):
                    dve.wait_ge(S["summed"], ch.unit(UNITS, UNITS - 1 + n))
                    dve.scalar_tensor_tensor(y[:, n, :], xc[:, ch.buf, n, :], cols[:, n, 6:7], y_ps[:, n, :], ALU.mult, ALU.add)\
                       .then_inc(S["y_done"], 1)
                for n in range(NHF):
                    dve.wait_ge(S["y_done"], ch.unit(NHF, NHF + n + 1))
                    dve.tensor_tensor(y[:, n, :], y[:, n, :], gate[:, ch.buf, n, :], ALU.mult).then_inc(S["gated"], 1)
            chunks(dve, first, body)


STAGES = {
    "L0": neighbourhood_l0,
    "L1": mamba_l1,
    "L2a": attention_l2,
    "L2f": experts_l2,
    "L3a": attention_l3,
    "L3f": filters_l3,
}


def build(nc, dram, out, stages=tuple(STAGES)):
    nc.disable_value_cache = True
    with ExitStack() as ctx:
        m = Memory(nc, ctx)
        k = load_constants(nc, m, dram)
        X = m.sb("X", [P, TOK])
        with ExitStack() as c:
            loaded = Memory(nc, c).sem("x_loaded")
            block = c.enter_context(nc.Block())

            @block.sync
            def _(sp):
                for b in range(BATCH):
                    sp.dma_start(X[:, b * T:(b + 1) * T], dram["x"][b]).then_inc(loaded, 16)
                sp.wait_ge(loaded, 16 * BATCH)

        for s in stages:
            STAGES[s](nc, k, dram, X)
        with ExitStack() as c:
            stored = Memory(nc, c).sem("x_stored")
            block = c.enter_context(nc.Block())

            @block.sync
            def _(sp):
                for b in range(BATCH):
                    sp.dma_start(out[b], X[:, b * T:(b + 1) * T]).then_inc(stored, 16)
                sp.wait_ge(stored, 16 * BATCH)


def lay_out(inputs):
    f = {n: np.asarray(a) for n, a in inputs.items()}

    def halves(a):
        return a.reshape(NHF, P, -1).transpose(1, 0, 2)

    o = constants()
    o["x"] = f["x"].reshape(BATCH, P, T)
    o["L0_w"] = np.concatenate([f["L0_conv_qkv_w"], f["L0_conv_proj_w"]], 1).transpose(2, 0, 1)
    o["L0_bias"] = np.concatenate([f["L0_conv_qkv_b"], f["L0_conv_proj_b"]], 1).reshape(2, 4, P).transpose(2, 0, 1)
    o["L0_ln"] = np.stack([f["L0_conv_ln_g"], f["L0_conv_ln_b"]], 1)
    o["L0_rpb"] = np.zeros((2, NH0, PR, PC), f["L0_conv_rpb"].dtype)
    o["L0_rpb"][:, :, PAD_R:PAD_R + RPB, PAD_C:PAD_C + RPB] = f["L0_conv_rpb"]
    o["L1_w_in"] = f["L1_conv_in_proj_w"].T
    o["L1_w_x"] = halves(f["L1_conv_x_proj_w"].T)
    o["L1_w_dt"] = f["L1_conv_dt_proj_w"].T
    o["L1_w_out"] = halves(f["L1_conv_out_proj_w"].T)
    o["L1_norm"] = np.stack([f["L1_conv_norm_w"], f["L1_conv_norm_b"]], 1)
    o["L1_cols"] = halves(np.concatenate([f["L1_conv_conv_w"]] + [f[n][:, None] for n in (
        "L1_conv_conv_b", "L1_conv_dt_proj_b", "L1_conv_D")], 1))
    o["L1_a_log"] = halves(f["L1_conv_A_log"])
    for n in ("L2_attn_Wq", "L2_attn_Wk", "L2_attn_Wv", "L2_ffn_router_w", "L2_ffn_expert_w", "L2_ffn_expert_b",
              "L3_attn_w_attn", "L3_attn_w_proj", "L3_ffn_M_u", "L3_ffn_M_phi_plus", "L3_ffn_M_phi_minus"):
        o[n] = f[n]
    for n in ("L2_ffn_router_b", "L3_ffn_sigma", "L3_ffn_log_weights", "L3_ffn_gumbel"):
        o[n] = f[n].reshape(1, -1)
    o["L3_ffn_phi"] = f["L3_ffn_phi"].reshape(HALF, 2, NK).transpose(2, 1, 0).reshape(P, HALF // 4)
    return {n: np.ascontiguousarray(a) for n, a in o.items()}


def kernel(**inputs):
    import concourse.bacc as bacc
    from concourse.bass_utils import run_bass_kernel_spmd

    nc = bacc.Bacc("TRN2", target_bir_lowering=False, num_devices=1)
    arrays = lay_out(inputs)
    dram = {n: nc.dram_tensor(n, a.shape, mybir.dt.from_np(a.dtype), kind="ExternalInput").ap() for n, a in arrays.items()}
    out = nc.dram_tensor("out", [BATCH, P, T], F32, kind="ExternalOutput").ap()
    build(nc, dram, out)
    r = run_bass_kernel_spmd(nc, [arrays], core_ids=[0])
    return r.results[0]["out"].reshape(BATCH, P, HW, HW)
```
